# Optimizing a Trainium2 kernel written in Bass

```python
import numpy as np
import jax
import jax.numpy as jnp

def _softmax(x, axis=-1):
    return jax.nn.softmax(x, axis=axis)

def _gelu(x):
    return jax.nn.gelu(x, approximate=True)

def _silu(x):
    return jax.nn.silu(x)

def _sigmoid(x):
    return jax.nn.sigmoid(x)

def _layernorm(x, axis=-1, eps=1e-05):
    m = jnp.mean(x, axis=axis, keepdims=True)
    v = jnp.var(x, axis=axis, keepdims=True)
    return (x - m) / jnp.sqrt(v + eps)

def _scatter_add(tgt, idx, src, axis=0):
    return tgt.at[idx].add(src)

def _segment_sum(src, seg, n):
    return jax.ops.segment_sum(src, seg, n)
kernel_name = 'mk_gnn_preln_d4_gnn_r32_3088fa'

def setup_inputs(seed: int=0):
    np.random.seed(seed)
    _w = jnp.asarray

    def _rec_inputs():
        import jax
        import jax.numpy as jnp
        _gk = jax.random.key(seed)
        x = -0.0003713 + 1 * jax.random.normal(jax.random.fold_in(_gk, 1), (50000, 128), jnp.float32)
        src = jax.random.randint(jax.random.fold_in(_gk, 2), (25000,), 0, 50000, jnp.int32)
        dst = jax.random.randint(jax.random.fold_in(_gk, 3), (25000,), 0, 50000, jnp.int32)
        _o = jnp.argsort(dst, stable=True)
        src = src[_o]
        dst = dst[_o]
        edge_attr_128 = -8.513e-05 + 0.999844 * jax.random.normal(jax.random.fold_in(_gk, 12), (25000, 128), jnp.float32)
        edge_type_4 = jax.random.randint(jax.random.fold_in(_gk, 14), (25000,), 0, 4, jnp.int32)
        edge_weight = jax.random.uniform(jax.random.fold_in(_gk, 15), (25000,), jnp.float32, 0.0, 0.999996)
        return (x, src, dst, edge_attr_128, edge_type_4, edge_weight)
    x, src, dst, edge_attr_128, edge_type_4, edge_weight = _rec_inputs()

    def _L0_gnn_setup():
        import jax, jax.numpy as jnp
        import numpy as np
        N_NODES = 3125
        N_EDGES = 25000
        FEATURE_DIM = 128
        DEPTH = 3
        key = jax.random.key(seed)
        k1, k2, k3 = jax.random.split(key, 3)
        x = jax.random.normal(k1, (N_NODES, FEATURE_DIM), dtype=jnp.float32)
        edge_index = jax.random.randint(k2, (2, N_EDGES), 0, N_NODES, dtype=jnp.int32)
        W = jax.random.normal(k3, (FEATURE_DIM, FEATURE_DIM), dtype=jnp.float32) * (1.0 / np.sqrt(FEATURE_DIM))
        b = jnp.zeros((FEATURE_DIM,), dtype=jnp.float32)
        return {'x': x, 'edge_index': edge_index, 'W': W, 'b': b}
    _L0_gnn_all = _L0_gnn_setup()
    _L0_gnn_in = {k: v for k, v in _L0_gnn_all.items() if k in ('W', 'b')}
    del _L0_gnn_all

    def _L1_gnn_setup():
        import jax, jax.numpy as jnp
        import numpy as np
        N_NODES, N_EDGES, HIDDEN, HOPS = (625, 20000, 128, 3)
        LEAKY_ALPHA = 0.2

        def _segment_softmax(scores, seg, num_segments):
            m = jax.ops.segment_max(scores, seg, num_segments)
            ex = jnp.exp(scores - m[seg])
            denom = jax.ops.segment_sum(ex, seg, num_segments)
            return ex / denom[seg]
        key = jax.random.key(seed)
        ks = jax.random.split(key, 9)
        s = 1.0 / np.sqrt(HIDDEN)
        return {'node_feat': jax.random.normal(ks[0], (N_NODES, HIDDEN), jnp.float32), 'edge_feat': jax.random.normal(ks[1], (N_EDGES, HIDDEN), jnp.float32), 'senders': jax.random.randint(ks[2], (N_EDGES,), 0, N_NODES), 'receivers': jax.random.randint(ks[3], (N_EDGES,), 0, N_NODES), 'Wq': jax.random.normal(ks[4], (HOPS, HIDDEN, HIDDEN), jnp.float32) * s, 'bq': jnp.zeros((HOPS, HIDDEN), jnp.float32), 'Wn': jax.random.normal(ks[5], (HOPS, HIDDEN, HIDDEN), jnp.float32) * s, 'bn': jnp.zeros((HOPS, HIDDEN), jnp.float32), 'We': jax.random.normal(ks[6], (HOPS, HIDDEN, HIDDEN), jnp.float32) * s, 'be': jnp.zeros((HOPS, HIDDEN), jnp.float32), 'attn': jax.random.normal(ks[7], (HOPS, HIDDEN), jnp.float32) * s}
    _L1_gnn_all = _L1_gnn_setup()
    _L1_gnn_in = {k: v for k, v in _L1_gnn_all.items() if k in ('Wq', 'bq', 'Wn', 'bn', 'We', 'be', 'attn')}
    del _L1_gnn_all

    def _L2_gnn_setup():
        import jax, jax.numpy as jnp
        import numpy as np
        NUM_RELATIONS = 4
        N_NODES = 625
        N_EDGES = 10000
        F_IN = 128
        HID = 128
        EMB = 128

        def _rgcn_conv(x, src, dst, edge_type, edge_weight, W, root, bias):
            xj = x[src]
            m = jnp.zeros((xj.shape[0], W.shape[2]), dtype=x.dtype)
            for r in range(W.shape[0]):
                mask = (edge_type == r).astype(x.dtype)[:, None]
                m = m + mask * (xj @ W[r])
            m = m * edge_weight[:, None]
            out = jax.ops.segment_sum(m, dst, num_segments=x.shape[0])
            return out + x @ root + bias
        key = jax.random.key(seed)
        ks = jax.random.split(key, 10)
        return {'x': jax.random.normal(ks[0], (N_NODES, F_IN), dtype=jnp.float32), 'edge_index': jax.random.randint(ks[1], (2, N_EDGES), 0, N_NODES, dtype=jnp.int64 if jax.config.jax_enable_x64 else jnp.int32).astype(jnp.int32), 'edge_type': jax.random.randint(ks[2], (N_EDGES,), 0, NUM_RELATIONS).astype(jnp.int32), 'edge_weight': jax.random.uniform(ks[3], (N_EDGES,), dtype=jnp.float32), 'W1': jax.random.normal(ks[4], (NUM_RELATIONS, F_IN, HID), dtype=jnp.float32) * 0.05, 'root1': jax.random.normal(ks[5], (F_IN, HID), dtype=jnp.float32) * 0.05, 'b1': jax.random.normal(ks[6], (HID,), dtype=jnp.float32) * 0.05, 'W2': jax.random.normal(ks[7], (NUM_RELATIONS, HID, EMB), dtype=jnp.float32) * 0.05, 'root2': jax.random.normal(ks[8], (HID, EMB), dtype=jnp.float32) * 0.05, 'b2': jax.random.normal(ks[9], (EMB,), dtype=jnp.float32) * 0.05}
    _L2_gnn_all = _L2_gnn_setup()
    _L2_gnn_in = {k: v for k, v in _L2_gnn_all.items() if k in ('W1', 'root1', 'b1', 'W2', 'root2', 'b2')}
    del _L2_gnn_all

    def _L3_gnn_setup():
        import jax, jax.numpy as jnp
        import numpy as np
        BN_EPS = 1e-05

        def _bn(z, gamma, beta):
            mean = jnp.mean(z, axis=0)
            var = jnp.mean(jnp.square(z - mean), axis=0)
            return (z - mean) * jax.lax.rsqrt(var + BN_EPS) * gamma + beta
        key = jax.random.key(seed)
        ks = jax.random.split(key, 8)
        N, E, H, L = (50000, 25000, 128, 5)
        s = 1.0 / np.sqrt(H)
        return {'x': jax.random.normal(ks[0], (N, H), dtype=jnp.float32), 'edge_index': jax.random.randint(ks[1], (2, E), 0, N, dtype=jnp.int32), 'W1': jax.random.normal(ks[2], (L, H, H), dtype=jnp.float32) * s, 'b1': jax.random.normal(ks[3], (L, H), dtype=jnp.float32) * s, 'g1': jnp.ones((L, H), dtype=jnp.float32), 'be1': jnp.zeros((L, H), dtype=jnp.float32), 'W2': jax.random.normal(ks[4], (L, H, H), dtype=jnp.float32) * s, 'b2': jax.random.normal(ks[5], (L, H), dtype=jnp.float32) * s, 'g2': jnp.ones((L, H), dtype=jnp.float32), 'be2': jnp.zeros((L, H), dtype=jnp.float32)}
    _L3_gnn_all = _L3_gnn_setup()
    _L3_gnn_in = {k: v for k, v in _L3_gnn_all.items() if k in ('W1', 'b1', 'g1', 'be1', 'W2', 'b2', 'g2', 'be2')}
    del _L3_gnn_all
    return {'x': x, 'src': src, 'dst': dst, 'edge_attr_128': edge_attr_128, 'edge_type_4': edge_type_4, 'edge_weight': edge_weight, 'L0_gnn_W': _L0_gnn_in['W'], 'L0_gnn_b': _L0_gnn_in['b'], 'L1_gnn_Wq': _L1_gnn_in['Wq'], 'L1_gnn_bq': _L1_gnn_in['bq'], 'L1_gnn_Wn': _L1_gnn_in['Wn'], 'L1_gnn_bn': _L1_gnn_in['bn'], 'L1_gnn_We': _L1_gnn_in['We'], 'L1_gnn_be': _L1_gnn_in['be'], 'L1_gnn_attn': _L1_gnn_in['attn'], 'L2_gnn_W1': _L2_gnn_in['W1'], 'L2_gnn_root1': _L2_gnn_in['root1'], 'L2_gnn_b1': _L2_gnn_in['b1'], 'L2_gnn_W2': _L2_gnn_in['W2'], 'L2_gnn_root2': _L2_gnn_in['root2'], 'L2_gnn_b2': _L2_gnn_in['b2'], 'L3_gnn_W1': _L3_gnn_in['W1'], 'L3_gnn_b1': _L3_gnn_in['b1'], 'L3_gnn_g1': _L3_gnn_in['g1'], 'L3_gnn_be1': _L3_gnn_in['be1'], 'L3_gnn_W2': _L3_gnn_in['W2'], 'L3_gnn_b2': _L3_gnn_in['b2'], 'L3_gnn_g2': _L3_gnn_in['g2'], 'L3_gnn_be2': _L3_gnn_in['be2']}

def reference(x, src, dst, edge_attr_128, edge_type_4, edge_weight, L0_gnn_W, L0_gnn_b, L1_gnn_Wq, L1_gnn_bq, L1_gnn_Wn, L1_gnn_bn, L1_gnn_We, L1_gnn_be, L1_gnn_attn, L2_gnn_W1, L2_gnn_root1, L2_gnn_b1, L2_gnn_W2, L2_gnn_root2, L2_gnn_b2, L3_gnn_W1, L3_gnn_b1, L3_gnn_g1, L3_gnn_be1, L3_gnn_W2, L3_gnn_b2, L3_gnn_g2, L3_gnn_be2):
    import jax
    import jax.numpy as jnp

    def _L0_gnn_ref(x, edge_index, W, b):
        import jax, jax.numpy as jnp
        import numpy as np
        N_NODES = 3125
        N_EDGES = 25000
        FEATURE_DIM = 128
        DEPTH = 3
        n = x.shape[0]
        loop = jnp.arange(n, dtype=edge_index.dtype)
        src = jnp.concatenate([edge_index[0], loop])
        dst = jnp.concatenate([edge_index[1], loop])
        ones = jnp.ones(src.shape[0], dtype=x.dtype)
        deg = jax.ops.segment_sum(ones, dst, num_segments=n)
        dis = jnp.where(deg > 0, jax.lax.rsqrt(deg), 0.0)
        norm = (dis[src] * dis[dst])[:, None]
        for _ in range(DEPTH):
            h = x @ W
            msg = h[src] * norm
            agg = jax.ops.segment_sum(msg, dst, num_segments=n)
            x = jax.nn.relu(agg + b)
        return x

    def _L1_gnn_ref(node_feat, edge_feat, senders, receivers, Wq, bq, Wn, bn, We, be, attn):
        import jax, jax.numpy as jnp
        import numpy as np
        N_NODES, N_EDGES, HIDDEN, HOPS = (625, 20000, 128, 3)
        LEAKY_ALPHA = 0.2

        def _segment_softmax(scores, seg, num_segments):
            m = jax.ops.segment_max(scores, seg, num_segments)
            ex = jnp.exp(scores - m[seg])
            denom = jax.ops.segment_sum(ex, seg, num_segments)
            return ex / denom[seg]
        n = node_feat.shape[0]
        h = node_feat
        for i in range(Wq.shape[0]):
            q = h @ Wq[i] + bq[i]
            v = (h @ Wn[i] + bn[i])[senders] + (edge_feat @ We[i] + be[i])
            feats = jax.nn.leaky_relu(q[receivers] + v, LEAKY_ALPHA)
            score = feats @ attn[i]
            alpha = _segment_softmax(score, receivers, n)
            pooled = jax.ops.segment_sum(alpha[:, None] * v, receivers, n)
            h = jax.nn.relu(pooled)
        return h

    def _L2_gnn_ref(x, edge_index, edge_type, edge_weight, W1, root1, b1, W2, root2, b2):
        import jax, jax.numpy as jnp
        import numpy as np
        NUM_RELATIONS = 4
        N_NODES = 625
        N_EDGES = 10000
        F_IN = 128
        HID = 128
        EMB = 128

        def _rgcn_conv(x, src, dst, edge_type, edge_weight, W, root, bias):
            xj = x[src]
            m = jnp.zeros((xj.shape[0], W.shape[2]), dtype=x.dtype)
            for r in range(W.shape[0]):
                mask = (edge_type == r).astype(x.dtype)[:, None]
                m = m + mask * (xj @ W[r])
            m = m * edge_weight[:, None]
            out = jax.ops.segment_sum(m, dst, num_segments=x.shape[0])
            return out + x @ root + bias
        src, dst = (edge_index[0], edge_index[1])
        ew = (edge_weight - edge_weight.min()) / (edge_weight.max() - edge_weight.min() + 1e-08)
        h = jax.nn.relu(_rgcn_conv(x, src, dst, edge_type, ew, W1, root1, b1))
        h = _rgcn_conv(h, src, dst, edge_type, ew, W2, root2, b2)
        return h

    def _L3_gnn_ref(x, edge_index, W1, b1, g1, be1, W2, b2, g2, be2):
        import jax, jax.numpy as jnp
        import numpy as np
        BN_EPS = 1e-05

        def _bn(z, gamma, beta):
            mean = jnp.mean(z, axis=0)
            var = jnp.mean(jnp.square(z - mean), axis=0)
            return (z - mean) * jax.lax.rsqrt(var + BN_EPS) * gamma + beta
        N = x.shape[0]
        L = W1.shape[0]
        src, dst = (edge_index[0], edge_index[1])
        h = x
        for l in range(L):
            agg = jax.ops.segment_sum(h[src], dst, num_segments=N)
            z = h + agg
            z = jax.nn.relu(_bn(z @ W1[l] + b1[l], g1[l], be1[l])) @ W2[l] + b2[l]
            z = _bn(z, g2[l], be2[l])
            if l < L - 1:
                z = jax.nn.relu(z)
            h = z
        return h
    edge_index = jnp.stack([src, dst])
    h = jnp.maximum(_layernorm(x, axis=-1), 0.0)
    x = x + _L0_gnn_ref(h, edge_index, L0_gnn_W, L0_gnn_b)
    h = jnp.maximum(_layernorm(x, axis=-1), 0.0)
    x = x + _L1_gnn_ref(h, edge_attr_128, src, dst, L1_gnn_Wq, L1_gnn_bq, L1_gnn_Wn, L1_gnn_bn, L1_gnn_We, L1_gnn_be, L1_gnn_attn)
    h = jnp.maximum(_layernorm(x, axis=-1), 0.0)
    x = x + _L2_gnn_ref(h, edge_index, edge_type_4, edge_weight, L2_gnn_W1, L2_gnn_root1, L2_gnn_b1, L2_gnn_W2, L2_gnn_root2, L2_gnn_b2)
    h = jnp.maximum(_layernorm(x, axis=-1), 0.0)
    x = x + _L3_gnn_ref(h, edge_index, L3_gnn_W1, L3_gnn_b1, L3_gnn_g1, L3_gnn_be1, L3_gnn_W2, L3_gnn_b2, L3_gnn_g2, L3_gnn_be2)
    return x

_drawn_inputs = setup_inputs


def setup_inputs(seed=0):
    import zlib

    import numpy as np

    out = dict(_drawn_inputs(seed))
    spreads = {'L0_gnn_b': (0.0, 0.1),
     'L1_gnn_bq': (0.0, 0.729),
     'L1_gnn_bn': (0.0, 0.1),
     'L1_gnn_be': (0.0, 0.1),
     'L3_gnn_g1': (1.0, 0.2),
     'L3_gnn_be1': (0.0, 0.1),
     'L3_gnn_g2': (1.0, 0.2),
     'L3_gnn_be2': (0.0, 0.1)}
    factors = {'L3_gnn_b1': 8.0, 'L3_gnn_b2': 8.0}
    for name, (base, spread) in spreads.items():
        noise = np.random.default_rng([zlib.crc32(name.encode()), seed]).standard_normal(out[name].shape)
        drawn = base * np.exp(spread * noise) if base else spread * noise
        out[name] = jnp.asarray(drawn.astype(out[name].dtype))
    for name, factor in factors.items():
        out[name] = (out[name] * factor).astype(out[name].dtype)
    return out
```

```python
import concourse.bass as bass
from concourse import mybir
from contextlib import ExitStack, contextmanager

FP32 = mybir.dt.float32
I32 = mybir.dt.int32
ALU = mybir.AluOpType
ACT = mybir.ActivationFunctionType
AX = mybir.AxisListType

P = 128
N = 50000
E = 25000
J = 4
WIN = P * J
NWIN = -(-N // WIN)
TAIL_P = (N - (NWIN - 1) * WIN) // J
TILES = 200
GROUPS = TILES // J
EPAD = TILES * P
SWIN = EPAD // WIN
ROWS_A = P
ROWS_B = TILES - P
FULL = E // P
REST = E - FULL * P
EPS = 1e-5
SKIP = float(1 << 20)
BIG = 1e30
HP, HC = 125, N // 125
EC = EPAD // P
assert N == HP * HC and TAIL_P * J + (NWIN - 1) * WIN == N and SWIN % 2 == 0 and NWIN % 2 == 0


class Memory:
    pass


def after(eng, sem, value):
    if isinstance(value, int) and value <= 0:
        return
    eng.wait_ge(sem, value)


def bc(ap, shape):
    return ap.broadcast_to(shape)


@contextmanager
def semaphores(nc, stage, names):
    s = {n: nc.alloc_semaphore(f"{stage}_{n}_{nc.next_id()}") for n in names.split()}
    yield s
    nc.clear_and_free_semaphores([s[n] for n in s])
    nc.all_engine_barrier()


def over_windows(eng, body, windows=NWIN):
    body(0, True, False)
    with eng.Fori(1, SWIN // 2) as i:
        body(i, True, False)
    if windows == NWIN:
        with eng.Fori(SWIN // 2, NWIN // 2 - 1) as i:
            body(i, False, False)
        body(NWIN // 2 - 1, False, True)


def over_groups(eng, body):
    body(0, False)
    with eng.Fori(1, GROUPS // 2 - 1) as i:
        body(i, False)
    body(GROUPS // 2 - 1, True)


def parts(last, u):
    return TAIL_P if last and u == 1 else P


def rows(table, w, p=P):
    return table[bass.ds(w * WIN, p * J), :].rearrange("(p j) f -> p (j f)", j=J)


def jview(tile, p=P):
    return tile[:p, :].rearrange("p (j f) -> p j f", j=J)


def build(nc, a, out):
    ctx = ExitStack()
    sb = lambda name, shape, dt=FP32: ctx.enter_context(nc.sbuf_tensor(name, shape, dt))
    dram = lambda name, shape, dt=FP32: nc.dram_tensor(name, shape, dt).ap()
    with ctx:
        m = Memory()
        m.a, m.out = a, out
        m.X = dram("X", [N, P])
        m.H = dram("H", [N, P])
        m.HC = dram("HC", [EPAD + P, P])
        m.Z1 = dram("Z1", [NWIN * P, WIN])
        m.XZ = dram("XZ", [N, 2 * P])
        m.V = dram("V", [EPAD, P])
        m.HAS = dram("HAS", [N, 1])
        m.PERM = dram("PERM", [N, 1], I32)
        m.NEW = dram("NEW", [EPAD + P])
        m.LIN = dram("LIN", [EPAD])
        m.DEG = dram("DEG", [EPAD])
        m.ident = sb("ident", [P, P])
        m.upper = sb("upper", [P, P])
        m.ones = sb("ones", [P, P])
        m.zeros = sb("zeros", [P, HC])
        m.iota = sb("iota", [P, P])
        m.src_old = sb("src_old", [P, TILES], I32)
        m.src = sb("src", [P, TILES], I32)
        m.src_c = sb("src_c", [P, TILES], I32)
        m.rank = sb("rank", [P, TILES], I32)
        m.has_idx = sb("has_idx", [P, TILES], I32)
        m.local = sb("local", [P, TILES])
        m.first = sb("first", [1, TILES], I32)
        m.alpha = sb("alpha", [P, TILES])
        m.score = sb("score", [P, TILES])
        m.tw = sb("tw", [P, TILES, J])
        m.perm = sb("perm", [P, NWIN * J], I32)
        m.dis = sb("dis", [P, NWIN * J])
        m.stats = sb("stats", [P, NWIN * 6])
        m.scale = sb("scale", [P, 1])
        m.shift = sb("shift", [P, 1])
        m.scale_row = sb("scale_row", [P, P])
        m.shift_row = sb("shift_row", [P, P])
        m.bias_row = sb("bias_row", [P, P])
        m.sums = sb("sums", [P, EPAD])
        m.stage_idx = [sb(f"stage_idx{u}", [P, 8], I32) for u in range(2)]
        m.big = [sb(f"buf{k}", [P, WIN]) for k in range(14)]
        m.sm = [sb(f"small{k}", [P, 256]) for k in range(8)]
        m.pair = [sb(f"pair{u}", [P, J, 2 * P]) for u in range(2)]
        m.small_i = sb("small_i", [P, 512], I32)
        m.wide = sb("wide", [P, 4 * P])
        m.ps = [ctx.enter_context(nc.psum_tensor(f"ps{k}", [P, WIN], FP32)) for k in range(8)]

        constants(nc, m)
        edge_lists(nc, m)
        mark_receivers(nc, m)
        renumber(nc, m)
        renumber_senders(nc, m)
        relation_weights(nc, m)
        degrees(nc, m)
        permute_input(nc, m)

        node_pass(nc, m, "ln0", None, None, residual=True, scaled=True)
        for k in range(3):
            edge_pass(nc, m, "gather")
            node_pass(nc, m, "gcn", a["L0_gnn_W"], a["L0_gnn_b"], residual=k == 2)

        for k in range(3):
            attention_scores(nc, m, k)
            segment_softmax(nc, m)
            edge_pass(nc, m, "values", scaled=True)
            node_pass(nc, m, "gat", None, None, residual=k == 2)

        relation_pass(nc, m, a["L2_gnn_W1"])
        node_pass(nc, m, "rel", a["L2_gnn_root1"], a["L2_gnn_b1"], residual=False)
        relation_pass(nc, m, a["L2_gnn_W2"])
        node_pass(nc, m, "rel", a["L2_gnn_root2"], a["L2_gnn_b2"], residual=True)

        for k in range(a["L3_gnn_W1"].shape[0]):
            edge_pass(nc, m, "gather", normed=k > 0)
            gin_first(nc, m, k)
            batch_norm(nc, m, a["L3_gnn_g1"], a["L3_gnn_be1"], None, k)
            gin_second(nc, m, k)
            batch_norm(nc, m, a["L3_gnn_g2"], a["L3_gnn_be2"], a["L3_gnn_b2"], k)
        finish(nc, m)


def constants(nc, m):
    with semaphores(nc, "const", "z made zrows zinit") as s, nc.Block() as block:
        @block.gpsimd
        def _(pool):
            nc.gpsimd.memset(m.ident[:], 0.0).then_inc(s["z"], 1)
            nc.gpsimd.memset(m.ones[:], 1.0)
            nc.gpsimd.memset(m.zeros[:], 0.0).then_inc(s["zinit"], 1)
            nc.gpsimd.iota(m.iota[:], pattern=[[1, P]], base=0, channel_multiplier=0,
                           allow_small_or_imprecise_dtypes=True)
            nc.gpsimd.memset(m.upper[:], 1.0).then_inc(s["z"], 1)
            pool.wait_ge(s["z"], 2)
            nc.gpsimd.affine_select(out=m.ident[:], in_=m.ident[:], compare_op=ALU.not_equal, fill=1.0,
                                    base=0, pattern=[[-1, P]], channel_multiplier=1).then_inc(s["made"], 1)
            nc.gpsimd.affine_select(out=m.upper[:], in_=m.upper[:], compare_op=ALU.is_gt, fill=0.0,
                                    base=0, pattern=[[1, P]], channel_multiplier=-1).then_inc(s["made"], 1)
            pool.wait_ge(s["made"], 2)

        @block.sync
        def _(sp):
            sp.wait_ge(s["zinit"], 1)
            sp.dma_start(m.HC[EPAD:EPAD + P, :], m.zeros[:, :P]).then_inc(s["zrows"], 16)
            sp.dma_start(m.HAS.rearrange("(p c) o -> p (c o)", p=HP), m.zeros[:HP, :]).then_inc(s["zrows"], 16)
            sp.wait_ge(s["zrows"], 32)


def load_tiled(sp, dst_a, dst_b, vec, sem):
    sp.dma_start(dst_a, vec[0:ROWS_A * P].rearrange("(t e) -> t e", e=P)).then_inc(sem, 16)
    sp.dma_start(dst_b[0:FULL - ROWS_A, :], vec[ROWS_A * P:FULL * P].rearrange("(t e) -> t e", e=P)).then_inc(sem, 16)
    sp.dma_start(dst_b[FULL - ROWS_A:FULL - ROWS_A + 1, 0:REST],
                 vec[FULL * P:E].rearrange("(t e) -> t e", t=1)).then_inc(sem, 16)


def edge_lists(nc, m):
    A, B = slice(0, ROWS_A), slice(0, ROWS_B)
    blocks = ((0, ROWS_A), (1, ROWS_B))
    di = [m.small_i[:, 0:P], m.small_i[:, P:2 * P]]
    si = [m.small_i[:, 2 * P:3 * P], m.small_i[:, 3 * P:4 * P]]
    pi = [m.src_old[:, 0:P], m.rank[:, 0:P]]
    dst, prev, new, scan, rnk, loc, srcf, hidx, ok, tmp = (
        [m.big[k][:, 0:P], m.big[k][:, P:2 * P]] for k in range(10))
    base, cols = m.sm[0], m.sm[1]
    with semaphores(nc, "prep", "fill ld d pe pp st") as s, nc.Block() as block:
        @block.sync
        def _(sp):
            sp.wait_ge(s["fill"], 1)
            load_tiled(sp, di[0], di[1], m.a["dst"], s["ld"])
            load_tiled(sp, si[0], si[1], m.a["src"], s["ld"])
            v = m.a["dst"]
            sp.dma_start(pi[0][0:1, 1:P], v[0:P - 1].rearrange("(t e) -> t e", t=1)).then_inc(s["ld"], 16)
            sp.dma_start(pi[0][1:P, :], v[P - 1:P * ROWS_A - 1].rearrange("(t e) -> t e", e=P)).then_inc(s["ld"], 16)
            sp.dma_start(pi[1][0:FULL - ROWS_A, :], v[P * ROWS_A - 1:P * FULL - 1].rearrange("(t e) -> t e", e=P)).then_inc(s["ld"], 16)
            sp.dma_start(pi[1][FULL - ROWS_A:FULL - ROWS_A + 1, 0:REST + 1],
                         v[P * FULL - 1:E].rearrange("(t e) -> t e", t=1)).then_inc(s["ld"], 16)
            sp.wait_ge(s["st"], 1)
            sp.dma_start(m.NEW[0:ROWS_A * P].rearrange("(t e) -> t e", e=P), new[0]).then_inc(s["pp"], 16)
            sp.dma_start(m.NEW[ROWS_A * P:EPAD].rearrange("(t e) -> t e", e=P), new[1][B, :]).then_inc(s["pp"], 16)
            sp.dma_start(m.NEW[EPAD:EPAD + P].rearrange("(t e) -> t e", t=1), m.ones[0:1, :]).then_inc(s["pp"], 16)
            sp.wait_ge(s["pp"], 48)

        @block.vector
        def _(v):
            n = [0]

            def link(ins):
                n[0] += 1
                ins.then_inc(s["d"], 1)
                v.wait_ge(s["d"], n[0])

            link(nc.vector.memset(m.small_i[:, 0:2 * P], -1))
            link(nc.vector.memset(m.small_i[:, 2 * P:4 * P], 0))
            link(nc.vector.memset(pi[0], -5))
            link(nc.vector.memset(pi[1], -1))
            nc.vector.memset(cols[:], 0.0).then_inc(s["fill"], 1)
            v.wait_ge(s["ld"], 10 * 16)
            v.wait_ge(s["fill"], 1)
            for b, r in blocks:
                q = slice(0, r)
                link(nc.vector.tensor_copy(dst[b][q], di[b][q]))
                link(nc.vector.tensor_copy(prev[b][q], pi[b][q]))
                link(nc.vector.tensor_copy(srcf[b][q], si[b][q]))
                link(nc.vector.tensor_tensor(new[b][q], dst[b][q], prev[b][q], ALU.not_equal))
                link(nc.vector.tensor_tensor_scan(scan[b][q], new[b][q], m.zeros[q, 0:P], 0.0, ALU.add, ALU.add))
                link(nc.vector.tensor_copy(cols[q, b:b + 1], scan[b][q, P - 1:P]))
                link(nc.vector.tensor_scalar(ok[b][q], dst[b][q], 0.0, None, ALU.is_ge))
            nc.vector.tensor_copy(cols[:, 2:3], cols[:, 0:1]).then_inc(s["st"], 1)
            v.wait_ge(s["pe"], 1)
            link(nc.vector.tensor_scalar(base[:, 0:2], m.ps[0][:, 0:2], -1.0, None, ALU.add))
            for b, r in blocks:
                q = slice(0, r)
                link(nc.vector.tensor_scalar(rnk[b][q], scan[b][q], base[q, b:b + 1], None, ALU.add))
                link(nc.vector.tensor_scalar(loc[b][q], rnk[b][q], rnk[b][q, 0:1], 1.0, ALU.subtract, ALU.add))
                link(nc.vector.tensor_tensor(loc[b][q], loc[b][q], ok[b][q], ALU.mult))
                link(nc.vector.tensor_scalar(loc[b][q], loc[b][q], -1.0, None, ALU.add))
                link(nc.vector.tensor_tensor(tmp[b][q], new[b][q], ok[b][q], ALU.mult))
                link(nc.vector.scalar_tensor_tensor(out=hidx[b][q], in0=dst[b][q], scalar=-SKIP, in1=tmp[b][q],
                                                    op0=ALU.add, op1=ALU.mult))
                link(nc.vector.tensor_scalar(hidx[b][q], hidx[b][q], SKIP, None, ALU.add))
            nc.vector.tensor_copy(cols[:, 3:4], cols[:, 0:1]).then_inc(s["st"], 1)
            v.wait_ge(s["pe"], 2)
            link(nc.vector.tensor_copy(m.rank[:], m.ps[1][:, 0:TILES]))
            link(nc.vector.tensor_copy(m.first[:], m.ps[1][0:1, 0:TILES]))
            link(nc.vector.tensor_copy(m.local[:], m.ps[2][:, 0:TILES]))
            link(nc.vector.tensor_copy(m.src_old[:], m.ps[3][:, 0:TILES]))
            link(nc.vector.tensor_copy(m.has_idx[:], m.ps[4][:, 0:TILES]))

        @block.tensor
        def _(pe):
            pe.wait_ge(s["st"], 1)
            nc.tensor.matmul(m.ps[0][:, 0:1], m.upper[:], cols[:, 0:1], start=True, stop=True)
            nc.tensor.matmul(m.ps[0][:, 1:2], m.ones[:], cols[:, 0:1], start=True, stop=False)
            nc.tensor.matmul(m.ps[0][:, 1:2], m.upper[:], cols[:, 1:2], start=False, stop=True).then_inc(s["pe"], 1)
            pe.wait_ge(s["st"], 2)
            for k, x in enumerate((rnk, loc, srcf, hidx)):
                nc.tensor.transpose(m.ps[1 + k][:, 0:ROWS_A], x[0][A], m.ident[:])
                last = nc.tensor.transpose(m.ps[1 + k][:, ROWS_A:TILES], x[1][B], m.ident[0:ROWS_B, 0:ROWS_B])
            last.then_inc(s["pe"], 1)


def indexed_loop(nc, s, cols, stages, each, free):
    pool = nc.gpsimd

    def body(i, last):
        for u in range(2):
            free(i, u)
            stage = stages[u][:, 0:J]
            nc.gpsimd.tensor_copy(stage, cols[:, bass.ds((2 * i + u) * J, J)]).then_inc(s["idx_ready"], 1)
            pool.wait_ge(s["idx_ready"], 1)
            pool.sem_clear(s["idx_ready"])
            each(i, u, stage)
    over_groups(pool, body)


def mark_receivers(nc, m):
    with semaphores(nc, "has", "idx_ready sc0 sc1 d") as s, nc.Block() as block:
        sc = [s["sc0"], s["sc1"]]

        @block.gpsimd
        def _(pool):
            def free(i, u):
                after(pool, sc[u], i * 16 * J)

            def each(i, u, stage):
                for j in range(J):
                    pool.indirect_dma_start(
                        out=m.HAS, out_offset=bass.IndirectOffsetOnAxis(ap=stage[:, j:j + 1], axis=0),
                        in_=m.ones[:, 0:1], in_offset=None, bounds_check=N - 1, oob_is_err=False).then_inc(sc[u], 16)
            indexed_loop(nc, s, m.has_idx, m.stage_idx, each, free)
            for u in range(2):
                pool.wait_ge(sc[u], GROUPS // 2 * 16 * J)


def renumber(nc, m):
    has, inc, num, t = (m.big[k][0:HP, 0:HC] for k in range(4))
    permi = m.small_i[0:HP, 0:HC]
    with semaphores(nc, "perm", "ld d tot pe io out back") as s, nc.Block() as block:
        @block.sync
        def _(sp):
            sp.dma_start(has, m.HAS.rearrange("(p c) o -> p (c o)", p=HP)).then_inc(s["ld"], 16)
            sp.wait_ge(s["out"], 1)
            sp.dma_start(m.PERM.rearrange("(p c) o -> p (c o)", p=HP), permi).then_inc(s["back"], 16)
            sp.wait_ge(s["back"], 16)
            full = (NWIN - 1) * WIN
            sp.dma_start(m.perm[:, 0:(NWIN - 1) * J].rearrange("p (w j) -> p w j", j=J),
                         m.PERM[0:full, :].rearrange("(w p j) o -> p w (j o)", p=P, j=J)).then_inc(s["back"], 16)
            sp.dma_start(m.perm[0:TAIL_P, (NWIN - 1) * J:NWIN * J],
                         m.PERM[full:N, :].rearrange("(p j) o -> p (j o)", j=J)).then_inc(s["back"], 16)
            sp.wait_ge(s["back"], 48)

        @block.gpsimd
        def _(pool):
            nc.gpsimd.iota(num, pattern=[[1, HC]], base=0, channel_multiplier=HC,
                           allow_small_or_imprecise_dtypes=True).then_inc(s["io"], 1)

        @block.vector
        def _(v):
            n = [0]

            def link(ins):
                n[0] += 1
                ins.then_inc(s["d"], 1)
                v.wait_ge(s["d"], n[0])
            v.wait_ge(s["ld"], 16)
            link(nc.vector.tensor_tensor_scan(inc, has, m.zeros[0:HP, 0:HC], 0.0, ALU.add, ALU.add))
            nc.vector.tensor_copy(m.sm[0][0:HP, 0:1], inc[:, HC - 1:HC]).then_inc(s["tot"], 1)
            v.wait_ge(s["pe"], 1)
            link(nc.vector.tensor_copy(m.sm[1][0:HP, 0:2], m.ps[0][0:HP, 0:2]))
            link(nc.vector.tensor_scalar(inc, inc, m.sm[1][0:HP, 0:1], None, ALU.add))
            v.wait_ge(s["io"], 1)
            link(nc.vector.scalar_tensor_tensor(out=t, in0=num, scalar=m.sm[1][0:HP, 1:2], in1=inc,
                                                op0=ALU.add, op1=ALU.subtract))
            link(nc.vector.scalar_tensor_tensor(out=inc, in0=inc, scalar=-1.0, in1=t, op0=ALU.add, op1=ALU.subtract))
            link(nc.vector.tensor_tensor(inc, inc, has, ALU.mult))
            nc.vector.tensor_tensor(permi, inc, t, ALU.add).then_inc(s["out"], 1)

        @block.tensor
        def _(pe):
            pe.wait_ge(s["tot"], 1)
            nc.tensor.matmul(m.ps[0][:, 0:1], m.upper[0:HP, :], m.sm[0][0:HP, 0:1], start=True, stop=True)
            nc.tensor.matmul(m.ps[0][:, 1:2], m.ones[0:HP, :], m.sm[0][0:HP, 0:1], start=True, stop=True).then_inc(s["pe"], 1)


def renumber_senders(nc, m):
    got_i = [m.small_i[:, u * J:(u + 1) * J] for u in range(2)]
    with semaphores(nc, "src", "idx_ready g0 g1 used d") as s, nc.Block() as block:
        g = [s["g0"], s["g1"]]

        @block.gpsimd
        def _(pool):
            def free(i, u):
                after(pool, s["used"], 2 * i + u - 1)

            def each(i, u, stage):
                for j in range(J):
                    pool.indirect_dma_start(
                        out=got_i[u][:, j:j + 1], out_offset=None, in_=m.PERM,
                        in_offset=bass.IndirectOffsetOnAxis(ap=stage[:, j:j + 1], axis=0)).then_inc(g[u], 16)
            indexed_loop(nc, s, m.src_old, m.stage_idx, each, free)

        @block.vector
        def _(v):
            def body(i, last):
                for u in range(2):
                    v.wait_ge(g[u], 16 * J * (i + 1))
                    nc.vector.tensor_copy(m.src[:, bass.ds((2 * i + u) * J, J)], got_i[u]).then_inc(s["used"], 1)
            over_groups(v, body)
            v.wait_ge(s["used"], GROUPS)
            nc.vector.tensor_scalar(m.src_c[:], m.src[:], float(EPAD), None, ALU.min).then_inc(s["d"], 1)
            v.wait_ge(s["d"], 1)


def relation_weights(nc, m):
    ew = [m.big[0][:, 0:P], m.big[0][:, P:2 * P]]
    ti = [m.small_i[:, 0:P], m.small_i[:, P:2 * P]]
    tf = [m.big[1][:, 0:P], m.big[1][:, P:2 * P]]
    lin = m.big[2][0:100, 0:250]
    c = m.sm[0]
    with semaphores(nc, "types", "fill ld d a pe b") as s, nc.Block() as block:
        @block.sync
        def _(sp):
            sp.wait_ge(s["fill"], 1)
            load_tiled(sp, ew[0], ew[1], m.a["edge_weight"], s["ld"])
            load_tiled(sp, ti[0], ti[1], m.a["edge_type_4"], s["ld"])
            sp.dma_start(lin, m.a["edge_weight"].rearrange("(p c) -> p c", p=100)).then_inc(s["ld"], 16)

        @block.vector
        def _(v):
            n = [0]

            def link(ins):
                n[0] += 1
                ins.then_inc(s["d"], 1)
                v.wait_ge(s["d"], n[0])
            link(nc.vector.memset(m.big[0][:, 0:2 * P], 0.0))
            nc.vector.memset(m.small_i[:, 0:2 * P], 0).then_inc(s["fill"], 1)
            v.wait_ge(s["ld"], 7 * 16)
            link(nc.vector.tensor_copy(m.big[1][:, 0:2 * P], m.small_i[:, 0:2 * P]))
            link(nc.vector.tensor_reduce(c[0:100, 0:1], lin, AX.X, ALU.max))
            link(nc.vector.tensor_reduce(c[0:100, 1:2], lin, AX.X, ALU.min))
            nc.vector.tensor_copy(c[0:100, 2:4], c[0:100, 0:2]).then_inc(s["a"], 1)
            v.wait_ge(s["pe"], 1)
            link(nc.vector.tensor_copy(m.sm[3][:, 0:TILES], m.ps[1][:, 0:TILES]))
            link(nc.vector.tensor_copy(m.sm[4][:, 0:TILES], m.ps[2][:, 0:TILES]))
            link(nc.vector.tensor_reduce(m.sm[1][0:1, 0:1], m.ps[0][0:1, 0:100], AX.X, ALU.max))
            link(nc.vector.tensor_reduce(m.sm[1][0:1, 1:2], m.ps[3][0:1, 0:100], AX.X, ALU.min))
            link(nc.vector.tensor_tensor(m.sm[1][0:1, 2:3], m.sm[1][0:1, 0:1], m.sm[1][0:1, 1:2], ALU.subtract))
            link(nc.vector.tensor_scalar(m.sm[1][0:1, 2:3], m.sm[1][0:1, 2:3], 1e-8, None, ALU.add))
            nc.vector.reciprocal(m.sm[1][0:1, 2:3], m.sm[1][0:1, 2:3]).then_inc(s["b"], 1)
            v.wait_ge(s["pe"], 2)
            link(nc.vector.tensor_copy(m.sm[2][:, 0:2], m.ps[4][:, 0:2]))
            link(nc.vector.tensor_scalar(m.sm[3][:, 0:TILES], m.sm[3][:, 0:TILES], m.sm[2][:, 0:1], m.sm[2][:, 1:2],
                                         ALU.subtract, ALU.mult))
            for r in range(J):
                link(nc.vector.scalar_tensor_tensor(out=m.tw[:, :, r], in0=m.sm[4][:, 0:TILES], scalar=float(r),
                                                    in1=m.sm[3][:, 0:TILES], op0=ALU.is_equal, op1=ALU.mult))

        @block.tensor
        def _(pe):
            pe.wait_ge(s["a"], 1)
            for k, x in ((1, ew), (2, tf)):
                nc.tensor.transpose(m.ps[k][:, 0:ROWS_A], x[0], m.ident[:])
                nc.tensor.transpose(m.ps[k][:, ROWS_A:TILES], x[1][0:ROWS_B], m.ident[0:ROWS_B, 0:ROWS_B])
            nc.tensor.transpose(m.ps[0][0:1, 0:100], c[0:100, 2:3], m.ident[0:100, 0:100])
            nc.tensor.transpose(m.ps[3][0:1, 0:100], c[0:100, 3:4], m.ident[0:100, 0:100]).then_inc(s["pe"], 1)
            pe.wait_ge(s["b"], 1)
            nc.tensor.matmul(m.ps[4][:, 0:2], m.ones[0:1, :], m.sm[1][0:1, 1:3], start=True, stop=True).then_inc(s["pe"], 1)


def degrees(nc, m):
    edge_pass(nc, m, "ones")
    deg = m.dis
    with semaphores(nc, "deg", "io z a d") as s, nc.Block() as block:
        @block.sync
        def _(sp):
            sp.dma_start(m.DEG.rearrange("(o n) -> o n", o=1), m.sums[0:1, :]).then_inc(s["io"], 16)
            sp.wait_ge(s["io"], 16)
            sp.wait_ge(s["z"], 1)
            sp.dma_start(deg[:, 0:SWIN * J].rearrange("p (w j) -> p w j", j=J),
                         m.DEG.rearrange("(w p j) -> p w j", p=P, j=J)).then_inc(s["io"], 16)

        @block.vector
        def _(v):
            nc.vector.memset(deg[:], 0.0).then_inc(s["z"], 1)
            v.wait_ge(s["io"], 32)
            nc.vector.tensor_scalar(deg[:], deg[:], 1.0, None, ALU.add).then_inc(s["d"], 1)
            v.wait_ge(s["a"], 1)
            nc.vector.reciprocal(m.dis[:], deg[:]).then_inc(s["d"], 1)

        @block.scalar
        def _(act):
            act.wait_ge(s["d"], 1)
            nc.scalar.activation(deg[:], deg[:], ACT.Sqrt).then_inc(s["a"], 1)


def permute_input(nc, m):
    with semaphores(nc, "permx", "ld0 ld1 sc0 sc1 idx_ready") as s, nc.Block() as block:
        ld, sc = [s["ld0"], s["ld1"]], [s["sc0"], s["sc1"]]

        @block.sync
        def _(sp):
            def body(i, summed, last):
                for u in range(2):
                    p = parts(last, u)
                    after(sp, sc[u], i * 16 * J)
                    sp.dma_start(m.big[u][:p, :], rows(m.a["x"], 2 * i + u, p)).then_inc(ld[u], 16)
            over_windows(sp, body)

        @block.gpsimd
        def _(pool):
            def body(i, summed, last):
                for u in range(2):
                    p = parts(last, u)
                    pool.wait_ge(ld[u], 16 * (i + 1))
                    nc.gpsimd.tensor_copy(m.stage_idx[u][:p, 0:J], m.perm[:p, bass.ds((2 * i + u) * J, J)]).then_inc(s["idx_ready"], 1)
                    pool.wait_ge(s["idx_ready"], 1)
                    pool.sem_clear(s["idx_ready"])
                    for j in range(J):
                        pool.indirect_dma_start(
                            out=m.X, out_offset=bass.IndirectOffsetOnAxis(ap=m.stage_idx[u][:p, j:j + 1], axis=0),
                            in_=m.big[u][:p, j * P:(j + 1) * P], in_offset=None).then_inc(sc[u], 16)
            over_windows(pool, body)
            for u in range(2):
                pool.wait_ge(sc[u], NWIN // 2 * 16 * J)


def add_sums(nc, v, m, s, i, u, bank):
    g = 2 * i + u
    firsts = [v.value_load(m.first[0:1, bass.ds(g * J + j, 1)], min_val=0, max_val=EPAD - P) for j in range(J)]
    for j in range(J):
        after(v, s["added"], g * J + j)
        cols = m.sums[:, bass.ds(firsts[j], P)]
        nc.vector.tensor_tensor(cols, cols, bank[:, j * P:(j + 1) * P], ALU.add).then_inc(s["added"], 1)


def edge_pass(nc, m, source, scaled=False, normed=False):
    got_t = m.big[0:2]
    tr = m.big[2:4]
    hot = m.big[4:6]
    with semaphores(nc, "edge", "idx_ready g0 g1 g2 g3 g4 g5 g6 g7 zero hot hot2 mul tr relu mm added") as s, nc.Block() as block:
        got = [s["g0"], s["g1"], s["g2"], s["g3"], s["g4"], s["g5"], s["g6"], s["g7"]]
        if source == "gather":
            @block.gpsimd
            def _(pool):
                def free(i, u):
                    after(pool, s["mul"] if normed else s["mm"], 2 * i + u - 1)

                def each(i, u, stage):
                    for j in range(J):
                        pool.indirect_dma_start(
                            out=got_t[u][:, j * P:(j + 1) * P], out_offset=None, in_=m.H,
                            in_offset=bass.IndirectOffsetOnAxis(ap=stage[:, j:j + 1], axis=0)).then_inc(got[J * u + j], 16)
                indexed_loop(nc, s, m.src, m.stage_idx, each, free)
        if source == "values":
            @block.sync
            def _(sp):
                def body(i, last):
                    for u in range(2):
                        g = 2 * i + u
                        after(sp, s["mm"], g - 1)
                        sp.dma_start(jview(got_t[u]), m.V[bass.ds(g * WIN, WIN), :].rearrange("(j p) f -> p j f", p=P)).then_inc(got[u], 16)
                over_groups(sp, body)

        @block.vector
        def _(v):
            nc.vector.memset(m.sums[:], 0.0).then_inc(s["zero"], 1)
            v.wait_ge(s["zero"], 1)

            def body(i, last):
                for u in range(2):
                    g = 2 * i + u
                    after(v, s["mm"], g - 1)
                    nc.vector.tensor_tensor(
                        jview(hot[u]), bc(m.iota[:, :].unsqueeze(1), [P, J, P]),
                        bc(m.local[:, bass.ds(g * J, J)].unsqueeze(2), [P, J, P]), ALU.is_equal).then_inc(s["hot"], 1)
                    if scaled:
                        v.wait_ge(s["hot"], g + 1)
                        nc.vector.tensor_tensor(
                            jview(hot[u]), jview(hot[u]),
                            bc(m.alpha[:, bass.ds(g * J, J)].unsqueeze(2), [P, J, P]), ALU.mult).then_inc(s["hot2"], 1)
                    if normed:
                        for j in range(J):
                            v.wait_ge(got[J * u + j], 16 * (i + 1))
                        nc.vector.tensor_tensor(jview(tr[u]), jview(got_t[u]), bc(m.scale_row[:, :].unsqueeze(1), [P, J, P]),
                                                ALU.mult).then_inc(s["mul"], 1)
                        v.wait_ge(s["mul"], g + 1)
                        nc.vector.tensor_tensor(jview(tr[u]), jview(tr[u]), bc(m.shift_row[:, :].unsqueeze(1), [P, J, P]),
                                                ALU.add).then_inc(s["tr"], 1)
                    v.wait_ge(s["mm"], g + 1)
                    add_sums(nc, v, m, s, i, u, m.ps[u])
            over_groups(v, body)
            v.wait_ge(s["added"], TILES)

        if normed:
            @block.scalar
            def _(act):
                def body(i, last):
                    for u in range(2):
                        act.wait_ge(s["tr"], 2 * i + u + 1)
                        nc.scalar.activation(tr[u][:], tr[u][:], ACT.Relu).then_inc(s["relu"], 1)
                over_groups(act, body)

        @block.tensor
        def _(pe):
            def body(i, last):
                for u in range(2):
                    g = 2 * i + u
                    pe.wait_ge(s["hot2"] if scaled else s["hot"], g + 1)
                    if normed:
                        pe.wait_ge(s["relu"], g + 1)
                    elif source == "values":
                        pe.wait_ge(got[u], 16 * (i + 1))
                    after(pe, s["added"], (g - 1) * J)
                    for j in range(J):
                        if source == "gather" and not normed:
                            pe.wait_ge(got[J * u + j], 16 * (i + 1))
                        lhs = m.ones[:] if source == "ones" else (tr if normed else got_t)[u][:, j * P:(j + 1) * P]
                        last_mm = nc.tensor.matmul(m.ps[u][:, j * P:(j + 1) * P], lhs, hot[u][:, j * P:(j + 1) * P],
                                                   start=True, stop=True)
                    last_mm.then_inc(s["mm"], 1)
            over_groups(pe, body)


def relation_pass(nc, m, weights):
    got_t, xT, hot = m.big[0:2], m.big[2:4], m.big[4:6]
    prod, hotw = m.big[6:8], m.big[8:10]
    w4 = m.wide
    with semaphores(nc, "rel", "idx_ready g0 g1 g2 g3 g4 g5 g6 g7 zero hot w hw tp cp pr pc mm added") as s, nc.Block() as block:
        got = [s["g0"], s["g1"], s["g2"], s["g3"], s["g4"], s["g5"], s["g6"], s["g7"]]

        @block.sync
        def _(sp):
            sp.dma_start(w4[:].rearrange("p (r f) -> p r f", r=J), weights.rearrange("r i o -> i r o")).then_inc(s["w"], 16)

        @block.gpsimd
        def _(pool):
            def free(i, u):
                after(pool, s["tp"], 2 * i + u - 1)

            def each(i, u, stage):
                for j in range(J):
                    pool.indirect_dma_start(
                        out=got_t[u][:, j * P:(j + 1) * P], out_offset=None, in_=m.H,
                        in_offset=bass.IndirectOffsetOnAxis(ap=stage[:, j:j + 1], axis=0)).then_inc(got[J * u + j], 16)
            indexed_loop(nc, s, m.src, m.stage_idx, each, free)

        @block.vector
        def _(v):
            nc.vector.memset(m.sums[:], 0.0).then_inc(s["zero"], 1)
            v.wait_ge(s["zero"], 1)

            def body(i, last):
                for u in range(2):
                    g = 2 * i + u
                    after(v, s["hw"], (g - 1) * J)
                    nc.vector.tensor_tensor(
                        jview(hot[u]), bc(m.iota[:, :].unsqueeze(1), [P, J, P]),
                        bc(m.local[:, bass.ds(g * J, J)].unsqueeze(2), [P, J, P]), ALU.is_equal).then_inc(s["hot"], 1)
                    v.wait_ge(s["hot"], g + 1)
                    for j in range(J):
                        t = g * J + j
                        after(v, s["mm"], t - 1)
                        nc.vector.tensor_tensor(
                            jview(hotw[j % 2]), bc(hot[u][:, j * P:(j + 1) * P].unsqueeze(1), [P, J, P]),
                            bc(m.tw[:, bass.ds(t, 1), :].rearrange("p o r -> p (o r)").unsqueeze(2), [P, J, P]),
                            ALU.mult).then_inc(s["hw"], 1)
                    v.wait_ge(s["mm"], (g + 1) * J)
                    add_sums(nc, v, m, s, i, u, m.ps[6 + u])
            over_groups(v, body)
            v.wait_ge(s["added"], TILES)

        @block.scalar
        def _(act):
            def body(i, last):
                for u in range(2):
                    g = 2 * i + u
                    act.wait_ge(s["tp"], g + 1)
                    after(act, s["pr"], (g - 1) * J)
                    nc.scalar.activation(xT[u][:], m.ps[u][:], ACT.Copy).then_inc(s["cp"], 1)
                    for j in range(J):
                        t = g * J + j
                        act.wait_ge(s["pr"], t + 1)
                        after(act, s["mm"], t - 1)
                        nc.scalar.activation(prod[j % 2][:], m.ps[2 + j % 2][:], ACT.Copy).then_inc(s["pc"], 1)
            over_groups(act, body)

        @block.tensor
        def _(pe):
            pe.wait_ge(s["w"], 16)

            def body(i, last):
                for u in range(2):
                    g = 2 * i + u
                    after(pe, s["cp"], g - 1)
                    for j in range(J):
                        pe.wait_ge(got[J * u + j], 16 * (i + 1))
                        tp = nc.tensor.transpose(m.ps[u][:, j * P:(j + 1) * P], got_t[u][:, j * P:(j + 1) * P], m.ident[:])
                    tp.then_inc(s["tp"], 1)
                    pe.wait_ge(s["cp"], g + 1)
                    after(pe, s["added"], (g - 1) * J)

                    def product(j):
                        t = g * J + j
                        after(pe, s["pc"], t - 1)
                        nc.tensor.matmul(m.ps[2 + j % 2][:], xT[u][:, j * P:(j + 1) * P], w4[:], start=True, stop=True).then_inc(s["pr"], 1)
                    product(0)
                    for j in range(J):
                        t = g * J + j
                        if j + 1 < J:
                            product(j + 1)
                        pe.wait_ge(s["pc"], t + 1)
                        pe.wait_ge(s["hw"], t + 1)
                        for r in range(J):
                            mm = nc.tensor.matmul(m.ps[6 + u][:, j * P:(j + 1) * P], prod[j % 2][:, r * P:(r + 1) * P],
                                                  hotw[j % 2][:, r * P:(r + 1) * P], start=(r == 0), stop=(r == J - 1))
                        mm.then_inc(s["mm"], 1)
            over_groups(pe, body)


def node_pass(nc, m, kind, weight, bias, residual, scaled=False):
    table = kind in ("gcn", "rel")
    hin, hs, cw, t1 = m.big[0:2], m.big[2:4], m.big[4:6], m.big[6:8]
    xt, ho = m.big[8:10], m.big[10:12]
    st, rs, nb, ve, flag = m.sm[0], m.sm[1][:, 0:8], m.sm[2][:, 0:8], m.sm[3][:, 0:8], m.sm[4]
    w_sb = m.big[12][:, 0:P]
    windows = NWIN if (table or residual) else SWIN
    dest = m.HC if (kind == "gat" and not residual) else m.H
    pairs = windows // 2
    names = "w wb ldh0 ldh1 ldx0 ldx1 tp hs cw py yd t1 t2 t3 xs bs ba ve sq rc ds nb ho sth0 sth1 stx0 stx1"
    with semaphores(nc, "node", names) as s, nc.Block() as block:
        ldh, ldx, sth, stx = [s["ldh0"], s["ldh1"]], [s["ldx0"], s["ldx1"]], [s["sth0"], s["sth1"]], [s["stx0"], s["stx1"]]

        @block.sync
        def _(sp):
            if weight is not None:
                sp.dma_start(w_sb, weight).then_inc(s["w"], 16)
                sp.dma_start(m.bias_row[:], bc(bias.unsqueeze(0), [P, P])).then_inc(s["wb"], 16)

            def body(i, summed, last):
                for u in range(2):
                    w, p = 2 * i + u, parts(last, u)
                    if table:
                        after(sp, s["tp"], w - 1)
                        sp.dma_start(hin[u][:p], rows(m.H, w, p)).then_inc(ldh[u], 16)
                    if residual:
                        if kind != "ln0":
                            after(sp, stx[u], 16 * i)
                        after(sp, s["ho"], w - 1)
                        sp.dma_start(xt[u][:p], rows(m.X, w, p)).then_inc(ldx[u], 16)
            if table or residual:
                over_windows(sp, body, windows)

        @block.tensor
        def _(pe):
            if weight is not None:
                pe.wait_ge(s["w"], 16)

            def body(i, summed, last):
                if table:
                    for u in range(2):
                        w, p = 2 * i + u, parts(last, u)
                        pe.wait_ge(ldh[u], 16 * (i + 1))
                        after(pe, s["hs"], w - 1)
                        for j in range(J):
                            tp = nc.tensor.transpose(m.ps[u][:, j * p:(j + 1) * p], hin[u][:p, j * P:(j + 1) * P], m.ident[:p, :p])
                        tp.then_inc(s["tp"], 1)
                for u in range(2):
                    w, p = 2 * i + u, parts(last, u)
                    if kind == "gat" and not summed:
                        continue
                    if table:
                        pe.wait_ge(s["hs"], w + 1)
                    if kind in ("rel", "gat") and summed:
                        pe.wait_ge(s["cw"], w + 1)
                    after(pe, s["yd"], w - 1)
                    for j in range(J):
                        o = m.ps[2 + u][:p, j * P:(j + 1) * P]
                        if kind == "gat":
                            mm = nc.tensor.transpose(o, cw[u][:, j * P:(j + 1) * P], m.ident[:])
                            continue
                        both = kind == "rel" and summed
                        mm = nc.tensor.matmul(o, hs[u][:, j * p:(j + 1) * p], w_sb, start=True, stop=not both)
                        if both:
                            mm = nc.tensor.matmul(o, cw[u][:, j * P:(j + 1) * P], m.ident[:], start=False, stop=True)
                    mm.then_inc(s["py"], 1)
            if kind != "ln0":
                over_windows(pe, body, windows)

        @block.vector
        def _(v):
            if weight is not None:
                v.wait_ge(s["wb"], 16)

            def body(i, summed, last):
                for u in range(2):
                    w, p = 2 * i + u, parts(last, u)
                    sums = m.sums[:, bass.ds(w * WIN, WIN)].rearrange("f (p j) -> f j p", j=J) if summed else None
                    if table:
                        v.wait_ge(s["tp"], w + 1)
                        after(v, s["py"], w - 1)
                        bank = m.ps[u][:, 0:J * p]
                        if kind == "gcn" and summed:
                            nc.vector.tensor_tensor(jview(hs[u]), jview(m.ps[u]), sums, ALU.add).then_inc(s["hs"], 1)
                        else:
                            nc.vector.tensor_copy(hs[u][:, 0:J * p], bank).then_inc(s["hs"], 1)
                    if kind in ("rel", "gat") and summed:
                        after(v, s["py"], w - 1)
                        nc.vector.tensor_scalar(jview(cw[u]), sums, 0.0 if kind == "gat" else -3.4e38, None, ALU.max).then_inc(s["cw"], 1)
                for u in range(2):
                    w, p = 2 * i + u, parts(last, u)
                    dis = bc(m.dis[:p, bass.ds(w * J, J)].unsqueeze(2), [p, J, P])
                    bias_b = bc(m.bias_row[:p, :].unsqueeze(1), [p, J, P])
                    py, t, x = jview(m.ps[2 + u], p), jview(t1[u], p), jview(xt[u], p)
                    has_y = kind != "ln0" and (kind != "gat" or summed)
                    if has_y:
                        v.wait_ge(s["py"], w + 1)
                    if residual:
                        v.wait_ge(ldx[u], 16 * (i + 1))
                    if kind == "gcn":
                        nc.vector.tensor_tensor(t, py, dis, ALU.mult).then_inc(s["yd"], 1)
                        v.wait_ge(s["yd"], w + 1)
                        nc.vector.tensor_tensor(t, t, bias_b, ALU.add).then_inc(s["t1"], 1)
                        v.wait_ge(s["t1"], w + 1)
                        if residual:
                            nc.vector.scalar_tensor_tensor(out=xt[u][:p], in0=t1[u][:p], scalar=0.0, in1=xt[u][:p],
                                                           op0=ALU.max, op1=ALU.add).then_inc(s["xs"], 1)
                        else:
                            after(v, sth[u], 16 * i)
                            nc.vector.scalar_tensor_tensor(out=jview(ho[u], p), in0=t, scalar=0.0, in1=dis,
                                                           op0=ALU.max, op1=ALU.mult).then_inc(s["ho"], 1)
                    if kind == "rel":
                        after(v, s["ho"], w - 1)
                        nc.vector.tensor_tensor(t, py, bias_b, ALU.add).then_inc(s["yd"], 1)
                        if residual:
                            v.wait_ge(s["yd"], w + 1)
                            nc.vector.tensor_tensor(xt[u][:p], xt[u][:p], t1[u][:p], ALU.add).then_inc(s["xs"], 1)
                    if kind == "gat" and residual:
                        if summed:
                            nc.vector.tensor_tensor(x, x, py, ALU.add).then_inc(s["yd"], 1)
                            v.wait_ge(s["yd"], w + 1)
                        nc.vector.memset(flag[:, u:u + 1], 0.0).then_inc(s["xs"], 1)
                if not residual:
                    return
                for u in range(2):
                    w, p = 2 * i + u, parts(last, u)
                    if kind != "ln0":
                        v.wait_ge(s["xs"], w + 1)
                    after(v, s["ve"], i)
                    for j in range(J):
                        bs = nc.vector.bn_stats(st[:p, 24 * u + 6 * j:24 * u + 6 * j + 6], xt[u][:p, j * P:(j + 1) * P])
                    bs.then_inc(s["bs"], 1)
                v.wait_ge(s["bs"], 2 * i + 2)
                after(v, s["nb"], i)
                halves = st[:, 0:48].rearrange("p (k c) -> p k c", c=6)
                e, o, ee, oo = (halves[:, :, c:c + 1] for c in (1, 4, 2, 5))
                mean2, diff, sq = (st[:, 64 + 8 * c:72 + 8 * c].unsqueeze(2) for c in range(3))
                nc.vector.tensor_tensor(mean2, e, o, ALU.add)
                nc.vector.tensor_tensor(diff, e, o, ALU.subtract)
                nc.vector.tensor_tensor(sq, ee, oo, ALU.add).then_inc(s["ba"], 1)
                v.wait_ge(s["ba"], 2 * i + 1)
                nc.vector.tensor_tensor(diff, diff, diff, ALU.mult)
                nc.vector.tensor_scalar(sq, sq, 1.0 / P, EPS, ALU.mult, ALU.add).then_inc(s["ba"], 1)
                v.wait_ge(s["ba"], 2 * i + 2)
                after(v, s["sq"], i)
                nc.vector.scalar_tensor_tensor(out=ve.unsqueeze(2), in0=diff, scalar=0.25, in1=sq, op0=ALU.mult, op1=ALU.add).then_inc(s["ve"], 1)
                v.wait_ge(s["sq"], i + 1)
                after(v, s["ho"], 2 * i)
                nc.vector.reciprocal(rs, ve).then_inc(s["rc"], 1)
                v.wait_ge(s["rc"], i + 1)
                if scaled:
                    nc.vector.tensor_tensor(rs, rs, m.dis[:, bass.ds(2 * i * J, 2 * J)], ALU.mult).then_inc(s["ds"], 1)
                    v.wait_ge(s["ds"], i + 1)
                nc.vector.scalar_tensor_tensor(out=nb.unsqueeze(2), in0=mean2, scalar=-0.5, in1=rs.unsqueeze(2),
                                               op0=ALU.mult, op1=ALU.mult).then_inc(s["nb"], 1)
            over_windows(v, body, windows)

        @block.scalar
        def _(act):
            def body(i, summed, last):
                if residual:
                    for u in range(2):
                        w, p = 2 * i + u, parts(last, u)
                        if kind != "ln0":
                            act.wait_ge(s["xs"], w + 1)
                            act.dma_start(rows(m.X, w, p), xt[u][:p]).then_inc(stx[u], 16)
                    act.wait_ge(s["ve"], i + 1)
                    nc.scalar.activation(ve, ve, ACT.Sqrt).then_inc(s["sq"], 1)
                for u in range(2):
                    w, p = 2 * i + u, parts(last, u)
                    if residual:
                        act.wait_ge(s["nb"], i + 1)
                        if kind == "ln0":
                            act.wait_ge(ldx[u], 16 * (i + 1))
                        after(act, sth[u], 16 * i)
                        for j in range(J):
                            r = nc.scalar.activation(ho[u][:p, j * P:(j + 1) * P], xt[u][:p, j * P:(j + 1) * P], ACT.Relu,
                                                     bias=nb[:p, J * u + j:J * u + j + 1], scale=rs[:p, J * u + j:J * u + j + 1])
                        r.then_inc(s["ho"], 1)
                    elif kind == "rel":
                        act.wait_ge(s["yd"], w + 1)
                        after(act, sth[u], 16 * i)
                        nc.scalar.activation(ho[u][:p], t1[u][:p], ACT.Relu).then_inc(s["ho"], 1)
                    elif kind == "gat":
                        act.wait_ge(s["py"], w + 1)
                        after(act, sth[u], 16 * i)
                        nc.scalar.activation(ho[u][:], m.ps[2 + u][:], ACT.Copy).then_inc(s["yd"], 1)
                    done = s["yd"] if kind == "gat" and not residual else s["ho"]
                    act.wait_ge(done, w + 1)
                    act.dma_start(rows(dest, w, p), ho[u][:p]).then_inc(sth[u], 16)
            over_windows(act, body, windows)
            for u in range(2):
                act.wait_ge(sth[u], 16 * pairs)
                if residual and kind != "ln0":
                    act.wait_ge(stx[u], 16 * pairs)


def attention_scores(nc, m, hop):
    a = m.a
    gs, gq, ea = m.big[0:2], m.big[2:4], m.big[4:6]
    sT, qT, eT, vs, f = m.big[6], m.big[7], m.big[8], m.big[9], m.big[10]
    vt = m.big[12:14]
    wn, we, wq = (m.wide[:, k * P:(k + 1) * P] for k in range(3))
    bias = m.sm[0]
    table, idx = (m.H, m.src) if hop == 0 else (m.HC, m.src_c)
    bS, bQ, bE, bV, bF, bC, bT = m.ps[0:7]
    names = "idx_ready w g0 g1 q0 q1 e0 e1 z bb tS tQ tE cS cQ cE pV pF vs f1 f2 sc vT cc vc st0 st1"
    with semaphores(nc, "att", names) as s, nc.Block() as block:
        gS, gQ, gE, stv = [s["g0"], s["g1"]], [s["q0"], s["q1"]], [s["e0"], s["e1"]], [s["st0"], s["st1"]]

        @block.sync
        def _(sp):
            for k, x in enumerate((a["L1_gnn_Wn"], a["L1_gnn_We"], a["L1_gnn_Wq"])):
                sp.dma_start((wn, we, wq)[k], x[hop]).then_inc(s["w"], 16)
            for k, x in ((0, a["L1_gnn_bq"]), (2, a["L1_gnn_attn"]), (3, a["L1_gnn_bn"]), (4, a["L1_gnn_be"])):
                sp.dma_start(bias[:, k:k + 1], x[hop].rearrange("(f o) -> f o", o=1)).then_inc(s["w"], 16)
            sp.wait_ge(s["z"], 1)

            def body(i, last):
                for u in range(2):
                    g = 2 * i + u
                    if last and u == 1:
                        continue
                    after(sp, s["tE"], g - 1)
                    if not last:
                        sp.dma_start(jview(ea[u]), a["edge_attr_128"][bass.ds(g * WIN, WIN), :].rearrange("(j p) f -> p j f", p=P)).then_inc(gE[u], 16)
                    else:
                        full = FULL % J
                        e0 = g * WIN
                        sp.dma_start(jview(ea[u])[:, 0:full, :], a["edge_attr_128"][e0:e0 + full * P, :].rearrange("(j p) f -> p j f", p=P)).then_inc(gE[u], 16)
                        sp.dma_start(ea[u][0:REST, full * P:(full + 1) * P], a["edge_attr_128"][FULL * P:E, :]).then_inc(gE[u], 16)
            over_groups(sp, body)

        @block.gpsimd
        def _(pool):
            def body(i, last):
                for u in range(2):
                    g = 2 * i + u
                    after(pool, s["tQ"], g - 1)
                    for k, cols in ((0, idx), (1, m.rank)):
                        nc.gpsimd.tensor_copy(m.stage_idx[u][:, k * J:(k + 1) * J], cols[:, bass.ds(g * J, J)]).then_inc(s["idx_ready"], 1)
                    pool.wait_ge(s["idx_ready"], 2)
                    pool.sem_clear(s["idx_ready"])
                    for k, dst_t, sem in ((0, gs[u], gS[u]), (1, gq[u], gQ[u])):
                        for j in range(J):
                            pool.indirect_dma_start(
                                out=dst_t[:, j * P:(j + 1) * P], out_offset=None, in_=table,
                                in_offset=bass.IndirectOffsetOnAxis(ap=m.stage_idx[u][:, k * J + j:k * J + j + 1], axis=0)).then_inc(sem, 16)
            over_groups(pool, body)

        @block.tensor
        def _(pe):
            pe.wait_ge(s["w"], 7 * 16)

            def body(i, last):
                for u in range(2):
                    g = 2 * i + u
                    for tile, bank, sem, read, done, when in (
                            (ea[u], bE, gE[u], s["cE"], s["tE"], 16 * (i + 1) + (16 if last and u == 0 else 0) - (16 if last and u == 1 else 0)),
                            (gs[u], bS, gS[u], s["cS"], s["tS"], 16 * J * (i + 1)), (gq[u], bQ, gQ[u], s["cQ"], s["tQ"], 16 * J * (i + 1))):
                        pe.wait_ge(sem, when)
                        after(pe, read, g)
                        for j in range(J):
                            tp = nc.tensor.transpose(bank[:, j * P:(j + 1) * P], tile[:, j * P:(j + 1) * P], m.ident[:])
                        tp.then_inc(done, 1)
                    after(pe, s["vs"], g)
                    pe.wait_ge(s["cE"], g + 1)
                    nc.tensor.matmul(bV[:], we, eT[:], start=True, stop=False)
                    pe.wait_ge(s["cS"], g + 1)
                    nc.tensor.matmul(bV[:], wn, sT[:], start=False, stop=True).then_inc(s["pV"], 1)
                    pe.wait_ge(s["cQ"], g + 1)
                    after(pe, s["f1"], g)
                    nc.tensor.matmul(bF[:], wq, qT[:], start=True, stop=True).then_inc(s["pF"], 1)
                    pe.wait_ge(s["vs"], g + 1)
                    after(pe, s["vc"], g)
                    for j in range(J):
                        t = nc.tensor.transpose(bT[:, j * P:(j + 1) * P], vs[:, j * P:(j + 1) * P], m.ident[:])
                    t.then_inc(s["vT"], 1)
                    pe.wait_ge(s["f2"], g + 1)
                    after(pe, s["cc"], g)
                    for j in range(J):
                        t = nc.tensor.matmul(bC[:, j:j + 1], f[:, j * P:(j + 1) * P], bias[:, 2:3], start=True, stop=True)
                    t.then_inc(s["sc"], 1)
            over_groups(pe, body)

        @block.scalar
        def _(act):
            act.wait_ge(s["bb"], 1)

            def body(i, last):
                for u in range(2):
                    g = 2 * i + u
                    act.wait_ge(s["tE"], g + 1)
                    after(act, s["pV"], g)
                    nc.scalar.activation(eT[:], bE[:], ACT.Copy).then_inc(s["cE"], 1)
                    act.wait_ge(s["tS"], g + 1)
                    nc.scalar.activation(sT[:], bS[:], ACT.Copy).then_inc(s["cS"], 1)
                    act.wait_ge(s["pV"], g + 1)
                    after(act, s["f1"], g)
                    after(act, s["vT"], g)
                    nc.scalar.activation(vs[:], bV[:], ACT.Identity, bias=bias[:, 1:2]).then_inc(s["vs"], 1)
                    act.wait_ge(s["vT"], g + 1)
                    after(act, stv[u], 16 * i)
                    nc.scalar.activation(vt[u][:], bT[:], ACT.Copy).then_inc(s["vc"], 1)
                    act.wait_ge(s["vc"], g + 1)
                    act.dma_start(m.V[bass.ds(g * WIN, WIN), :].rearrange("(j p) f -> p j f", p=P), jview(vt[u])).then_inc(stv[u], 16)
            over_groups(act, body)
            for u in range(2):
                act.wait_ge(stv[u], 16 * GROUPS // 2)

        @block.vector
        def _(v):
            nc.vector.memset(ea[0][:], 0.0)
            nc.vector.memset(ea[1][:], 0.0).then_inc(s["z"], 1)
            v.wait_ge(s["w"], 7 * 16)
            nc.vector.tensor_tensor(bias[:, 1:2], bias[:, 3:4], bias[:, 4:5], ALU.add).then_inc(s["bb"], 1)

            def body(i, last):
                for u in range(2):
                    g = 2 * i + u
                    v.wait_ge(s["tQ"], g + 1)
                    after(v, s["pF"], g)
                    nc.vector.tensor_copy(qT[:], bQ[:]).then_inc(s["cQ"], 1)
                    v.wait_ge(s["pF"], g + 1)
                    v.wait_ge(s["vs"], g + 1)
                    after(v, s["sc"], g)
                    nc.vector.scalar_tensor_tensor(out=f[:], in0=bF[:], scalar=bias[:, 0:1], in1=vs[:],
                                                   op0=ALU.add, op1=ALU.add).then_inc(s["f1"], 1)
                    v.wait_ge(s["f1"], g + 1)
                    nc.vector.scalar_tensor_tensor(out=f[:], in0=f[:], scalar=0.2, in1=f[:],
                                                   op0=ALU.mult, op1=ALU.max).then_inc(s["f2"], 1)
                    v.wait_ge(s["sc"], g + 1)
                    nc.vector.tensor_copy(m.score[:, bass.ds(g * J, J)], bC[:, 0:J]).then_inc(s["cc"], 1)
            over_groups(v, body)


def segment_softmax(nc, m):
    sc, fw, new, nxt, pen, penn, keep, tot = (m.big[k][:, 0:EC] for k in range(8))
    col, row = m.sm[1], m.sm[2]
    with semaphores(nc, "soft", "pa pb io d vp pv va av") as s, nc.Block() as block:
        @block.sync
        def _(sp):
            sp.dma_start(new, m.NEW[0:EPAD].rearrange("(p c) -> p c", c=EC)).then_inc(s["io"], 16)
            sp.dma_start(nxt, m.NEW[1:EPAD + 1].rearrange("(p c) -> p c", c=EC)).then_inc(s["io"], 16)
            sp.wait_ge(s["pb"], 1)
            sp.dma_start(m.LIN[0:ROWS_A * P].rearrange("(t e) -> t e", e=P), m.big[8][:, 0:P]).then_inc(s["io"], 16)
            sp.dma_start(m.LIN[ROWS_A * P:EPAD].rearrange("(t e) -> t e", e=P), m.big[8][0:ROWS_B, P:2 * P]).then_inc(s["io"], 16)
            sp.wait_ge(s["io"], 64)
            sp.dma_start(sc, m.LIN.rearrange("(p c) -> p c", c=EC)).then_inc(s["io"], 16)
            sp.wait_ge(s["pb"], 2)
            sp.dma_start(m.LIN.rearrange("(p c) -> p c", c=EC), tot).then_inc(s["io"], 16)
            sp.wait_ge(s["io"], 96)
            sp.dma_start(m.big[8][:, 0:P], m.LIN[0:ROWS_A * P].rearrange("(t e) -> t e", e=P)).then_inc(s["io"], 16)
            sp.dma_start(m.big[8][0:ROWS_B, P:2 * P], m.LIN[ROWS_A * P:EPAD].rearrange("(t e) -> t e", e=P)).then_inc(s["io"], 16)

        @block.tensor
        def _(pe):
            nc.tensor.transpose(m.ps[0][:, 0:P], m.score[:, 0:ROWS_A], m.ident[:])
            nc.tensor.transpose(m.ps[0][0:ROWS_B, P:2 * P], m.score[:, ROWS_A:TILES], m.ident[:]).then_inc(s["pa"], 1)
            for k in range(4):
                pe.wait_ge(s["vp"], 2 * k + 1)
                nc.tensor.transpose(m.ps[1][0:1, 0:P], col[:, 0:1], m.ident[:])
                nc.tensor.transpose(m.ps[1][0:1, P:2 * P], col[:, 1:2], m.ident[:]).then_inc(s["pv"], 1)
                pe.wait_ge(s["vp"], 2 * k + 2)
                nc.tensor.transpose(m.ps[2][:, 0:1], row[0:1, 0:P], m.ident[0:1, 0:1]).then_inc(s["pv"], 1)
            pe.wait_ge(s["io"], 128)
            nc.tensor.transpose(m.ps[3][:, 0:ROWS_A], m.big[8][:, 0:P], m.ident[:])
            nc.tensor.transpose(m.ps[3][:, ROWS_A:TILES], m.big[8][0:ROWS_B, P:2 * P], m.ident[0:ROWS_B, 0:ROWS_B]).then_inc(s["pa"], 1)

        @block.scalar
        def _(act):
            act.wait_ge(s["va"], 1)
            nc.scalar.activation(sc, sc, ACT.Exp).then_inc(s["av"], 1)

        @block.vector
        def _(v):
            n = [0]

            def link(ins):
                n[0] += 1
                ins.then_inc(s["d"], 1)
                v.wait_ge(s["d"], n[0])

            def rev(x):
                return x[:, ::-1]

            k = [0]

            def scan(dst, stop_, x, backward, op0, op1, unit):
                r = rev if backward else (lambda y: y)
                link(nc.vector.tensor_tensor_scan(r(dst), r(stop_), r(x), unit, op0, op1))
                end = 0 if backward else EC - 1
                link(nc.vector.tensor_copy(col[:, 0:1], dst[:, end:end + 1]))
                link(nc.vector.tensor_reduce(col[:, 1:2], stop_, AX.X, ALU.min))
                nc.vector.memset(row[0:1, 0:P], unit).then_inc(s["vp"], 1)
                k[0] += 1
                v.wait_ge(s["pv"], k[0])
                v.wait_ge(s["vp"], k[0])
                link(nc.vector.tensor_copy(row[0:1, P:2 * P], m.ps[1][0:1, P:2 * P]))
                link(nc.vector.tensor_copy(m.sm[3][0:1, 0:P], m.ps[1][0:1, 0:P]))
                link(nc.vector.tensor_tensor_scan(r(m.sm[3][0:1, P:2 * P]), r(row[0:1, P:2 * P]), r(m.sm[3][0:1, 0:P]),
                                                  unit, op0, op1))
                if backward:
                    nc.vector.tensor_copy(row[0:1, 0:P - 1], m.sm[3][0:1, P + 1:2 * P]).then_inc(s["vp"], 1)
                else:
                    nc.vector.tensor_copy(row[0:1, 1:P], m.sm[3][0:1, P:2 * P - 1]).then_inc(s["vp"], 1)
                k[0] += 1
                v.wait_ge(s["pv"], k[0])
                link(nc.vector.tensor_copy(col[:, 2:3], m.ps[2][:, 0:1]))
                link(nc.vector.tensor_tensor_scan(r(dst), r(stop_), r(x), col[:, 2:3], op0, op1))

            v.wait_ge(s["pa"], 1)
            link(nc.vector.tensor_copy(m.big[8][:, 0:P], m.ps[0][:, 0:P]))
            nc.vector.tensor_copy(m.big[8][0:ROWS_B, P:2 * P], m.ps[0][0:ROWS_B, P:2 * P]).then_inc(s["pb"], 1)
            v.wait_ge(s["io"], 80)
            link(nc.vector.tensor_scalar(pen, new, -BIG, None, ALU.mult))
            link(nc.vector.tensor_scalar(penn, nxt, -BIG, None, ALU.mult))
            link(nc.vector.tensor_scalar(keep, new, -1.0, 1.0, ALU.mult, ALU.add))
            scan(fw, pen, sc, False, ALU.add, ALU.max, -BIG)
            scan(tot, penn, fw, True, ALU.add, ALU.max, -BIG)
            nc.vector.tensor_tensor(sc, sc, tot, ALU.subtract).then_inc(s["va"], 1)
            v.wait_ge(s["av"], 1)
            scan(fw, keep, sc, False, ALU.mult, ALU.add, 0.0)
            scan(tot, penn, fw, True, ALU.add, ALU.max, -BIG)
            link(nc.vector.reciprocal(tot, tot))
            nc.vector.tensor_tensor(tot, tot, sc, ALU.mult).then_inc(s["pb"], 1)
            v.wait_ge(s["pa"], 2)
            nc.vector.tensor_copy(m.alpha[:], m.ps[3][:, 0:TILES]).then_inc(s["va"], 1)


def gin_first(nc, m, layer):
    hin, hT, z = m.big[0:2], m.big[2:4], m.big[4:6]
    w_sb, b = m.big[12][:, 0:P], m.sm[0]
    with semaphores(nc, "gin1", "w ldh0 ldh1 tp hT hs pz z1 bs st0 st1") as s, nc.Block() as block:
        ldh, stz = [s["ldh0"], s["ldh1"]], [s["st0"], s["st1"]]

        @block.sync
        def _(sp):
            sp.dma_start(w_sb, m.a["L3_gnn_W1"][layer]).then_inc(s["w"], 16)
            sp.dma_start(b[:, 0:1], m.a["L3_gnn_b1"][layer].rearrange("(f o) -> f o", o=1)).then_inc(s["w"], 16)

            def body(i, summed, last):
                for u in range(2):
                    w, p = 2 * i + u, parts(last, u)
                    after(sp, s["tp"], w - 1)
                    sp.dma_start(hin[u][:p], rows(m.H, w, p)).then_inc(ldh[u], 16)
            over_windows(sp, body)

        @block.tensor
        def _(pe):
            pe.wait_ge(s["w"], 32)

            def body(i, summed, last):
                for u in range(2):
                    w, p = 2 * i + u, parts(last, u)
                    pe.wait_ge(ldh[u], 16 * (i + 1))
                    after(pe, s["hT"], w - 1)
                    for j in range(J):
                        t = nc.tensor.transpose(m.ps[u][:, j * p:(j + 1) * p], hin[u][:p, j * P:(j + 1) * P], m.ident[:p, :p])
                    t.then_inc(s["tp"], 1)
                for u in range(2):
                    w, p = 2 * i + u, parts(last, u)
                    pe.wait_ge(s["hs"], w + 1)
                    after(pe, s["z1"], w - 1)
                    nc.tensor.matmul(m.ps[2 + u][:, 0:J * p], w_sb, hT[u][:, 0:J * p], start=True, stop=True).then_inc(s["pz"], 1)
            over_windows(pe, body)

        @block.scalar
        def _(act):
            act.wait_ge(s["w"], 32)

            def body(i, summed, last):
                for u in range(2):
                    w, c = 2 * i + u, J * parts(last, u)
                    act.wait_ge(s["tp"], w + 1)
                    after(act, s["pz"], w - 1)
                    if layer:
                        nc.scalar.activation(hT[u][:, 0:c], m.ps[u][:, 0:c], ACT.Relu, bias=m.shift[:], scale=m.scale[:]).then_inc(s["hT"], 1)
                    else:
                        nc.scalar.activation(hT[u][:, 0:c], m.ps[u][:, 0:c], ACT.Copy).then_inc(s["hT"], 1)
                for u in range(2):
                    w, c = 2 * i + u, J * parts(last, u)
                    act.wait_ge(s["pz"], w + 1)
                    after(act, s["bs"], w - 1)
                    after(act, stz[u], 16 * i)
                    nc.scalar.activation(z[u][:, 0:c], m.ps[2 + u][:, 0:c], ACT.Identity, bias=b[:, 0:1]).then_inc(s["z1"], 1)
                    act.wait_ge(s["z1"], w + 1)
                    act.dma_start(m.Z1[bass.ds(w * P, P), 0:c], z[u][:, 0:c]).then_inc(stz[u], 16)
            over_windows(act, body)
            for u in range(2):
                act.wait_ge(stz[u], 16 * NWIN // 2)

        @block.vector
        def _(v):
            def body(i, summed, last):
                for u in range(2):
                    w = 2 * i + u
                    v.wait_ge(s["hT"], w + 1)
                    if summed:
                        sums = m.sums[:, bass.ds(w * WIN, WIN)].rearrange("f (p j) -> f j p", j=J)
                        nc.vector.tensor_tensor(jview(hT[u]), jview(hT[u]), sums, ALU.add).then_inc(s["hs"], 1)
                    else:
                        nc.vector.memset(m.sm[1][:, u:u + 1], 0.0).then_inc(s["hs"], 1)
                for u in range(2):
                    w, c = 2 * i + u, J * parts(last, u)
                    v.wait_ge(s["z1"], w + 1)
                    nc.vector.bn_stats(m.stats[:, bass.ds(w * 6, 6)], z[u][:, 0:c]).then_inc(s["bs"], 1)
            over_windows(v, body)
            v.wait_ge(s["bs"], NWIN)


def batch_norm(nc, m, gamma, beta, extra, layer):
    p = m.sm[0]
    with semaphores(nc, "bn", "ld d v a pe") as s, nc.Block() as block:
        @block.sync
        def _(sp):
            for k, x in enumerate((gamma, beta, extra)):
                if x is not None:
                    sp.dma_start(p[:, k:k + 1], x[layer].rearrange("(f o) -> f o", o=1)).then_inc(s["ld"], 16)

        @block.scalar
        def _(act):
            act.wait_ge(s["v"], 1)
            nc.scalar.activation(p[:, 5:6], p[:, 4:5], ACT.Sqrt).then_inc(s["a"], 1)

        @block.tensor
        def _(pe):
            pe.wait_ge(s["v"], 2)
            nc.tensor.matmul(m.ps[0][:, 0:P], m.sm[1][:, 0:P], m.ident[:], start=True, stop=True)
            nc.tensor.matmul(m.ps[0][:, P:2 * P], m.sm[2][:, 0:P], m.ident[:], start=True, stop=True).then_inc(s["pe"], 1)

        @block.vector
        def _(v):
            n = [0]

            def link(ins):
                n[0] += 1
                ins.then_inc(s["d"], 1)
                v.wait_ge(s["d"], n[0])
            link(nc.vector.bn_aggr(p[:, 3:5], m.stats[:]))
            v.wait_ge(s["ld"], 16 * (2 if extra is None else 3))
            nc.vector.tensor_scalar(p[:, 4:5], p[:, 4:5], EPS, None, ALU.add).then_inc(s["v"], 1)
            if extra is not None:
                link(nc.vector.tensor_tensor(p[:, 3:4], p[:, 3:4], p[:, 2:3], ALU.add))
            v.wait_ge(s["a"], 1)
            link(nc.vector.reciprocal(p[:, 6:7], p[:, 5:6]))
            link(nc.vector.tensor_tensor(m.scale[:], p[:, 6:7], p[:, 0:1], ALU.mult))
            link(nc.vector.tensor_tensor(p[:, 7:8], p[:, 3:4], m.scale[:], ALU.mult))
            link(nc.vector.tensor_tensor(m.shift[:], p[:, 1:2], p[:, 7:8], ALU.subtract))
            link(nc.vector.tensor_scalar(m.sm[1][:, 0:P], m.ones[:], m.scale[:], None, ALU.mult))
            nc.vector.tensor_scalar(m.sm[2][:, 0:P], m.ones[:], m.shift[:], None, ALU.mult).then_inc(s["v"], 1)
            v.wait_ge(s["pe"], 1)
            link(nc.vector.tensor_copy(m.scale_row[:], m.ps[0][:, 0:P]))
            link(nc.vector.tensor_copy(m.shift_row[:], m.ps[0][:, P:2 * P]))


def gin_second(nc, m, layer):
    final = layer == m.a["L3_gnn_W1"].shape[0] - 1
    zin, act_t, ho = m.big[0:2], m.big[2:4], [m.big[6], m.big[8]]
    xz = m.pair
    w_sb = m.big[12][:, 0:P]
    with semaphores(nc, "gin2", "w wb ld0 ld1 lx0 lx1 a py pz ho bs st0 st1") as s, nc.Block() as block:
        ld, lx, sto = [s["ld0"], s["ld1"]], [s["lx0"], s["lx1"]], [s["st0"], s["st1"]]

        @block.sync
        def _(sp):
            sp.dma_start(w_sb, m.a["L3_gnn_W2"][layer]).then_inc(s["w"], 16)
            sp.dma_start(m.bias_row[:], bc(m.a["L3_gnn_b2"][layer].unsqueeze(0), [P, P])).then_inc(s["wb"], 16)

            def body(i, summed, last):
                for u in range(2):
                    w, p = 2 * i + u, parts(last, u)
                    after(sp, s["a"], w - 1)
                    sp.dma_start(zin[u][:, 0:J * p], m.Z1[bass.ds(w * P, P), 0:J * p]).then_inc(ld[u], 16)
                    if final:
                        after(sp, sto[u], 16 * i)
                        sp.dma_start(xz[u][:p, :, 0:P], m.X[bass.ds(w * WIN, p * J), :].rearrange("(p j) f -> p j f", j=J)).then_inc(lx[u], 16)
            over_windows(sp, body)

        @block.scalar
        def _(act):
            def body(i, summed, last):
                for u in range(2):
                    w, c = 2 * i + u, J * parts(last, u)
                    act.wait_ge(ld[u], 16 * (i + 1))
                    after(act, s["pz"], w - 1)
                    nc.scalar.activation(act_t[u][:, 0:c], zin[u][:, 0:c], ACT.Relu, bias=m.shift[:], scale=m.scale[:]).then_inc(s["a"], 1)
                for u in range(2):
                    w, p = 2 * i + u, parts(last, u)
                    act.wait_ge(s["ho"], w + 1)
                    if final:
                        act.wait_ge(lx[u], 16 * (i + 1))
                        act.dma_start(m.XZ[bass.ds(w * WIN, p * J), :].rearrange("(p j) f -> p (j f)", j=J),
                                      xz[u][:p].rearrange("p j f -> p (j f)")).then_inc(sto[u], 16)
                    else:
                        act.dma_start(rows(m.H, w, p), ho[u][:p]).then_inc(sto[u], 16)
            over_windows(act, body)
            for u in range(2):
                act.wait_ge(sto[u], 16 * NWIN // 2)

        @block.tensor
        def _(pe):
            pe.wait_ge(s["w"], 16)

            def body(i, summed, last):
                for u in range(2):
                    w, p = 2 * i + u, parts(last, u)
                    pe.wait_ge(s["a"], w + 1)
                    after(pe, s["ho"], w - 1)
                    for j in range(J):
                        t = nc.tensor.matmul(m.ps[u][:p, j * P:(j + 1) * P], act_t[u][:, j * p:(j + 1) * p], w_sb, start=True, stop=True)
                    t.then_inc(s["py"], 1)
                    after(pe, s["bs"], w - 1)
                    nc.tensor.matmul(m.ps[2 + u][:, 0:J * p], w_sb, act_t[u][:, 0:J * p], start=True, stop=True).then_inc(s["pz"], 1)
            over_windows(pe, body)

        @block.vector
        def _(v):
            v.wait_ge(s["wb"], 16)

            def body(i, summed, last):
                for u in range(2):
                    w, p = 2 * i + u, parts(last, u)
                    v.wait_ge(s["py"], w + 1)
                    after(v, sto[u], 16 * i)
                    dst = xz[u][:p, :, P:2 * P] if final else jview(ho[u], p)
                    nc.vector.tensor_tensor(dst, jview(m.ps[u], p), bc(m.bias_row[:p, :].unsqueeze(1), [p, J, P]), ALU.add).then_inc(s["ho"], 1)
                    v.wait_ge(s["pz"], w + 1)
                    nc.vector.bn_stats(m.stats[:, bass.ds(w * 6, 6)], m.ps[2 + u][:, 0:J * p]).then_inc(s["bs"], 1)
            over_windows(v, body)
            v.wait_ge(s["bs"], NWIN)


def finish(nc, m):
    xz, o = m.pair, [m.big[6], m.big[8]]
    with semaphores(nc, "fin", "idx_ready g0 g1 t1 t2 t3 st0 st1") as s, nc.Block() as block:
        g, sto = [s["g0"], s["g1"]], [s["st0"], s["st1"]]

        @block.gpsimd
        def _(pool):
            def body(i, summed, last):
                for u in range(2):
                    w, p = 2 * i + u, parts(last, u)
                    after(pool, s["t3"], w - 1)
                    nc.gpsimd.tensor_copy(m.stage_idx[u][:p, 0:J], m.perm[:p, bass.ds(w * J, J)]).then_inc(s["idx_ready"], 1)
                    pool.wait_ge(s["idx_ready"], 1)
                    pool.sem_clear(s["idx_ready"])
                    for j in range(J):
                        pool.indirect_dma_start(
                            out=xz[u][:p, j, :], out_offset=None, in_=m.XZ,
                            in_offset=bass.IndirectOffsetOnAxis(ap=m.stage_idx[u][:p, j:j + 1], axis=0)).then_inc(g[u], 16)
            over_windows(pool, body)

        @block.vector
        def _(v):
            def body(i, summed, last):
                for u in range(2):
                    w, p = 2 * i + u, parts(last, u)
                    v.wait_ge(g[u], 16 * J * (i + 1))
                    after(v, sto[u], 16 * i)
                    x, z, t = xz[u][:p, :, 0:P], xz[u][:p, :, P:2 * P], jview(o[u], p)
                    nc.vector.tensor_tensor(t, z, bc(m.scale_row[:p, :].unsqueeze(1), [p, J, P]), ALU.mult).then_inc(s["t1"], 1)
                    v.wait_ge(s["t1"], w + 1)
                    nc.vector.tensor_tensor(t, t, bc(m.shift_row[:p, :].unsqueeze(1), [p, J, P]), ALU.add).then_inc(s["t2"], 1)
                    v.wait_ge(s["t2"], w + 1)
                    nc.vector.tensor_tensor(t, t, x, ALU.add).then_inc(s["t3"], 1)
            over_windows(v, body)

        @block.sync
        def _(sp):
            def body(i, summed, last):
                for u in range(2):
                    w, p = 2 * i + u, parts(last, u)
                    sp.wait_ge(s["t3"], w + 1)
                    sp.dma_start(rows(m.out, w, p), o[u][:p]).then_inc(sto[u], 16)
            over_windows(sp, body)
            for u in range(2):
                sp.wait_ge(sto[u], 16 * NWIN // 2)


INPUTS = ["x", "src", "dst", "edge_attr_128", "edge_type_4", "edge_weight", "L0_gnn_W", "L0_gnn_b", "L1_gnn_Wq",
          "L1_gnn_bq", "L1_gnn_Wn", "L1_gnn_bn", "L1_gnn_We", "L1_gnn_be", "L1_gnn_attn", "L2_gnn_W1", "L2_gnn_root1",
          "L2_gnn_b1", "L2_gnn_W2", "L2_gnn_root2", "L2_gnn_b2", "L3_gnn_W1", "L3_gnn_b1", "L3_gnn_g1", "L3_gnn_be1",
          "L3_gnn_W2", "L3_gnn_b2", "L3_gnn_g2", "L3_gnn_be2"]


def kernel(**inputs):
    import numpy as _np
    import concourse.bacc as _bacc
    from concourse import mybir as _mybir
    from concourse.bass_utils import run_bass_kernel_spmd as _run

    nc = _bacc.Bacc("TRN2", target_bir_lowering=False, num_devices=1)
    arrays, aps = {}, {}
    for name in INPUTS:
        arr = _np.ascontiguousarray(inputs[name])
        arrays[f"in_{name}_dram"] = arr
        aps[name] = nc.dram_tensor(f"in_{name}_dram", arr.shape, _mybir.dt.from_np(arr.dtype), kind="ExternalInput").ap()
    out = nc.dram_tensor("out_dram", (N, P), _mybir.dt.float32, kind="ExternalOutput").ap()
    build(nc, aps, out)
    r = _run(nc, [arrays], core_ids=[0])
    return r.results[0]["out_dram"]
```

```python
import concourse.bass as bass
from concourse import mybir
from contextlib import ExitStack, contextmanager

FP32 = mybir.dt.float32
I32 = mybir.dt.int32
ALU = mybir.AluOpType
ACT = mybir.ActivationFunctionType
AX = mybir.AxisListType

P = 128
N = 50000
E = 25000
J = 4
WIN = P * J
NWIN = -(-N // WIN)
TAIL_P = (N - (NWIN - 1) * WIN) // J
TILES = 200
GROUPS = TILES // J
EPAD = TILES * P
U = 4
SWIN = -(-EPAD // (WIN * U)) * U
SCOLS = SWIN * WIN
ITERS = -(-NWIN // U)
ROWS_A = P
ROWS_B = TILES - P
FULL = E // P
REST = E - FULL * P
STEP = 256
EPS = 1e-5
SKIP = float(1 << 20)
BIG = 1e30
HP, HC = 125, N // 125
EC = EPAD // P
assert N == HP * HC and TAIL_P * J + (NWIN - 1) * WIN == N and NWIN % U == 2


class Memory:
    pass


def after(eng, sem, value):
    if isinstance(value, int) and value <= 0:
        return
    eng.wait_ge(sem, value)


def bc(ap, shape):
    return ap.broadcast_to(shape)


@contextmanager
def semaphores(nc, stage, names):
    s = {n: nc.alloc_semaphore(f"{stage}_{n}_{nc.next_id()}") for n in names.split()}
    yield s
    nc.clear_and_free_semaphores([s[n] for n in s])
    nc.all_engine_barrier()


def over_windows(eng, body, windows=NWIN):
    body(0, True, False)
    with eng.Fori(1, SWIN // U) as i:
        body(i, True, False)
    if windows == NWIN:
        with eng.Fori(SWIN // U, ITERS - 1) as i:
            body(i, False, False)
        body(ITERS - 1, False, True)


def clear_sums(nc, pool, m, used):
    def body(i, summed, last):
        for u in range(U):
            w = U * i + u
            pool.wait_ge(used, w + 1)
            nc.gpsimd.tensor_copy(m.sums[:, bass.ds(w * WIN, WIN)], bc(m.zeros[:, 0:1], [P, WIN]))
    over_windows(pool, body, SWIN)


def slots(last):
    return range(NWIN % U if last else U)


def rounds(u, windows=NWIN):
    return -(-(windows - u) // U)


def over_groups(eng, body):
    body(0, False)
    with eng.Fori(1, GROUPS // 2 - 1) as i:
        body(i, False)
    body(GROUPS // 2 - 1, True)


def parts(last, u):
    return TAIL_P if last and u == 1 else P


def rows(table, w, p=P):
    return table[bass.ds(w * WIN, p * J), :].rearrange("(p j) f -> p (j f)", j=J)


def jview(tile, p=P):
    return tile[:p, :].rearrange("p (j f) -> p j f", j=J)


def build(nc, a, out):
    ctx = ExitStack()
    sb = lambda name, shape, dt=FP32: ctx.enter_context(nc.sbuf_tensor(name, shape, dt))
    dram = lambda name, shape, dt=FP32: nc.dram_tensor(name, shape, dt).ap()
    with ctx:
        m = Memory()
        m.a, m.out = a, out
        m.X = dram("X", [N, P])
        m.H = dram("H", [N, P])
        m.HC = dram("HC", [SCOLS + P, P])
        m.Z1 = dram("Z1", [NWIN * P, WIN])
        m.XZ = dram("XZ", [N, 2 * P])
        m.V = dram("V", [EPAD, P])
        m.HAS = dram("HAS", [N, 1])
        m.PERM = dram("PERM", [N, 1], I32)
        m.NEW = dram("NEW", [EPAD + P])
        m.LIN = dram("LIN", [EPAD])
        m.DEG = dram("DEG", [SCOLS])
        m.ident = sb("ident", [P, P])
        m.upper = sb("upper", [P, P])
        m.ones = sb("ones", [P, P])
        m.zeros = sb("zeros", [P, HC])
        m.iota = sb("iota", [P, P])
        m.src_old = sb("src_old", [P, TILES], I32)
        m.src = sb("src", [P, TILES], I32)
        m.src_c = sb("src_c", [P, TILES], I32)
        m.rank = sb("rank", [P, TILES], I32)
        m.has_idx = sb("has_idx", [P, TILES], I32)
        m.local = sb("local", [P, TILES])
        m.first = sb("first", [1, GROUPS], I32)
        m.steps = sb("steps", [1, GROUPS], I32)
        m.zero_k = sb("zero_k", [1, WIN], mybir.dt.bfloat16)
        m.alpha = sb("alpha", [P, TILES])
        m.score = sb("score", [P, TILES])
        m.tw = sb("tw", [P, TILES, J])
        m.perm = sb("perm", [P, NWIN * J], I32)
        m.dis = sb("dis", [P, NWIN * J])
        m.stats = sb("stats", [P, NWIN * 6])
        m.scale = sb("scale", [P, 1])
        m.shift = sb("shift", [P, 1])
        m.scale_row = sb("scale_row", [P, P])
        m.shift_row = sb("shift_row", [P, P])
        m.bias_row = sb("bias_row", [P, P])
        m.sums = sb("sums", [P, SCOLS])
        m.stage_idx = [sb(f"stage_idx{u}", [P, 8], I32) for u in range(U)]
        m.work = sb("work", [P, 6 * U, WIN])
        m.big = [m.work[:, k, :] for k in range(6 * U)]
        m.sm = [sb(f"small{k}", [P, 256]) for k in range(5)]
        m.w_sb = sb("w_sb", [P, P])
        m.small_i = sb("small_i", [P, 512], I32)
        m.pair = [m.work[:, 4 * U + 2 * u:4 * U + 2 * u + 2, :].rearrange("p a (b f) -> p (a b) f", f=2 * P) for u in range(U // 2)]
        m.pair += [m.work[:, 3 * U + 2 * u:3 * U + 2 * u + 2, :].rearrange("p a (b f) -> p (a b) f", f=2 * P) for u in range(U // 2)]
        m.wide = sb("wide", [P, 4 * P])
        m.ps = [ctx.enter_context(nc.psum_tensor(f"ps{k}", [P, WIN], FP32)) for k in range(8)]

        constants(nc, m)
        edge_lists(nc, m)
        mark_receivers(nc, m)
        renumber(nc, m)
        renumber_senders(nc, m)
        relation_weights(nc, m)
        degrees(nc, m)
        permute_input(nc, m)

        node_pass(nc, m, "ln0", None, None, residual=True, scaled=True)
        for k in range(3):
            edge_pass(nc, m, "gather")
            node_pass(nc, m, "gcn", a["L0_gnn_W"], a["L0_gnn_b"], residual=k == 2)

        for k in range(3):
            attention_scores(nc, m, k)
            segment_softmax(nc, m)
            edge_pass(nc, m, "values", scaled=True)
            node_pass(nc, m, "gat", None, None, residual=k == 2)

        relation_pass(nc, m, a["L2_gnn_W1"])
        node_pass(nc, m, "rel", a["L2_gnn_root1"], a["L2_gnn_b1"], residual=False)
        relation_pass(nc, m, a["L2_gnn_W2"])
        node_pass(nc, m, "rel", a["L2_gnn_root2"], a["L2_gnn_b2"], residual=True)

        for k in range(a["L3_gnn_W1"].shape[0]):
            edge_pass(nc, m, "gather", normed=k > 0)
            gin_first(nc, m, k)
            batch_norm(nc, m, a["L3_gnn_g1"], a["L3_gnn_be1"], None, k)
            gin_second(nc, m, k)
            batch_norm(nc, m, a["L3_gnn_g2"], a["L3_gnn_be2"], a["L3_gnn_b2"], k)
        finish(nc, m)


def constants(nc, m):
    with semaphores(nc, "const", "z made zrows zinit") as s, nc.Block() as block:
        @block.gpsimd
        def _(pool):
            nc.gpsimd.memset(m.ident[:], 0.0).then_inc(s["z"], 1)
            nc.gpsimd.memset(m.ones[:], 1.0)
            nc.gpsimd.memset(m.zero_k[:], 0.0)
            nc.gpsimd.memset(m.zeros[:], 0.0).then_inc(s["zinit"], 1)
            nc.gpsimd.memset(m.sums[:], 0.0)
            nc.gpsimd.iota(m.iota[:], pattern=[[1, P]], base=0, channel_multiplier=0,
                           allow_small_or_imprecise_dtypes=True)
            nc.gpsimd.memset(m.upper[:], 1.0).then_inc(s["z"], 1)
            pool.wait_ge(s["z"], 2)
            nc.gpsimd.affine_select(out=m.ident[:], in_=m.ident[:], compare_op=ALU.not_equal, fill=1.0,
                                    base=0, pattern=[[-1, P]], channel_multiplier=1).then_inc(s["made"], 1)
            nc.gpsimd.affine_select(out=m.upper[:], in_=m.upper[:], compare_op=ALU.is_gt, fill=0.0,
                                    base=0, pattern=[[1, P]], channel_multiplier=-1).then_inc(s["made"], 1)
            pool.wait_ge(s["made"], 2)

        @block.sync
        def _(sp):
            sp.wait_ge(s["zinit"], 1)
            sp.dma_start(m.HC[SCOLS:SCOLS + P, :], m.zeros[:, :P]).then_inc(s["zrows"], 16)
            sp.dma_start(m.HAS.rearrange("(p c) o -> p (c o)", p=HP), m.zeros[:HP, :]).then_inc(s["zrows"], 16)
            sp.wait_ge(s["zrows"], 32)


def load_tiled(sp, dst_a, dst_b, vec, sem):
    sp.dma_start(dst_a, vec[0:ROWS_A * P].rearrange("(t e) -> t e", e=P)).then_inc(sem, 16)
    sp.dma_start(dst_b[0:FULL - ROWS_A, :], vec[ROWS_A * P:FULL * P].rearrange("(t e) -> t e", e=P)).then_inc(sem, 16)
    sp.dma_start(dst_b[FULL - ROWS_A:FULL - ROWS_A + 1, 0:REST],
                 vec[FULL * P:E].rearrange("(t e) -> t e", t=1)).then_inc(sem, 16)


def edge_lists(nc, m):
    A, B = slice(0, ROWS_A), slice(0, ROWS_B)
    blocks = ((0, ROWS_A), (1, ROWS_B))
    di = [m.small_i[:, 0:P], m.small_i[:, P:2 * P]]
    si = [m.small_i[:, 2 * P:3 * P], m.small_i[:, 3 * P:4 * P]]
    pi = [m.src_old[:, 0:P], m.rank[:, 0:P]]
    dst, prev, new, scan, rnk, loc, srcf, hidx, ok, tmp = (
        [m.big[k][:, 0:P], m.big[k][:, P:2 * P]] for k in range(10))
    base, cols = m.sm[0], m.sm[1]
    with semaphores(nc, "prep", "fill ld d pe pp st") as s, nc.Block() as block:
        @block.sync
        def _(sp):
            sp.wait_ge(s["fill"], 1)
            load_tiled(sp, di[0], di[1], m.a["dst"], s["ld"])
            load_tiled(sp, si[0], si[1], m.a["src"], s["ld"])
            v = m.a["dst"]
            sp.dma_start(pi[0][0:1, 1:P], v[0:P - 1].rearrange("(t e) -> t e", t=1)).then_inc(s["ld"], 16)
            sp.dma_start(pi[0][1:P, :], v[P - 1:P * ROWS_A - 1].rearrange("(t e) -> t e", e=P)).then_inc(s["ld"], 16)
            sp.dma_start(pi[1][0:FULL - ROWS_A, :], v[P * ROWS_A - 1:P * FULL - 1].rearrange("(t e) -> t e", e=P)).then_inc(s["ld"], 16)
            sp.dma_start(pi[1][FULL - ROWS_A:FULL - ROWS_A + 1, 0:REST + 1],
                         v[P * FULL - 1:E].rearrange("(t e) -> t e", t=1)).then_inc(s["ld"], 16)
            sp.wait_ge(s["st"], 1)
            sp.dma_start(m.NEW[0:ROWS_A * P].rearrange("(t e) -> t e", e=P), new[0]).then_inc(s["pp"], 16)
            sp.dma_start(m.NEW[ROWS_A * P:EPAD].rearrange("(t e) -> t e", e=P), new[1][B, :]).then_inc(s["pp"], 16)
            sp.dma_start(m.NEW[EPAD:EPAD + P].rearrange("(t e) -> t e", t=1), m.ones[0:1, :]).then_inc(s["pp"], 16)
            sp.wait_ge(s["pp"], 48)

        @block.vector
        def _(v):
            n = [0]

            def link(ins):
                n[0] += 1
                ins.then_inc(s["d"], 1)
                v.wait_ge(s["d"], n[0])

            link(nc.vector.memset(m.small_i[:, 0:2 * P], -1))
            link(nc.vector.memset(m.small_i[:, 2 * P:4 * P], 0))
            link(nc.vector.memset(pi[0], -5))
            link(nc.vector.memset(pi[1], -1))
            nc.vector.memset(cols[:], 0.0).then_inc(s["fill"], 1)
            v.wait_ge(s["ld"], 10 * 16)
            v.wait_ge(s["fill"], 1)
            for b, r in blocks:
                q = slice(0, r)
                link(nc.vector.tensor_copy(dst[b][q], di[b][q]))
                link(nc.vector.tensor_copy(prev[b][q], pi[b][q]))
                link(nc.vector.tensor_copy(srcf[b][q], si[b][q]))
                link(nc.vector.tensor_tensor(new[b][q], dst[b][q], prev[b][q], ALU.not_equal))
                link(nc.vector.tensor_tensor_scan(scan[b][q], new[b][q], m.zeros[q, 0:P], 0.0, ALU.add, ALU.add))
                link(nc.vector.tensor_copy(cols[q, b:b + 1], scan[b][q, P - 1:P]))
                link(nc.vector.tensor_scalar(ok[b][q], dst[b][q], 0.0, None, ALU.is_ge))
            nc.vector.tensor_copy(cols[:, 2:3], cols[:, 0:1]).then_inc(s["st"], 1)
            v.wait_ge(s["pe"], 1)
            link(nc.vector.tensor_scalar(base[:, 0:2], m.ps[0][:, 0:2], -1.0, None, ALU.add))
            for b, r in blocks:
                q = slice(0, r)
                link(nc.vector.tensor_scalar(rnk[b][q], scan[b][q], base[q, b:b + 1], None, ALU.add))
                link(nc.vector.tensor_scalar(loc[b][q], rnk[b][q], rnk[b][q, 0:1], 1.0, ALU.subtract, ALU.add))
                link(nc.vector.tensor_tensor(loc[b][q], loc[b][q], ok[b][q], ALU.mult))
                link(nc.vector.tensor_scalar(loc[b][q], loc[b][q], -1.0, None, ALU.add))
                link(nc.vector.tensor_tensor(tmp[b][q], new[b][q], ok[b][q], ALU.mult))
                link(nc.vector.scalar_tensor_tensor(out=hidx[b][q], in0=dst[b][q], scalar=-SKIP, in1=tmp[b][q],
                                                    op0=ALU.add, op1=ALU.mult))
                link(nc.vector.tensor_scalar(hidx[b][q], hidx[b][q], SKIP, None, ALU.add))
            nc.vector.tensor_copy(cols[:, 3:4], cols[:, 0:1]).then_inc(s["st"], 1)
            v.wait_ge(s["pe"], 2)
            link(nc.vector.tensor_copy(m.rank[:], m.ps[1][:, 0:TILES]))
            link(nc.vector.tensor_copy(cols[0:1, 0:TILES], m.ps[1][0:1, 0:TILES]))
            f4 = cols[0:1, 0:TILES].rearrange("o (g j) -> o g j", j=J)
            d3 = base[0:1, 0:3 * GROUPS].rearrange("o (g j) -> o g j", j=3)
            link(nc.vector.tensor_copy(m.first[:].unsqueeze(2), f4[:, :, 0:1]))
            link(nc.vector.tensor_tensor(d3, f4[:, :, 1:4], f4[:, :, 0:3], ALU.subtract))
            for c in (2, 1):
                link(nc.vector.scalar_tensor_tensor(out=d3[:, :, c - 1:c], in0=d3[:, :, c:c + 1], scalar=float(STEP),
                                                    in1=d3[:, :, c - 1:c], op0=ALU.mult, op1=ALU.add))
            link(nc.vector.tensor_copy(m.steps[:].unsqueeze(2), d3[:, :, 0:1]))
            link(nc.vector.tensor_copy(m.local[:], m.ps[2][:, 0:TILES]))
            link(nc.vector.tensor_copy(m.src_old[:], m.ps[3][:, 0:TILES]))
            link(nc.vector.tensor_copy(m.has_idx[:], m.ps[4][:, 0:TILES]))

        @block.tensor
        def _(pe):
            pe.wait_ge(s["st"], 1)
            nc.tensor.matmul(m.ps[0][:, 0:1], m.upper[:], cols[:, 0:1], start=True, stop=True)
            nc.tensor.matmul(m.ps[0][:, 1:2], m.ones[:], cols[:, 0:1], start=True, stop=False)
            nc.tensor.matmul(m.ps[0][:, 1:2], m.upper[:], cols[:, 1:2], start=False, stop=True).then_inc(s["pe"], 1)
            pe.wait_ge(s["st"], 2)
            for k, x in enumerate((rnk, loc, srcf, hidx)):
                nc.tensor.transpose(m.ps[1 + k][:, 0:ROWS_A], x[0][A], m.ident[:])
                last = nc.tensor.transpose(m.ps[1 + k][:, ROWS_A:TILES], x[1][B], m.ident[0:ROWS_B, 0:ROWS_B])
            last.then_inc(s["pe"], 1)


def indexed_loop(nc, s, cols, stages, each, free):
    pool = nc.gpsimd

    def body(i, last):
        for u in range(2):
            free(i, u)
            stage = stages[u][:, 0:J]
            nc.gpsimd.tensor_copy(stage, cols[:, bass.ds((2 * i + u) * J, J)]).then_inc(s["idx_ready"], 1)
            pool.wait_ge(s["idx_ready"], 1)
            pool.sem_clear(s["idx_ready"])
            each(i, u, stage)
    over_groups(pool, body)


def mark_receivers(nc, m):
    with semaphores(nc, "has", "idx_ready sc0 sc1 d") as s, nc.Block() as block:
        sc = [s["sc0"], s["sc1"]]

        @block.gpsimd
        def _(pool):
            def free(i, u):
                after(pool, sc[u], i * 16 * J)

            def each(i, u, stage):
                for j in range(J):
                    pool.indirect_dma_start(
                        out=m.HAS, out_offset=bass.IndirectOffsetOnAxis(ap=stage[:, j:j + 1], axis=0),
                        in_=m.ones[:, 0:1], in_offset=None, bounds_check=N - 1, oob_is_err=False).then_inc(sc[u], 16)
            indexed_loop(nc, s, m.has_idx, m.stage_idx, each, free)
            for u in range(2):
                pool.wait_ge(sc[u], GROUPS // 2 * 16 * J)


def renumber(nc, m):
    has, inc, num, t = (m.big[k][0:HP, 0:HC] for k in range(4))
    permi = m.small_i[0:HP, 0:HC]
    with semaphores(nc, "perm", "ld d tot pe io out back") as s, nc.Block() as block:
        @block.sync
        def _(sp):
            sp.dma_start(has, m.HAS.rearrange("(p c) o -> p (c o)", p=HP)).then_inc(s["ld"], 16)
            sp.wait_ge(s["out"], 1)
            sp.dma_start(m.PERM.rearrange("(p c) o -> p (c o)", p=HP), permi).then_inc(s["back"], 16)
            sp.wait_ge(s["back"], 16)
            full = (NWIN - 1) * WIN
            sp.dma_start(m.perm[:, 0:(NWIN - 1) * J].rearrange("p (w j) -> p w j", j=J),
                         m.PERM[0:full, :].rearrange("(w p j) o -> p w (j o)", p=P, j=J)).then_inc(s["back"], 16)
            sp.dma_start(m.perm[0:TAIL_P, (NWIN - 1) * J:NWIN * J],
                         m.PERM[full:N, :].rearrange("(p j) o -> p (j o)", j=J)).then_inc(s["back"], 16)
            sp.wait_ge(s["back"], 48)

        @block.gpsimd
        def _(pool):
            nc.gpsimd.iota(num, pattern=[[1, HC]], base=0, channel_multiplier=HC,
                           allow_small_or_imprecise_dtypes=True).then_inc(s["io"], 1)

        @block.vector
        def _(v):
            n = [0]

            def link(ins):
                n[0] += 1
                ins.then_inc(s["d"], 1)
                v.wait_ge(s["d"], n[0])
            v.wait_ge(s["ld"], 16)
            link(nc.vector.tensor_tensor_scan(inc, has, m.zeros[0:HP, 0:HC], 0.0, ALU.add, ALU.add))
            nc.vector.tensor_copy(m.sm[0][0:HP, 0:1], inc[:, HC - 1:HC]).then_inc(s["tot"], 1)
            v.wait_ge(s["pe"], 1)
            link(nc.vector.tensor_copy(m.sm[1][0:HP, 0:2], m.ps[0][0:HP, 0:2]))
            link(nc.vector.tensor_scalar(inc, inc, m.sm[1][0:HP, 0:1], None, ALU.add))
            v.wait_ge(s["io"], 1)
            link(nc.vector.scalar_tensor_tensor(out=t, in0=num, scalar=m.sm[1][0:HP, 1:2], in1=inc,
                                                op0=ALU.add, op1=ALU.subtract))
            link(nc.vector.scalar_tensor_tensor(out=inc, in0=inc, scalar=-1.0, in1=t, op0=ALU.add, op1=ALU.subtract))
            link(nc.vector.tensor_tensor(inc, inc, has, ALU.mult))
            nc.vector.tensor_tensor(permi, inc, t, ALU.add).then_inc(s["out"], 1)

        @block.tensor
        def _(pe):
            pe.wait_ge(s["tot"], 1)
            nc.tensor.matmul(m.ps[0][:, 0:1], m.upper[0:HP, :], m.sm[0][0:HP, 0:1], start=True, stop=True)
            nc.tensor.matmul(m.ps[0][:, 1:2], m.ones[0:HP, :], m.sm[0][0:HP, 0:1], start=True, stop=True).then_inc(s["pe"], 1)


def renumber_senders(nc, m):
    got_i = [m.small_i[:, u * J:(u + 1) * J] for u in range(2)]
    with semaphores(nc, "src", "idx_ready g0 g1 used d") as s, nc.Block() as block:
        g = [s["g0"], s["g1"]]

        @block.gpsimd
        def _(pool):
            def free(i, u):
                after(pool, s["used"], 2 * i + u - 1)

            def each(i, u, stage):
                for j in range(J):
                    pool.indirect_dma_start(
                        out=got_i[u][:, j:j + 1], out_offset=None, in_=m.PERM,
                        in_offset=bass.IndirectOffsetOnAxis(ap=stage[:, j:j + 1], axis=0)).then_inc(g[u], 16)
            indexed_loop(nc, s, m.src_old, m.stage_idx, each, free)

        @block.vector
        def _(v):
            def body(i, last):
                for u in range(2):
                    v.wait_ge(g[u], 16 * J * (i + 1))
                    nc.vector.tensor_copy(m.src[:, bass.ds((2 * i + u) * J, J)], got_i[u]).then_inc(s["used"], 1)
            over_groups(v, body)
            v.wait_ge(s["used"], GROUPS)
            nc.vector.tensor_scalar(m.src_c[:], m.src[:], float(SCOLS), None, ALU.min).then_inc(s["d"], 1)
            v.wait_ge(s["d"], 1)


def relation_weights(nc, m):
    ew = [m.big[0][:, 0:P], m.big[0][:, P:2 * P]]
    ti = [m.small_i[:, 0:P], m.small_i[:, P:2 * P]]
    tf = [m.big[1][:, 0:P], m.big[1][:, P:2 * P]]
    lin = m.big[2][0:100, 0:250]
    c = m.sm[0]
    with semaphores(nc, "types", "fill ld d a pe b") as s, nc.Block() as block:
        @block.sync
        def _(sp):
            sp.wait_ge(s["fill"], 1)
            load_tiled(sp, ew[0], ew[1], m.a["edge_weight"], s["ld"])
            load_tiled(sp, ti[0], ti[1], m.a["edge_type_4"], s["ld"])
            sp.dma_start(lin, m.a["edge_weight"].rearrange("(p c) -> p c", p=100)).then_inc(s["ld"], 16)

        @block.vector
        def _(v):
            n = [0]

            def link(ins):
                n[0] += 1
                ins.then_inc(s["d"], 1)
                v.wait_ge(s["d"], n[0])
            link(nc.vector.memset(m.big[0][:, 0:2 * P], 0.0))
            nc.vector.memset(m.small_i[:, 0:2 * P], 0).then_inc(s["fill"], 1)
            v.wait_ge(s["ld"], 7 * 16)
            link(nc.vector.tensor_copy(m.big[1][:, 0:2 * P], m.small_i[:, 0:2 * P]))
            link(nc.vector.tensor_reduce(c[0:100, 0:1], lin, AX.X, ALU.max))
            link(nc.vector.tensor_reduce(c[0:100, 1:2], lin, AX.X, ALU.min))
            nc.vector.tensor_copy(c[0:100, 2:4], c[0:100, 0:2]).then_inc(s["a"], 1)
            v.wait_ge(s["pe"], 1)
            link(nc.vector.tensor_copy(m.sm[3][:, 0:TILES], m.ps[1][:, 0:TILES]))
            link(nc.vector.tensor_copy(m.sm[4][:, 0:TILES], m.ps[2][:, 0:TILES]))
            link(nc.vector.tensor_reduce(m.sm[1][0:1, 0:1], m.ps[0][0:1, 0:100], AX.X, ALU.max))
            link(nc.vector.tensor_reduce(m.sm[1][0:1, 1:2], m.ps[3][0:1, 0:100], AX.X, ALU.min))
            link(nc.vector.tensor_tensor(m.sm[1][0:1, 2:3], m.sm[1][0:1, 0:1], m.sm[1][0:1, 1:2], ALU.subtract))
            link(nc.vector.tensor_scalar(m.sm[1][0:1, 2:3], m.sm[1][0:1, 2:3], 1e-8, None, ALU.add))
            nc.vector.reciprocal(m.sm[1][0:1, 2:3], m.sm[1][0:1, 2:3]).then_inc(s["b"], 1)
            v.wait_ge(s["pe"], 2)
            link(nc.vector.tensor_copy(m.sm[2][:, 0:2], m.ps[4][:, 0:2]))
            link(nc.vector.tensor_scalar(m.sm[3][:, 0:TILES], m.sm[3][:, 0:TILES], m.sm[2][:, 0:1], m.sm[2][:, 1:2],
                                         ALU.subtract, ALU.mult))
            for r in range(J):
                link(nc.vector.scalar_tensor_tensor(out=m.tw[:, :, r], in0=m.sm[4][:, 0:TILES], scalar=float(r),
                                                    in1=m.sm[3][:, 0:TILES], op0=ALU.is_equal, op1=ALU.mult))

        @block.tensor
        def _(pe):
            pe.wait_ge(s["a"], 1)
            for k, x in ((1, ew), (2, tf)):
                nc.tensor.transpose(m.ps[k][:, 0:ROWS_A], x[0], m.ident[:])
                nc.tensor.transpose(m.ps[k][:, ROWS_A:TILES], x[1][0:ROWS_B], m.ident[0:ROWS_B, 0:ROWS_B])
            nc.tensor.transpose(m.ps[0][0:1, 0:100], c[0:100, 2:3], m.ident[0:100, 0:100])
            nc.tensor.transpose(m.ps[3][0:1, 0:100], c[0:100, 3:4], m.ident[0:100, 0:100]).then_inc(s["pe"], 1)
            pe.wait_ge(s["b"], 1)
            nc.tensor.matmul(m.ps[4][:, 0:2], m.ones[0:1, :], m.sm[1][0:1, 1:3], start=True, stop=True).then_inc(s["pe"], 1)


def degrees(nc, m):
    edge_pass(nc, m, "ones")
    deg = m.dis
    with semaphores(nc, "deg", "io z a d") as s, nc.Block() as block:
        @block.sync
        def _(sp):
            sp.dma_start(m.DEG.rearrange("(o n) -> o n", o=1), m.sums[0:1, :]).then_inc(s["io"], 16)
            sp.wait_ge(s["io"], 16)
            sp.wait_ge(s["z"], 1)
            sp.dma_start(deg[:, 0:SWIN * J].rearrange("p (w j) -> p w j", j=J),
                         m.DEG.rearrange("(w p j) -> p w j", p=P, j=J)).then_inc(s["io"], 16)

        @block.vector
        def _(v):
            nc.vector.memset(deg[:], 0.0).then_inc(s["z"], 1)
            v.wait_ge(s["io"], 32)
            nc.vector.memset(m.sums[:], 0.0)
            nc.vector.tensor_scalar(deg[:], deg[:], 1.0, None, ALU.add).then_inc(s["d"], 1)
            v.wait_ge(s["a"], 1)
            nc.vector.reciprocal(m.dis[:], deg[:]).then_inc(s["d"], 1)

        @block.scalar
        def _(act):
            act.wait_ge(s["d"], 1)
            nc.scalar.activation(deg[:], deg[:], ACT.Sqrt).then_inc(s["a"], 1)


def permute_input(nc, m):
    with semaphores(nc, "permx", "ld0 ld1 ld2 ld3 sc0 sc1 sc2 sc3 idx_ready") as s, nc.Block() as block:
        ld, sc = ([s[f"{n}{u}"] for u in range(U)] for n in ("ld", "sc"))

        @block.sync
        def _(sp):
            def body(i, summed, last):
                for u in slots(last):
                    p = parts(last, u)
                    after(sp, sc[u], i * 16 * J)
                    sp.dma_start(m.big[u][:p, :], rows(m.a["x"], U * i + u, p)).then_inc(ld[u], 16)
            over_windows(sp, body)

        @block.gpsimd
        def _(pool):
            def body(i, summed, last):
                for u in slots(last):
                    p = parts(last, u)
                    pool.wait_ge(ld[u], 16 * (i + 1))
                    nc.gpsimd.tensor_copy(m.stage_idx[u][:p, 0:J], m.perm[:p, bass.ds((U * i + u) * J, J)]).then_inc(s["idx_ready"], 1)
                    pool.wait_ge(s["idx_ready"], 1)
                    pool.sem_clear(s["idx_ready"])
                    for j in range(J):
                        pool.indirect_dma_start(
                            out=m.X, out_offset=bass.IndirectOffsetOnAxis(ap=m.stage_idx[u][:p, j:j + 1], axis=0),
                            in_=m.big[u][:p, j * P:(j + 1) * P], in_offset=None).then_inc(sc[u], 16)
            over_windows(pool, body)
            for u in range(U):
                pool.wait_ge(sc[u], rounds(u) * 16 * J)


def tile_columns(pe, m, banks, g):
    packed = pe.value_load(m.steps[0:1, bass.ds(g, 1)], min_val=0, max_val=P * (1 + STEP + STEP * STEP))
    first = [0]
    for j in range(1, J):
        step = (packed >> (8 * (j - 1))) & (STEP - 1) if j < J - 1 else packed >> (8 * (j - 1))
        first.append(pe.snap((first[-1] + step).with_bounds(min_val=0, max_val=j * P)))
    return [[bank[:, bass.ds(x, P)] for x in first] for bank in banks]


def clear_bank(nc, m, bank):
    nc.tensor.matmul(bank[:], m.zero_k[:, 0:P], m.zero_k[:], start=True, stop=False, skip_group_check=True)


def group_columns(v, m, g):
    first = v.value_load(m.first[0:1, bass.ds(g, 1)], min_val=0, max_val=EPAD - WIN)
    return m.sums[:, bass.ds(first, WIN)]


def add_sums(nc, v, s, g, cols, bank):
    after(v, s["added"], g)
    nc.vector.tensor_tensor(cols, cols, bank[:], ALU.add).then_inc(s["added"], 1)


def edge_pass(nc, m, source, scaled=False, normed=False):
    got_t = m.big[0:2]
    tr = m.big[2:4]
    hot = m.big[4:6]
    with semaphores(nc, "edge", "idx_ready g0 g1 g2 g3 g4 g5 g6 g7 hot hot2 mul tr relu mm added") as s, nc.Block() as block:
        got = [s["g0"], s["g1"], s["g2"], s["g3"], s["g4"], s["g5"], s["g6"], s["g7"]]
        if source == "gather":
            @block.gpsimd
            def _(pool):
                def free(i, u):
                    after(pool, s["mul"] if normed else s["mm"], 2 * i + u - 1)

                def each(i, u, stage):
                    for j in range(J):
                        pool.indirect_dma_start(
                            out=got_t[u][:, j * P:(j + 1) * P], out_offset=None, in_=m.H,
                            in_offset=bass.IndirectOffsetOnAxis(ap=stage[:, j:j + 1], axis=0)).then_inc(got[J * u + j], 16)
                indexed_loop(nc, s, m.src, m.stage_idx, each, free)
        if source == "values":
            @block.sync
            def _(sp):
                def body(i, last):
                    for u in range(2):
                        g = 2 * i + u
                        after(sp, s["mm"], g - 1)
                        sp.dma_start(jview(got_t[u]), m.V[bass.ds(g * WIN, WIN), :].rearrange("(j p) f -> p j f", p=P)).then_inc(got[u], 16)
                over_groups(sp, body)

        @block.vector
        def _(v):
            def add(g, u):
                cols = group_columns(v, m, g)
                v.wait_ge(s["mm"], g + 1)
                add_sums(nc, v, s, g, cols, m.ps[u])

            def body(i, last):
                for u in range(2):
                    g = 2 * i + u
                    after(v, s["mm"], g - 1)
                    nc.vector.tensor_tensor(
                        jview(hot[u]), bc(m.iota[:, :].unsqueeze(1), [P, J, P]),
                        bc(m.local[:, bass.ds(g * J, J)].unsqueeze(2), [P, J, P]), ALU.is_equal).then_inc(s["hot"], 1)
                    if scaled:
                        v.wait_ge(s["hot"], g + 1)
                        nc.vector.tensor_tensor(
                            jview(hot[u]), jview(hot[u]),
                            bc(m.alpha[:, bass.ds(g * J, J)].unsqueeze(2), [P, J, P]), ALU.mult).then_inc(s["hot2"], 1)
                    if not (isinstance(i, int) and i + u == 0):
                        add(g - 1, 1 - u)
                    if normed:
                        for j in range(J):
                            v.wait_ge(got[J * u + j], 16 * (i + 1))
                        nc.vector.tensor_tensor(jview(tr[u]), jview(got_t[u]), bc(m.scale_row[:, :].unsqueeze(1), [P, J, P]),
                                                ALU.mult).then_inc(s["mul"], 1)
                        v.wait_ge(s["mul"], g + 1)
                        nc.vector.tensor_tensor(jview(tr[u]), jview(tr[u]), bc(m.shift_row[:, :].unsqueeze(1), [P, J, P]),
                                                ALU.add).then_inc(s["tr"], 1)
            over_groups(v, body)
            add(GROUPS - 1, 1)
            v.wait_ge(s["added"], GROUPS)

        if normed:
            @block.scalar
            def _(act):
                def body(i, last):
                    for u in range(2):
                        act.wait_ge(s["tr"], 2 * i + u + 1)
                        nc.scalar.activation(tr[u][:], tr[u][:], ACT.Relu).then_inc(s["relu"], 1)
                over_groups(act, body)

        @block.tensor
        def _(pe):
            def body(i, last):
                for u in range(2):
                    g = 2 * i + u
                    pe.wait_ge(s["hot2"] if scaled else s["hot"], g + 1)
                    if normed:
                        pe.wait_ge(s["relu"], g + 1)
                    elif source == "values":
                        pe.wait_ge(got[u], 16 * (i + 1))
                    at = tile_columns(pe, m, [m.ps[u]], g)[0]
                    after(pe, s["added"], g - 1)
                    clear_bank(nc, m, m.ps[u])
                    for j in range(J):
                        if source == "gather" and not normed:
                            pe.wait_ge(got[J * u + j], 16 * (i + 1))
                        lhs = m.ones[:] if source == "ones" else (tr if normed else got_t)[u][:, j * P:(j + 1) * P]
                        last_mm = nc.tensor.matmul(at[j], lhs, hot[u][:, j * P:(j + 1) * P],
                                                   start=False, stop=(j == J - 1), skip_group_check=True)
                    last_mm.then_inc(s["mm"], 1)
            over_groups(pe, body)


def relation_pass(nc, m, weights):
    got_t, hot = m.big[0:2], m.big[2:4]
    by_type = [m.big[4 + J * u:4 + J * (u + 1)] for u in range(2)]
    hot_w = [m.big[12 + J * u:12 + J * (u + 1)] for u in range(2)]
    w4 = m.wide
    with semaphores(nc, "rel", "idx_ready g0 g1 g2 g3 g4 g5 g6 g7 hot w hw ag cp mm added") as s, nc.Block() as block:
        got = [s[f"g{k}"] for k in range(2 * J)]

        @block.sync
        def _(sp):
            sp.dma_start(w4[:].rearrange("p (r f) -> p r f", r=J), weights.rearrange("r i o -> i r o")).then_inc(s["w"], 16)

        @block.gpsimd
        def _(pool):
            def free(i, u):
                after(pool, s["ag"], (2 * i + u - 1) * J)

            def each(i, u, stage):
                for j in range(J):
                    pool.indirect_dma_start(
                        out=got_t[u][:, j * P:(j + 1) * P], out_offset=None, in_=m.H,
                        in_offset=bass.IndirectOffsetOnAxis(ap=stage[:, j:j + 1], axis=0)).then_inc(got[J * u + j], 16)
            indexed_loop(nc, s, m.src, m.stage_idx, each, free)

        @block.vector
        def _(v):
            def add(g, u):
                cols = group_columns(v, m, g)
                v.wait_ge(s["mm"], g + 1)
                add_sums(nc, v, s, g, cols, m.ps[J + u])

            def body(i, last):
                for u in range(2):
                    g = 2 * i + u
                    after(v, s["hw"], (g - 1) * J)
                    nc.vector.tensor_tensor(
                        jview(hot[u]), bc(m.iota[:, :].unsqueeze(1), [P, J, P]),
                        bc(m.local[:, bass.ds(g * J, J)].unsqueeze(2), [P, J, P]), ALU.is_equal).then_inc(s["hot"], 1)
                    v.wait_ge(s["hot"], g + 1)
                    after(v, s["ag"], (g - 1) * J)
                    for r in range(J):
                        nc.vector.tensor_tensor(
                            jview(hot_w[u][r]), jview(hot[u]),
                            bc(m.tw[:, bass.ds(g * J, J), r:r + 1], [P, J, P]), ALU.mult).then_inc(s["hw"], 1)
                    if not (isinstance(i, int) and i + u == 0):
                        add(g - 1, 1 - u)
            over_groups(v, body)
            add(GROUPS - 1, 1)
            v.wait_ge(s["added"], GROUPS)

        @block.scalar
        def _(act):
            def body(i, last):
                for u in range(2):
                    g = 2 * i + u
                    after(act, s["mm"], g - 1)
                    for r in range(J):
                        act.wait_ge(s["ag"], g * J + r + 1)
                        nc.scalar.activation(by_type[u][r][:], m.ps[r][:], ACT.Copy).then_inc(s["cp"], 1)
            over_groups(act, body)

        @block.tensor
        def _(pe):
            pe.wait_ge(s["w"], 16)

            def body(i, last):
                for u in range(2):
                    g = 2 * i + u
                    out = m.ps[J + u]
                    at = tile_columns(pe, m, m.ps[0:J], g)

                    def through(r):
                        pe.wait_ge(s["cp"], g * J + r + 1)
                        return nc.tensor.matmul(out[:], w4[:, r * P:(r + 1) * P], by_type[u][r][:], start=(r == 0), stop=(r == J - 1))
                    for j in range(J):
                        pe.wait_ge(got[J * u + j], 16 * (i + 1))
                    for r in range(J):
                        after(pe, s["cp"], (g - 1) * J + r + 1)
                        clear_bank(nc, m, m.ps[r])
                        pe.wait_ge(s["hw"], g * J + r + 1)
                        for j in range(J):
                            ag = nc.tensor.matmul(at[r][j], got_t[u][:, j * P:(j + 1) * P], hot_w[u][r][:, j * P:(j + 1) * P],
                                                  start=False, stop=(j == J - 1), skip_group_check=True)
                        ag.then_inc(s["ag"], 1)
                        if r == 0:
                            after(pe, s["added"], g - 1)
                        else:
                            through(r - 1)
                    through(J - 1).then_inc(s["mm"], 1)
            over_groups(pe, body)


def node_pass(nc, m, kind, weight, bias, residual, scaled=False):
    table = kind in ("gcn", "rel")
    hin, hs, cw, t1, xt, ho = (m.big[k * U:(k + 1) * U] for k in range(6))
    st, rs, nb, ve = (m.sm[0:2], *([m.sm[k][:, 0:8], m.sm[k][:, 8:16]] for k in (2, 3, 4)))
    flag = m.sm[4][:, 32:32 + U]
    w_sb = m.w_sb[:]
    windows = NWIN if (table or residual) else SWIN
    dest = m.HC if (kind == "gat" and not residual) else m.H
    names = "w wb ldh0 ldh1 ldh2 ldh3 ldx0 ldx1 ldx2 ldx3 tp hs cw py yd t1 t2 t3 xs bs ba ve sq rc ds nb ho sth0 sth1 sth2 sth3 stx0 stx1 stx2 stx3"
    with semaphores(nc, "node", names) as s, nc.Block() as block:
        ldh, ldx, sth, stx = ([s[f"{n}{u}"] for u in range(U)] for n in ("ldh", "ldx", "sth", "stx"))

        @block.sync
        def _(sp):
            if weight is not None:
                sp.dma_start(w_sb, weight).then_inc(s["w"], 16)
                sp.dma_start(m.bias_row[:], bc(bias.unsqueeze(0), [P, P])).then_inc(s["wb"], 16)

            def body(i, summed, last):
                stored = 16 * (i + 1) - 16
                for u in slots(last):
                    w, p = U * i + u, parts(last, u)
                    if table:
                        after(sp, s["tp"], w - U + 1)
                        sp.dma_start(hin[u][:p], rows(m.H, w, p)).then_inc(ldh[u], 16)
                    if residual:
                        after(sp, s["ho"], w - U + 1)
                        if kind != "ln0":
                            after(sp, stx[u], stored)
                        sp.dma_start(xt[u][:p], rows(m.X, w, p)).then_inc(ldx[u], 16)
            if table or residual:
                over_windows(sp, body, windows)

        if kind != "ln0":
            @block.gpsimd
            def _(pool):
                clear_sums(nc, pool, m, s["hs"] if kind == "gcn" else s["cw"])

        @block.tensor
        def _(pe):
            if weight is not None:
                pe.wait_ge(s["w"], 16)

            def body(i, summed, last):
                if table:
                    for u in slots(last):
                        w, p = U * i + u, parts(last, u)
                        pe.wait_ge(ldh[u], 16 * (i + 1))
                        after(pe, s["hs"], w - U + 1)
                        for j in range(J):
                            tp = nc.tensor.transpose(m.ps[u][:, j * p:(j + 1) * p], hin[u][:p, j * P:(j + 1) * P], m.ident[:p, :p])
                        tp.then_inc(s["tp"], 1)
                for u in slots(last):
                    w, p = U * i + u, parts(last, u)
                    if kind == "gat" and not summed:
                        continue
                    if table:
                        pe.wait_ge(s["hs"], w + 1)
                    if kind in ("rel", "gat") and summed:
                        pe.wait_ge(s["cw"], w + 1)
                    after(pe, s["yd"], w - U + 1)
                    for j in range(J):
                        o = m.ps[U + u][:p, j * P:(j + 1) * P]
                        if kind == "gat":
                            mm = nc.tensor.transpose(o, cw[u][:, j * P:(j + 1) * P], m.ident[:])
                            continue
                        both = kind == "rel" and summed
                        mm = nc.tensor.matmul(o, hs[u][:, j * p:(j + 1) * p], w_sb, start=True, stop=not both)
                        if both:
                            mm = nc.tensor.matmul(o, cw[u][:, j * P:(j + 1) * P], m.ident[:], start=False, stop=True)
                    mm.then_inc(s["py"], 1)
            if kind != "ln0":
                over_windows(pe, body, windows)

        @block.vector
        def _(v):
            if weight is not None:
                v.wait_ge(s["wb"], 16)

            def body(i, summed, last):
                for u in slots(last):
                    w, p = U * i + u, parts(last, u)
                    sums = m.sums[:, bass.ds(w * WIN, WIN)].rearrange("f (p j) -> f j p", j=J) if summed else None
                    if table:
                        v.wait_ge(s["tp"], w + 1)
                        after(v, s["py"], w - U + 1)
                        bank = m.ps[u][:, 0:J * p]
                        if kind == "gcn" and summed:
                            nc.vector.tensor_tensor(jview(hs[u]), jview(m.ps[u]), sums, ALU.add).then_inc(s["hs"], 1)
                        else:
                            nc.vector.tensor_copy(hs[u][:, 0:J * p], bank).then_inc(s["hs"], 1)
                    if kind in ("rel", "gat") and summed:
                        after(v, s["py"], w - U + 1)
                        nc.vector.tensor_scalar(jview(cw[u]), sums, 0.0 if kind == "gat" else -3.4e38, None, ALU.max).then_inc(s["cw"], 1)
                for h in range(1 if last else 2):
                    q = 2 * i + h
                    for u in (2 * h, 2 * h + 1):
                        w, p = U * i + u, parts(last, u)
                        dis = bc(m.dis[:p, bass.ds(w * J, J)].unsqueeze(2), [p, J, P])
                        bias_b = bc(m.bias_row[:p, :].unsqueeze(1), [p, J, P])
                        py, t, x = jview(m.ps[U + u], p), jview(t1[u], p), jview(xt[u], p)
                        has_y = kind != "ln0" and (kind != "gat" or summed and residual)
                        if has_y:
                            v.wait_ge(s["py"], w + 1)
                        if residual:
                            v.wait_ge(ldx[u], 16 * (i + 1))
                        if kind == "gcn":
                            nc.vector.tensor_tensor(t, py, dis, ALU.mult).then_inc(s["yd"], 1)
                            v.wait_ge(s["yd"], w + 1)
                            nc.vector.tensor_tensor(t, t, bias_b, ALU.add).then_inc(s["t1"], 1)
                            v.wait_ge(s["t1"], w + 1)
                            if residual:
                                nc.vector.scalar_tensor_tensor(out=xt[u][:p], in0=t1[u][:p], scalar=0.0, in1=xt[u][:p],
                                                               op0=ALU.max, op1=ALU.add).then_inc(s["xs"], 1)
                            else:
                                after(v, sth[u], 16 * i)
                                nc.vector.scalar_tensor_tensor(out=jview(ho[u], p), in0=t, scalar=0.0, in1=dis,
                                                               op0=ALU.max, op1=ALU.mult).then_inc(s["ho"], 1)
                        if kind == "rel":
                            after(v, s["ho"], w - U + 1)
                            nc.vector.tensor_tensor(t, py, bias_b, ALU.add).then_inc(s["yd"], 1)
                            if residual:
                                v.wait_ge(s["yd"], w + 1)
                                nc.vector.tensor_tensor(xt[u][:p], xt[u][:p], t1[u][:p], ALU.add).then_inc(s["xs"], 1)
                        if kind == "gat" and residual:
                            if summed:
                                nc.vector.tensor_tensor(x, x, py, ALU.add).then_inc(s["yd"], 1)
                                v.wait_ge(s["yd"], w + 1)
                            nc.vector.memset(flag[:, u:u + 1], 0.0).then_inc(s["xs"], 1)
                    if not residual:
                        continue
                    for u in (2 * h, 2 * h + 1):
                        w, p = U * i + u, parts(last, u)
                        if kind != "ln0":
                            v.wait_ge(s["xs"], w + 1)
                        after(v, s["nb"], q - 1)
                        for j in range(J):
                            bs = nc.vector.bn_stats(st[h][:p, 24 * (u - 2 * h) + 6 * j:24 * (u - 2 * h) + 6 * j + 6], xt[u][:p, j * P:(j + 1) * P])
                        bs.then_inc(s["bs"], 1)
                    v.wait_ge(s["bs"], 2 * q + 2)
                    halves = st[h][:, 0:48].rearrange("p (k c) -> p k c", c=6)
                    e, o, ee, oo = (halves[:, :, c:c + 1] for c in (1, 4, 2, 5))
                    mean2, diff, sq = (st[h][:, 64 + 8 * c:72 + 8 * c].unsqueeze(2) for c in range(3))
                    nc.vector.tensor_tensor(mean2, e, o, ALU.add)
                    nc.vector.tensor_tensor(diff, e, o, ALU.subtract)
                    nc.vector.tensor_tensor(sq, ee, oo, ALU.add).then_inc(s["ba"], 1)
                    v.wait_ge(s["ba"], 2 * q + 1)
                    nc.vector.tensor_tensor(diff, diff, diff, ALU.mult)
                    nc.vector.tensor_scalar(sq, sq, 1.0 / P, EPS, ALU.mult, ALU.add).then_inc(s["ba"], 1)
                    v.wait_ge(s["ba"], 2 * q + 2)
                    after(v, s["rc"], q - 1)
                    nc.vector.scalar_tensor_tensor(out=ve[h].unsqueeze(2), in0=diff, scalar=0.25, in1=sq, op0=ALU.mult, op1=ALU.add).then_inc(s["ve"], 1)
                    v.wait_ge(s["sq"], q + 1)
                    after(v, s["ho"], 2 * (q - 1))
                    nc.vector.reciprocal(rs[h], ve[h]).then_inc(s["rc"], 1)
                    v.wait_ge(s["rc"], q + 1)
                    if scaled:
                        nc.vector.tensor_tensor(rs[h], rs[h], m.dis[:, bass.ds(2 * q * J, 2 * J)], ALU.mult).then_inc(s["ds"], 1)
                        v.wait_ge(s["ds"], q + 1)
                    nc.vector.scalar_tensor_tensor(out=nb[h].unsqueeze(2), in0=mean2, scalar=-0.5, in1=rs[h].unsqueeze(2),
                                                   op0=ALU.mult, op1=ALU.mult).then_inc(s["nb"], 1)
            over_windows(v, body, windows)

        @block.scalar
        def _(act):
            def body(i, summed, last):
                for h in range(1 if last else 2):
                    q = 2 * i + h
                    if residual:
                        for u in (2 * h, 2 * h + 1):
                            w, p = U * i + u, parts(last, u)
                            if kind != "ln0":
                                act.wait_ge(s["xs"], w + 1)
                                act.dma_start(rows(m.X, w, p), xt[u][:p]).then_inc(stx[u], 16)
                        act.wait_ge(s["ve"], q + 1)
                        nc.scalar.activation(ve[h], ve[h], ACT.Sqrt).then_inc(s["sq"], 1)
                    for u in (2 * h, 2 * h + 1):
                        w, p = U * i + u, parts(last, u)
                        if residual:
                            act.wait_ge(s["nb"], q + 1)
                            if kind == "ln0":
                                act.wait_ge(ldx[u], 16 * (i + 1))
                            after(act, sth[u], 16 * i)
                            for j in range(J):
                                c = J * (u - 2 * h) + j
                                r = nc.scalar.activation(ho[u][:p, j * P:(j + 1) * P], xt[u][:p, j * P:(j + 1) * P], ACT.Relu,
                                                         bias=nb[h][:p, c:c + 1], scale=rs[h][:p, c:c + 1])
                            r.then_inc(s["ho"], 1)
                        elif kind == "rel":
                            act.wait_ge(s["yd"], w + 1)
                            after(act, sth[u], 16 * i)
                            nc.scalar.activation(ho[u][:p], t1[u][:p], ACT.Relu).then_inc(s["ho"], 1)
                        elif kind == "gat":
                            act.wait_ge(s["py"], w + 1)
                            after(act, sth[u], 16 * i)
                            nc.scalar.activation(ho[u][:], m.ps[U + u][:], ACT.Copy).then_inc(s["yd"], 1)
                        done = s["yd"] if kind == "gat" and not residual else s["ho"]
                        act.wait_ge(done, w + 1)
                        act.dma_start(rows(dest, w, p), ho[u][:p]).then_inc(sth[u], 16)
            over_windows(act, body, windows)
            for u in range(U):
                act.wait_ge(sth[u], 16 * rounds(u, windows))
                if residual and kind != "ln0":
                    act.wait_ge(stx[u], 16 * rounds(u, windows))


def attention_scores(nc, m, hop):
    a = m.a
    gs, gq, ea = m.big[0:2], m.big[2:4], m.big[4:6]
    sT, qT, eT, vs, f = m.big[6], m.big[7], m.big[8], m.big[9], m.big[10]
    vt = m.big[12:14]
    wn, we, wq = (m.wide[:, k * P:(k + 1) * P] for k in range(3))
    bias = m.sm[0]
    table, idx = (m.H, m.src) if hop == 0 else (m.HC, m.src_c)
    bS, bQ, bE, bV, bF, bC, bT = m.ps[0:7]
    names = "idx_ready w g0 g1 q0 q1 e0 e1 z bb tS tQ tE cS cQ cE pV pF vs f1 f2 sc vT cc vc st0 st1"
    with semaphores(nc, "att", names) as s, nc.Block() as block:
        gS, gQ, gE, stv = [s["g0"], s["g1"]], [s["q0"], s["q1"]], [s["e0"], s["e1"]], [s["st0"], s["st1"]]

        @block.sync
        def _(sp):
            for k, x in enumerate((a["L1_gnn_Wn"], a["L1_gnn_We"], a["L1_gnn_Wq"])):
                sp.dma_start((wn, we, wq)[k], x[hop]).then_inc(s["w"], 16)
            for k, x in ((0, a["L1_gnn_bq"]), (2, a["L1_gnn_attn"]), (3, a["L1_gnn_bn"]), (4, a["L1_gnn_be"])):
                sp.dma_start(bias[:, k:k + 1], x[hop].rearrange("(f o) -> f o", o=1)).then_inc(s["w"], 16)
            sp.wait_ge(s["z"], 1)

            def body(i, last):
                for u in range(2):
                    g = 2 * i + u
                    if last and u == 1:
                        continue
                    after(sp, s["tE"], g - 1)
                    if not last:
                        sp.dma_start(jview(ea[u]), a["edge_attr_128"][bass.ds(g * WIN, WIN), :].rearrange("(j p) f -> p j f", p=P)).then_inc(gE[u], 16)
                    else:
                        full = FULL % J
                        e0 = g * WIN
                        sp.dma_start(jview(ea[u])[:, 0:full, :], a["edge_attr_128"][e0:e0 + full * P, :].rearrange("(j p) f -> p j f", p=P)).then_inc(gE[u], 16)
                        sp.dma_start(ea[u][0:REST, full * P:(full + 1) * P], a["edge_attr_128"][FULL * P:E, :]).then_inc(gE[u], 16)
            over_groups(sp, body)

        @block.gpsimd
        def _(pool):
            def body(i, last):
                for u in range(2):
                    g = 2 * i + u
                    after(pool, s["tQ"], g - 1)
                    for k, cols in ((0, idx), (1, m.rank)):
                        nc.gpsimd.tensor_copy(m.stage_idx[u][:, k * J:(k + 1) * J], cols[:, bass.ds(g * J, J)]).then_inc(s["idx_ready"], 1)
                    pool.wait_ge(s["idx_ready"], 2)
                    pool.sem_clear(s["idx_ready"])
                    for k, dst_t, sem in ((0, gs[u], gS[u]), (1, gq[u], gQ[u])):
                        for j in range(J):
                            pool.indirect_dma_start(
                                out=dst_t[:, j * P:(j + 1) * P], out_offset=None, in_=table,
                                in_offset=bass.IndirectOffsetOnAxis(ap=m.stage_idx[u][:, k * J + j:k * J + j + 1], axis=0)).then_inc(sem, 16)
            over_groups(pool, body)

        @block.tensor
        def _(pe):
            pe.wait_ge(s["w"], 7 * 16)

            def body(i, last):
                for u in range(2):
                    g = 2 * i + u
                    for tile, bank, sem, read, done, when in (
                            (ea[u], bE, gE[u], s["cE"], s["tE"], 16 * (i + 1) + (16 if last and u == 0 else 0) - (16 if last and u == 1 else 0)),
                            (gs[u], bS, gS[u], s["cS"], s["tS"], 16 * J * (i + 1)), (gq[u], bQ, gQ[u], s["cQ"], s["tQ"], 16 * J * (i + 1))):
                        pe.wait_ge(sem, when)
                        after(pe, read, g)
                        for j in range(J):
                            tp = nc.tensor.transpose(bank[:, j * P:(j + 1) * P], tile[:, j * P:(j + 1) * P], m.ident[:])
                        tp.then_inc(done, 1)
                    after(pe, s["vs"], g)
                    pe.wait_ge(s["cE"], g + 1)
                    nc.tensor.matmul(bV[:], we, eT[:], start=True, stop=False)
                    pe.wait_ge(s["cS"], g + 1)
                    nc.tensor.matmul(bV[:], wn, sT[:], start=False, stop=True).then_inc(s["pV"], 1)
                    pe.wait_ge(s["cQ"], g + 1)
                    after(pe, s["f1"], g)
                    nc.tensor.matmul(bF[:], wq, qT[:], start=True, stop=True).then_inc(s["pF"], 1)
                    pe.wait_ge(s["vs"], g + 1)
                    after(pe, s["vc"], g)
                    for j in range(J):
                        t = nc.tensor.transpose(bT[:, j * P:(j + 1) * P], vs[:, j * P:(j + 1) * P], m.ident[:])
                    t.then_inc(s["vT"], 1)
                    pe.wait_ge(s["f2"], g + 1)
                    after(pe, s["cc"], g)
                    for j in range(J):
                        t = nc.tensor.matmul(bC[:, j:j + 1], f[:, j * P:(j + 1) * P], bias[:, 2:3], start=True, stop=True)
                    t.then_inc(s["sc"], 1)
            over_groups(pe, body)

        @block.scalar
        def _(act):
            act.wait_ge(s["bb"], 1)

            def body(i, last):
                for u in range(2):
                    g = 2 * i + u
                    act.wait_ge(s["tE"], g + 1)
                    after(act, s["pV"], g)
                    nc.scalar.activation(eT[:], bE[:], ACT.Copy).then_inc(s["cE"], 1)
                    act.wait_ge(s["tS"], g + 1)
                    nc.scalar.activation(sT[:], bS[:], ACT.Copy).then_inc(s["cS"], 1)
                    act.wait_ge(s["pV"], g + 1)
                    after(act, s["f1"], g)
                    after(act, s["vT"], g)
                    nc.scalar.activation(vs[:], bV[:], ACT.Identity, bias=bias[:, 1:2]).then_inc(s["vs"], 1)
                    act.wait_ge(s["vT"], g + 1)
                    after(act, stv[u], 16 * i)
                    nc.scalar.activation(vt[u][:], bT[:], ACT.Copy).then_inc(s["vc"], 1)
                    act.wait_ge(s["vc"], g + 1)
                    act.dma_start(m.V[bass.ds(g * WIN, WIN), :].rearrange("(j p) f -> p j f", p=P), jview(vt[u])).then_inc(stv[u], 16)
            over_groups(act, body)
            for u in range(2):
                act.wait_ge(stv[u], 16 * GROUPS // 2)

        @block.vector
        def _(v):
            nc.vector.memset(ea[0][:], 0.0)
            nc.vector.memset(ea[1][:], 0.0).then_inc(s["z"], 1)
            v.wait_ge(s["w"], 7 * 16)
            nc.vector.tensor_tensor(bias[:, 1:2], bias[:, 3:4], bias[:, 4:5], ALU.add).then_inc(s["bb"], 1)

            def body(i, last):
                for u in range(2):
                    g = 2 * i + u
                    v.wait_ge(s["tQ"], g + 1)
                    after(v, s["pF"], g)
                    nc.vector.tensor_copy(qT[:], bQ[:]).then_inc(s["cQ"], 1)
                    v.wait_ge(s["pF"], g + 1)
                    v.wait_ge(s["vs"], g + 1)
                    after(v, s["sc"], g)
                    nc.vector.scalar_tensor_tensor(out=f[:], in0=bF[:], scalar=bias[:, 0:1], in1=vs[:],
                                                   op0=ALU.add, op1=ALU.add).then_inc(s["f1"], 1)
                    v.wait_ge(s["f1"], g + 1)
                    nc.vector.scalar_tensor_tensor(out=f[:], in0=f[:], scalar=0.2, in1=f[:],
                                                   op0=ALU.mult, op1=ALU.max).then_inc(s["f2"], 1)
                    v.wait_ge(s["sc"], g + 1)
                    nc.vector.tensor_copy(m.score[:, bass.ds(g * J, J)], bC[:, 0:J]).then_inc(s["cc"], 1)
            over_groups(v, body)


def segment_softmax(nc, m):
    sc, fw, new, nxt, pen, penn, keep, tot = (m.big[k][:, 0:EC] for k in range(8))
    col, row = m.sm[1], m.sm[2]
    with semaphores(nc, "soft", "pa pb io d vp pv va av") as s, nc.Block() as block:
        @block.sync
        def _(sp):
            sp.dma_start(new, m.NEW[0:EPAD].rearrange("(p c) -> p c", c=EC)).then_inc(s["io"], 16)
            sp.dma_start(nxt, m.NEW[1:EPAD + 1].rearrange("(p c) -> p c", c=EC)).then_inc(s["io"], 16)
            sp.wait_ge(s["pb"], 1)
            sp.dma_start(m.LIN[0:ROWS_A * P].rearrange("(t e) -> t e", e=P), m.big[8][:, 0:P]).then_inc(s["io"], 16)
            sp.dma_start(m.LIN[ROWS_A * P:EPAD].rearrange("(t e) -> t e", e=P), m.big[8][0:ROWS_B, P:2 * P]).then_inc(s["io"], 16)
            sp.wait_ge(s["io"], 64)
            sp.dma_start(sc, m.LIN.rearrange("(p c) -> p c", c=EC)).then_inc(s["io"], 16)
            sp.wait_ge(s["pb"], 2)
            sp.dma_start(m.LIN.rearrange("(p c) -> p c", c=EC), tot).then_inc(s["io"], 16)
            sp.wait_ge(s["io"], 96)
            sp.dma_start(m.big[8][:, 0:P], m.LIN[0:ROWS_A * P].rearrange("(t e) -> t e", e=P)).then_inc(s["io"], 16)
            sp.dma_start(m.big[8][0:ROWS_B, P:2 * P], m.LIN[ROWS_A * P:EPAD].rearrange("(t e) -> t e", e=P)).then_inc(s["io"], 16)

        @block.tensor
        def _(pe):
            nc.tensor.transpose(m.ps[0][:, 0:P], m.score[:, 0:ROWS_A], m.ident[:])
            nc.tensor.transpose(m.ps[0][0:ROWS_B, P:2 * P], m.score[:, ROWS_A:TILES], m.ident[:]).then_inc(s["pa"], 1)
            for k in range(4):
                pe.wait_ge(s["vp"], 2 * k + 1)
                nc.tensor.transpose(m.ps[1][0:1, 0:P], col[:, 0:1], m.ident[:])
                nc.tensor.transpose(m.ps[1][0:1, P:2 * P], col[:, 1:2], m.ident[:]).then_inc(s["pv"], 1)
                pe.wait_ge(s["vp"], 2 * k + 2)
                nc.tensor.transpose(m.ps[2][:, 0:1], row[0:1, 0:P], m.ident[0:1, 0:1]).then_inc(s["pv"], 1)
            pe.wait_ge(s["io"], 128)
            nc.tensor.transpose(m.ps[3][:, 0:ROWS_A], m.big[8][:, 0:P], m.ident[:])
            nc.tensor.transpose(m.ps[3][:, ROWS_A:TILES], m.big[8][0:ROWS_B, P:2 * P], m.ident[0:ROWS_B, 0:ROWS_B]).then_inc(s["pa"], 1)

        @block.scalar
        def _(act):
            act.wait_ge(s["va"], 1)
            nc.scalar.activation(sc, sc, ACT.Exp).then_inc(s["av"], 1)

        @block.vector
        def _(v):
            n = [0]

            def link(ins):
                n[0] += 1
                ins.then_inc(s["d"], 1)
                v.wait_ge(s["d"], n[0])

            def rev(x):
                return x[:, ::-1]

            k = [0]

            def scan(dst, stop_, x, backward, op0, op1, unit):
                r = rev if backward else (lambda y: y)
                link(nc.vector.tensor_tensor_scan(r(dst), r(stop_), r(x), unit, op0, op1))
                end = 0 if backward else EC - 1
                link(nc.vector.tensor_copy(col[:, 0:1], dst[:, end:end + 1]))
                link(nc.vector.tensor_reduce(col[:, 1:2], stop_, AX.X, ALU.min))
                nc.vector.memset(row[0:1, 0:P], unit).then_inc(s["vp"], 1)
                k[0] += 1
                v.wait_ge(s["pv"], k[0])
                v.wait_ge(s["vp"], k[0])
                link(nc.vector.tensor_copy(row[0:1, P:2 * P], m.ps[1][0:1, P:2 * P]))
                link(nc.vector.tensor_copy(m.sm[3][0:1, 0:P], m.ps[1][0:1, 0:P]))
                link(nc.vector.tensor_tensor_scan(r(m.sm[3][0:1, P:2 * P]), r(row[0:1, P:2 * P]), r(m.sm[3][0:1, 0:P]),
                                                  unit, op0, op1))
                if backward:
                    nc.vector.tensor_copy(row[0:1, 0:P - 1], m.sm[3][0:1, P + 1:2 * P]).then_inc(s["vp"], 1)
                else:
                    nc.vector.tensor_copy(row[0:1, 1:P], m.sm[3][0:1, P:2 * P - 1]).then_inc(s["vp"], 1)
                k[0] += 1
                v.wait_ge(s["pv"], k[0])
                link(nc.vector.tensor_copy(col[:, 2:3], m.ps[2][:, 0:1]))
                link(nc.vector.tensor_tensor_scan(r(dst), r(stop_), r(x), col[:, 2:3], op0, op1))

            v.wait_ge(s["pa"], 1)
            link(nc.vector.tensor_copy(m.big[8][:, 0:P], m.ps[0][:, 0:P]))
            nc.vector.tensor_copy(m.big[8][0:ROWS_B, P:2 * P], m.ps[0][0:ROWS_B, P:2 * P]).then_inc(s["pb"], 1)
            v.wait_ge(s["io"], 80)
            link(nc.vector.tensor_scalar(pen, new, -BIG, None, ALU.mult))
            link(nc.vector.tensor_scalar(penn, nxt, -BIG, None, ALU.mult))
            link(nc.vector.tensor_scalar(keep, new, -1.0, 1.0, ALU.mult, ALU.add))
            scan(fw, pen, sc, False, ALU.add, ALU.max, -BIG)
            scan(tot, penn, fw, True, ALU.add, ALU.max, -BIG)
            nc.vector.tensor_tensor(sc, sc, tot, ALU.subtract).then_inc(s["va"], 1)
            v.wait_ge(s["av"], 1)
            scan(fw, keep, sc, False, ALU.mult, ALU.add, 0.0)
            scan(tot, penn, fw, True, ALU.add, ALU.max, -BIG)
            link(nc.vector.reciprocal(tot, tot))
            nc.vector.tensor_tensor(tot, tot, sc, ALU.mult).then_inc(s["pb"], 1)
            v.wait_ge(s["pa"], 2)
            nc.vector.tensor_copy(m.alpha[:], m.ps[3][:, 0:TILES]).then_inc(s["va"], 1)


def gin_first(nc, m, layer):
    hin, hT, z = m.big[0:U], m.big[U:2 * U], m.big[2 * U:3 * U]
    w_sb, b = m.w_sb[:], m.sm[0]
    with semaphores(nc, "gin1", "w ldh0 ldh1 ldh2 ldh3 tp hT hs pz z1 bs st0 st1 st2 st3") as s, nc.Block() as block:
        ldh, stz = ([s[f"{n}{u}"] for u in range(U)] for n in ("ldh", "st"))

        @block.sync
        def _(sp):
            sp.dma_start(w_sb, m.a["L3_gnn_W1"][layer]).then_inc(s["w"], 16)
            sp.dma_start(b[:, 0:1], m.a["L3_gnn_b1"][layer].rearrange("(f o) -> f o", o=1)).then_inc(s["w"], 16)

            def body(i, summed, last):
                for u in slots(last):
                    w, p = U * i + u, parts(last, u)
                    after(sp, s["tp"], w - U + 1)
                    sp.dma_start(hin[u][:p], rows(m.H, w, p)).then_inc(ldh[u], 16)
            over_windows(sp, body)

        @block.gpsimd
        def _(pool):
            clear_sums(nc, pool, m, s["hs"])

        @block.tensor
        def _(pe):
            pe.wait_ge(s["w"], 32)

            def body(i, summed, last):
                for u in slots(last):
                    w, p = U * i + u, parts(last, u)
                    pe.wait_ge(ldh[u], 16 * (i + 1))
                    after(pe, s["hT"], w - U + 1)
                    for j in range(J):
                        t = nc.tensor.transpose(m.ps[u][:, j * p:(j + 1) * p], hin[u][:p, j * P:(j + 1) * P], m.ident[:p, :p])
                    t.then_inc(s["tp"], 1)
                for u in slots(last):
                    w, p = U * i + u, parts(last, u)
                    pe.wait_ge(s["hs"], w + 1)
                    after(pe, s["z1"], w - U + 1)
                    nc.tensor.matmul(m.ps[U + u][:, 0:J * p], w_sb, hT[u][:, 0:J * p], start=True, stop=True).then_inc(s["pz"], 1)
            over_windows(pe, body)

        @block.scalar
        def _(act):
            act.wait_ge(s["w"], 32)

            def body(i, summed, last):
                for u in slots(last):
                    w, c = U * i + u, J * parts(last, u)
                    act.wait_ge(s["tp"], w + 1)
                    after(act, s["pz"], w - U + 1)
                    if layer:
                        nc.scalar.activation(hT[u][:, 0:c], m.ps[u][:, 0:c], ACT.Relu, bias=m.shift[:], scale=m.scale[:]).then_inc(s["hT"], 1)
                    else:
                        nc.scalar.activation(hT[u][:, 0:c], m.ps[u][:, 0:c], ACT.Copy).then_inc(s["hT"], 1)
                for u in slots(last):
                    w, c = U * i + u, J * parts(last, u)
                    act.wait_ge(s["pz"], w + 1)
                    after(act, s["bs"], w - U + 1)
                    after(act, stz[u], 16 * i)
                    nc.scalar.activation(z[u][:, 0:c], m.ps[U + u][:, 0:c], ACT.Identity, bias=b[:, 0:1]).then_inc(s["z1"], 1)
                    act.wait_ge(s["z1"], w + 1)
                    act.dma_start(m.Z1[bass.ds(w * P, P), 0:c], z[u][:, 0:c]).then_inc(stz[u], 16)
            over_windows(act, body)
            for u in range(U):
                act.wait_ge(stz[u], 16 * rounds(u))

        @block.vector
        def _(v):
            def body(i, summed, last):
                for u in slots(last):
                    w = U * i + u
                    v.wait_ge(s["hT"], w + 1)
                    if summed:
                        sums = m.sums[:, bass.ds(w * WIN, WIN)].rearrange("f (p j) -> f j p", j=J)
                        nc.vector.tensor_tensor(jview(hT[u]), jview(hT[u]), sums, ALU.add).then_inc(s["hs"], 1)
                    else:
                        nc.vector.memset(m.sm[1][:, u:u + 1], 0.0).then_inc(s["hs"], 1)
                for u in slots(last):
                    w, c = U * i + u, J * parts(last, u)
                    v.wait_ge(s["z1"], w + 1)
                    nc.vector.bn_stats(m.stats[:, bass.ds(w * 6, 6)], z[u][:, 0:c]).then_inc(s["bs"], 1)
            over_windows(v, body)
            v.wait_ge(s["bs"], NWIN)


def batch_norm(nc, m, gamma, beta, extra, layer):
    p = m.sm[0]
    with semaphores(nc, "bn", "ld d v a pe") as s, nc.Block() as block:
        @block.sync
        def _(sp):
            for k, x in enumerate((gamma, beta, extra)):
                if x is not None:
                    sp.dma_start(p[:, k:k + 1], x[layer].rearrange("(f o) -> f o", o=1)).then_inc(s["ld"], 16)

        @block.scalar
        def _(act):
            act.wait_ge(s["v"], 1)
            nc.scalar.activation(p[:, 5:6], p[:, 4:5], ACT.Sqrt).then_inc(s["a"], 1)

        @block.tensor
        def _(pe):
            pe.wait_ge(s["v"], 2)
            nc.tensor.matmul(m.ps[0][:, 0:P], m.sm[1][:, 0:P], m.ident[:], start=True, stop=True)
            nc.tensor.matmul(m.ps[0][:, P:2 * P], m.sm[2][:, 0:P], m.ident[:], start=True, stop=True).then_inc(s["pe"], 1)

        @block.vector
        def _(v):
            n = [0]

            def link(ins):
                n[0] += 1
                ins.then_inc(s["d"], 1)
                v.wait_ge(s["d"], n[0])
            link(nc.vector.bn_aggr(p[:, 3:5], m.stats[:]))
            v.wait_ge(s["ld"], 16 * (2 if extra is None else 3))
            nc.vector.tensor_scalar(p[:, 4:5], p[:, 4:5], EPS, None, ALU.add).then_inc(s["v"], 1)
            if extra is not None:
                link(nc.vector.tensor_tensor(p[:, 3:4], p[:, 3:4], p[:, 2:3], ALU.add))
            v.wait_ge(s["a"], 1)
            link(nc.vector.reciprocal(p[:, 6:7], p[:, 5:6]))
            link(nc.vector.tensor_tensor(m.scale[:], p[:, 6:7], p[:, 0:1], ALU.mult))
            link(nc.vector.tensor_tensor(p[:, 7:8], p[:, 3:4], m.scale[:], ALU.mult))
            link(nc.vector.tensor_tensor(m.shift[:], p[:, 1:2], p[:, 7:8], ALU.subtract))
            link(nc.vector.tensor_scalar(m.sm[1][:, 0:P], m.ones[:], m.scale[:], None, ALU.mult))
            nc.vector.tensor_scalar(m.sm[2][:, 0:P], m.ones[:], m.shift[:], None, ALU.mult).then_inc(s["v"], 1)
            v.wait_ge(s["pe"], 1)
            link(nc.vector.tensor_copy(m.scale_row[:], m.ps[0][:, 0:P]))
            link(nc.vector.tensor_copy(m.shift_row[:], m.ps[0][:, P:2 * P]))


def gin_second(nc, m, layer):
    final = layer == m.a["L3_gnn_W1"].shape[0] - 1
    zin, act_t, ho = m.big[0:U], m.big[U:2 * U], m.big[2 * U:3 * U]
    xz = m.pair
    w_sb = m.w_sb[:]
    with semaphores(nc, "gin2", "w wb ld0 ld1 ld2 ld3 lx0 lx1 lx2 lx3 a py pz ho bs st0 st1 st2 st3") as s, nc.Block() as block:
        ld, lx, sto = ([s[f"{n}{u}"] for u in range(U)] for n in ("ld", "lx", "st"))

        @block.sync
        def _(sp):
            sp.dma_start(w_sb, m.a["L3_gnn_W2"][layer]).then_inc(s["w"], 16)
            sp.dma_start(m.bias_row[:], bc(m.a["L3_gnn_b2"][layer].unsqueeze(0), [P, P])).then_inc(s["wb"], 16)

            def body(i, summed, last):
                for u in slots(last):
                    w, p = U * i + u, parts(last, u)
                    after(sp, s["a"], w - U + 1)
                    sp.dma_start(zin[u][:, 0:J * p], m.Z1[bass.ds(w * P, P), 0:J * p]).then_inc(ld[u], 16)
                    if final:
                        after(sp, sto[u], 16 * i)
                        sp.dma_start(xz[u][:p, :, 0:P], m.X[bass.ds(w * WIN, p * J), :].rearrange("(p j) f -> p j f", j=J)).then_inc(lx[u], 16)
            over_windows(sp, body)

        @block.scalar
        def _(act):
            def body(i, summed, last):
                for u in slots(last):
                    w, c = U * i + u, J * parts(last, u)
                    act.wait_ge(ld[u], 16 * (i + 1))
                    after(act, s["pz"], w - U + 1)
                    nc.scalar.activation(act_t[u][:, 0:c], zin[u][:, 0:c], ACT.Relu, bias=m.shift[:], scale=m.scale[:]).then_inc(s["a"], 1)
                for u in slots(last):
                    w, p = U * i + u, parts(last, u)
                    act.wait_ge(s["ho"], w + 1)
                    if final:
                        act.wait_ge(lx[u], 16 * (i + 1))
                        act.dma_start(m.XZ[bass.ds(w * WIN, p * J), :].rearrange("(p j) f -> p (j f)", j=J),
                                      xz[u][:p].rearrange("p j f -> p (j f)")).then_inc(sto[u], 16)
                    else:
                        act.dma_start(rows(m.H, w, p), ho[u][:p]).then_inc(sto[u], 16)
            over_windows(act, body)
            for u in range(U):
                act.wait_ge(sto[u], 16 * rounds(u))

        @block.tensor
        def _(pe):
            pe.wait_ge(s["w"], 16)

            def body(i, summed, last):
                for u in slots(last):
                    w, p = U * i + u, parts(last, u)
                    pe.wait_ge(s["a"], w + 1)
                    after(pe, s["ho"], w - U + 1)
                    for j in range(J):
                        t = nc.tensor.matmul(m.ps[u][:p, j * P:(j + 1) * P], act_t[u][:, j * p:(j + 1) * p], w_sb, start=True, stop=True)
                    t.then_inc(s["py"], 1)
                    after(pe, s["bs"], w - U + 1)
                    nc.tensor.matmul(m.ps[U + u][:, 0:J * p], w_sb, act_t[u][:, 0:J * p], start=True, stop=True).then_inc(s["pz"], 1)
            over_windows(pe, body)

        @block.vector
        def _(v):
            v.wait_ge(s["wb"], 16)

            def body(i, summed, last):
                for u in slots(last):
                    w, p = U * i + u, parts(last, u)
                    v.wait_ge(s["py"], w + 1)
                    after(v, sto[u], 16 * i)
                    dst = xz[u][:p, :, P:2 * P] if final else jview(ho[u], p)
                    nc.vector.tensor_tensor(dst, jview(m.ps[u], p), bc(m.bias_row[:p, :].unsqueeze(1), [p, J, P]), ALU.add).then_inc(s["ho"], 1)
                    v.wait_ge(s["pz"], w + 1)
                    nc.vector.bn_stats(m.stats[:, bass.ds(w * 6, 6)], m.ps[U + u][:, 0:J * p]).then_inc(s["bs"], 1)
            over_windows(v, body)
            v.wait_ge(s["bs"], NWIN)


def finish(nc, m):
    xz, o = m.pair, m.big[0:U]
    with semaphores(nc, "fin", "idx_ready g0 g1 g2 g3 t1 t2 t3 st0 st1 st2 st3") as s, nc.Block() as block:
        g, sto = ([s[f"{n}{u}"] for u in range(U)] for n in ("g", "st"))

        @block.gpsimd
        def _(pool):
            def body(i, summed, last):
                for u in slots(last):
                    w, p = U * i + u, parts(last, u)
                    after(pool, s["t3"], w - U + 1)
                    nc.gpsimd.tensor_copy(m.stage_idx[u][:p, 0:J], m.perm[:p, bass.ds(w * J, J)]).then_inc(s["idx_ready"], 1)
                    pool.wait_ge(s["idx_ready"], 1)
                    pool.sem_clear(s["idx_ready"])
                    for j in range(J):
                        pool.indirect_dma_start(
                            out=xz[u][:p, j, :], out_offset=None, in_=m.XZ,
                            in_offset=bass.IndirectOffsetOnAxis(ap=m.stage_idx[u][:p, j:j + 1], axis=0)).then_inc(g[u], 16)
            over_windows(pool, body)

        @block.vector
        def _(v):
            def body(i, summed, last):
                for u in slots(last):
                    w, p = U * i + u, parts(last, u)
                    v.wait_ge(g[u], 16 * J * (i + 1))
                    after(v, sto[u], 16 * i)
                    x, z, t = xz[u][:p, :, 0:P], xz[u][:p, :, P:2 * P], jview(o[u], p)
                    nc.vector.tensor_tensor(t, z, bc(m.scale_row[:p, :].unsqueeze(1), [p, J, P]), ALU.mult).then_inc(s["t1"], 1)
                    v.wait_ge(s["t1"], w + 1)
                    nc.vector.tensor_tensor(t, t, bc(m.shift_row[:p, :].unsqueeze(1), [p, J, P]), ALU.add).then_inc(s["t2"], 1)
                    v.wait_ge(s["t2"], w + 1)
                    nc.vector.tensor_tensor(t, t, x, ALU.add).then_inc(s["t3"], 1)
            over_windows(v, body)

        @block.sync
        def _(sp):
            def body(i, summed, last):
                for u in slots(last):
                    w, p = U * i + u, parts(last, u)
                    sp.wait_ge(s["t3"], w + 1)
                    sp.dma_start(rows(m.out, w, p), o[u][:p]).then_inc(sto[u], 16)
            over_windows(sp, body)
            for u in range(U):
                sp.wait_ge(sto[u], 16 * rounds(u))


INPUTS = ["x", "src", "dst", "edge_attr_128", "edge_type_4", "edge_weight", "L0_gnn_W", "L0_gnn_b", "L1_gnn_Wq",
          "L1_gnn_bq", "L1_gnn_Wn", "L1_gnn_bn", "L1_gnn_We", "L1_gnn_be", "L1_gnn_attn", "L2_gnn_W1", "L2_gnn_root1",
          "L2_gnn_b1", "L2_gnn_W2", "L2_gnn_root2", "L2_gnn_b2", "L3_gnn_W1", "L3_gnn_b1", "L3_gnn_g1", "L3_gnn_be1",
          "L3_gnn_W2", "L3_gnn_b2", "L3_gnn_g2", "L3_gnn_be2"]


def kernel(**inputs):
    import numpy as _np
    import concourse.bacc as _bacc
    from concourse import mybir as _mybir
    from concourse.bass_utils import run_bass_kernel_spmd as _run

    nc = _bacc.Bacc("TRN2", target_bir_lowering=False, num_devices=1)
    arrays, aps = {}, {}
    for name in INPUTS:
        arr = _np.ascontiguousarray(inputs[name])
        arrays[f"in_{name}_dram"] = arr
        aps[name] = nc.dram_tensor(f"in_{name}_dram", arr.shape, _mybir.dt.from_np(arr.dtype), kind="ExternalInput").ap()
    out = nc.dram_tensor("out_dram", (N, P), _mybir.dt.float32, kind="ExternalOutput").ap()
    build(nc, aps, out)
    r = _run(nc, [arrays], core_ids=[0])
    return r.results[0]["out_dram"]
```

```python
import concourse.bass as bass
from concourse import mybir
from contextlib import ExitStack, contextmanager

FP32 = mybir.dt.float32
I32 = mybir.dt.int32
ALU = mybir.AluOpType
ACT = mybir.ActivationFunctionType
AX = mybir.AxisListType

P = 128
N = 50000
E = 25000
J = 4
WIN = P * J
NWIN = -(-N // WIN)
TAIL_P = (N - (NWIN - 1) * WIN) // J
TILES = 200
GROUPS = TILES // J
EPAD = TILES * P
U = 4
SWIN = -(-EPAD // (WIN * U)) * U
SCOLS = SWIN * WIN
ITERS = -(-NWIN // U)
ROWS_A = P
ROWS_B = TILES - P
FULL = E // P
REST = E - FULL * P
STEP = 256
EPS = 1e-5
SKIP = float(1 << 20)
BIG = 1e30
HP, HC = 125, N // 125
EC = EPAD // P
assert N == HP * HC and TAIL_P * J + (NWIN - 1) * WIN == N and NWIN % U == 2


class Memory:
    pass


def after(eng, sem, value):
    if isinstance(value, int) and value <= 0:
        return
    eng.wait_ge(sem, value)


def bc(ap, shape):
    return ap.broadcast_to(shape)


@contextmanager
def semaphores(nc, stage, names):
    s = {n: nc.alloc_semaphore(f"{stage}_{n}_{nc.next_id()}") for n in names.split()}
    yield s
    nc.clear_and_free_semaphores([s[n] for n in s])
    nc.all_engine_barrier()


def over_windows(eng, body, windows=NWIN):
    body(0, True, False)
    body(1, True, False)
    with eng.Fori(2, SWIN // U) as i:
        body(i, True, False)
    if windows == NWIN:
        with eng.Fori(SWIN // U, ITERS - 1) as i:
            body(i, False, False)
        body(ITERS - 1, False, True)



def started(i, count=1):
    return not isinstance(i, int) or i >= count


def clear_sums(nc, pool, m, used):
    def body(i, summed, last):
        for u in range(U):
            w = U * i + u
            pool.wait_ge(used, w + 1)
            nc.gpsimd.tensor_copy(m.sums[:, bass.ds(w * WIN, WIN)], bc(m.zeros[:, 0:1], [P, WIN]))
    over_windows(pool, body, SWIN)


def slots(last):
    return range(NWIN % U if last else U)


def rounds(u, windows=NWIN):
    return -(-(windows - u) // U)


def over_groups(eng, body):
    body(0, False)
    with eng.Fori(1, GROUPS // 2 - 1) as i:
        body(i, False)
    body(GROUPS // 2 - 1, True)


def parts(last, u):
    return TAIL_P if last and u == 1 else P


def rows(table, w, p=P):
    return table[bass.ds(w * WIN, p * J), :].rearrange("(p j) f -> p (j f)", j=J)


def jview(tile, p=P):
    return tile[:p, :].rearrange("p (j f) -> p j f", j=J)


def build(nc, a, out):
    ctx = ExitStack()
    sb = lambda name, shape, dt=FP32: ctx.enter_context(nc.sbuf_tensor(name, shape, dt))
    dram = lambda name, shape, dt=FP32: nc.dram_tensor(name, shape, dt).ap()
    with ctx:
        m = Memory()
        m.a, m.out = a, out
        m.X = dram("X", [N, P])
        m.H = dram("H", [N, P])
        m.HC = dram("HC", [SCOLS + P, P])
        m.Z1 = dram("Z1", [NWIN * P, WIN])
        m.XZ = dram("XZ", [N, 2 * P])
        m.V = dram("V", [EPAD, P])
        m.HAS = dram("HAS", [N, 1])
        m.PERM = dram("PERM", [N, 1], I32)
        m.NEW = dram("NEW", [EPAD + P])
        m.LIN = dram("LIN", [EPAD])
        m.DEG = dram("DEG", [SCOLS])
        m.ident = sb("ident", [P, P])
        m.upper = sb("upper", [P, P])
        m.ones = sb("ones", [P, P])
        m.zeros = sb("zeros", [P, HC])
        m.iota = sb("iota", [P, P])
        m.src_old = sb("src_old", [P, TILES], I32)
        m.src = sb("src", [P, TILES], I32)
        m.src_c = sb("src_c", [P, TILES], I32)
        m.rank = sb("rank", [P, TILES], I32)
        m.has_idx = sb("has_idx", [P, TILES], I32)
        m.local = sb("local", [P, TILES])
        m.first = sb("first", [1, GROUPS], I32)
        m.steps = sb("steps", [1, GROUPS], I32)
        m.zero_k = sb("zero_k", [1, WIN], mybir.dt.bfloat16)
        m.alpha = sb("alpha", [P, TILES])
        m.score = sb("score", [P, TILES])
        m.tw = sb("tw", [P, TILES, J])
        m.perm = sb("perm", [P, NWIN * J], I32)
        m.dis = sb("dis", [P, NWIN * J])
        m.stats = sb("stats", [P, NWIN * 6])
        m.scale = sb("scale", [P, 1])
        m.shift = sb("shift", [P, 1])
        m.scale_row = sb("scale_row", [P, P])
        m.shift_row = sb("shift_row", [P, P])
        m.bias_row = sb("bias_row", [P, P])
        m.sums = sb("sums", [P, SCOLS])
        m.stage_idx = [sb(f"stage_idx{u}", [P, 8], I32) for u in range(U)]
        m.work = sb("work", [P, 6 * U, WIN])
        m.big = [m.work[:, k, :] for k in range(6 * U)]
        m.sm = [sb(f"small{k}", [P, 256]) for k in range(5)]
        m.w_sb = sb("w_sb", [P, P])
        m.small_i = sb("small_i", [P, 512], I32)
        m.pair = [m.work[:, 4 * U + 2 * u:4 * U + 2 * u + 2, :].rearrange("p a (b f) -> p (a b) f", f=2 * P) for u in range(U // 2)]
        m.pair += [m.work[:, 3 * U + 2 * u:3 * U + 2 * u + 2, :].rearrange("p a (b f) -> p (a b) f", f=2 * P) for u in range(U // 2)]
        m.wide = sb("wide", [P, 4 * P])
        m.ps = [ctx.enter_context(nc.psum_tensor(f"ps{k}", [P, WIN], FP32)) for k in range(8)]

        constants(nc, m)
        edge_lists(nc, m)
        mark_receivers(nc, m)
        renumber(nc, m)
        relation_weights(nc, m)
        degrees(nc, m)
        permute_input(nc, m)

        residual_pass(nc, m, "ln0", scaled=True)
        for k in range(3):
            edge_pass(nc, m, "gather")
            if k < 2:
                node_pass(nc, m, "gcn", a["L0_gnn_W"], a["L0_gnn_b"])
        residual_pass(nc, m, "gcn", a["L0_gnn_W"], a["L0_gnn_b"])

        for k in range(3):
            attention_scores(nc, m, k)
            segment_softmax(nc, m)
            edge_pass(nc, m, "values", scaled=True)
            if k < 2:
                node_pass(nc, m, "gat")
        residual_pass(nc, m, "gat")

        relation_pass(nc, m, a["L2_gnn_W1"])
        node_pass(nc, m, "rel", a["L2_gnn_root1"], a["L2_gnn_b1"])
        relation_pass(nc, m, a["L2_gnn_W2"])
        residual_pass(nc, m, "rel", a["L2_gnn_root2"], a["L2_gnn_b2"])

        for k in range(a["L3_gnn_W1"].shape[0]):
            edge_pass(nc, m, "gather", normed=k > 0)
            gin_first(nc, m, k)
            batch_norm(nc, m, a["L3_gnn_g1"], a["L3_gnn_be1"], None, k)
            gin_second(nc, m, k)
            batch_norm(nc, m, a["L3_gnn_g2"], a["L3_gnn_be2"], a["L3_gnn_b2"], k)
        finish(nc, m)


def constants(nc, m):
    with semaphores(nc, "const", "z made zrows zinit") as s, nc.Block() as block:
        @block.gpsimd
        def _(pool):
            nc.gpsimd.memset(m.ident[:], 0.0).then_inc(s["z"], 1)
            nc.gpsimd.memset(m.ones[:], 1.0)
            nc.gpsimd.memset(m.zero_k[:], 0.0)
            nc.gpsimd.memset(m.zeros[:], 0.0).then_inc(s["zinit"], 1)
            nc.gpsimd.memset(m.sums[:], 0.0)
            nc.gpsimd.iota(m.iota[:], pattern=[[1, P]], base=0, channel_multiplier=0,
                           allow_small_or_imprecise_dtypes=True)
            nc.gpsimd.memset(m.upper[:], 1.0).then_inc(s["z"], 1)
            pool.wait_ge(s["z"], 2)
            nc.gpsimd.affine_select(out=m.ident[:], in_=m.ident[:], compare_op=ALU.not_equal, fill=1.0,
                                    base=0, pattern=[[-1, P]], channel_multiplier=1).then_inc(s["made"], 1)
            nc.gpsimd.affine_select(out=m.upper[:], in_=m.upper[:], compare_op=ALU.is_gt, fill=0.0,
                                    base=0, pattern=[[1, P]], channel_multiplier=-1).then_inc(s["made"], 1)
            pool.wait_ge(s["made"], 2)

        @block.sync
        def _(sp):
            sp.wait_ge(s["zinit"], 1)
            sp.dma_start(m.HC[SCOLS:SCOLS + P, :], m.zeros[:, :P]).then_inc(s["zrows"], 16)
            sp.dma_start(m.HAS.rearrange("(p c) o -> p (c o)", p=HP), m.zeros[:HP, :]).then_inc(s["zrows"], 16)
            sp.wait_ge(s["zrows"], 32)


def load_tiled(sp, dst_a, dst_b, vec, sem):
    sp.dma_start(dst_a, vec[0:ROWS_A * P].rearrange("(t e) -> t e", e=P)).then_inc(sem, 16)
    sp.dma_start(dst_b[0:FULL - ROWS_A, :], vec[ROWS_A * P:FULL * P].rearrange("(t e) -> t e", e=P)).then_inc(sem, 16)
    sp.dma_start(dst_b[FULL - ROWS_A:FULL - ROWS_A + 1, 0:REST],
                 vec[FULL * P:E].rearrange("(t e) -> t e", t=1)).then_inc(sem, 16)


def edge_lists(nc, m):
    A, B = slice(0, ROWS_A), slice(0, ROWS_B)
    blocks = ((0, ROWS_A), (1, ROWS_B))
    di = [m.small_i[:, 0:P], m.small_i[:, P:2 * P]]
    si = [m.small_i[:, 2 * P:3 * P], m.small_i[:, 3 * P:4 * P]]
    pi = [m.src_old[:, 0:P], m.rank[:, 0:P]]
    dst, prev, new, scan, rnk, loc, srcf, hidx, ok, tmp = (
        [m.big[k][:, 0:P], m.big[k][:, P:2 * P]] for k in range(10))
    base, cols = m.sm[0], m.sm[1]
    with semaphores(nc, "prep", "fill ld d pe pp st") as s, nc.Block() as block:
        @block.sync
        def _(sp):
            sp.wait_ge(s["fill"], 1)
            load_tiled(sp, di[0], di[1], m.a["dst"], s["ld"])
            load_tiled(sp, si[0], si[1], m.a["src"], s["ld"])
            v = m.a["dst"]
            sp.dma_start(pi[0][0:1, 1:P], v[0:P - 1].rearrange("(t e) -> t e", t=1)).then_inc(s["ld"], 16)
            sp.dma_start(pi[0][1:P, :], v[P - 1:P * ROWS_A - 1].rearrange("(t e) -> t e", e=P)).then_inc(s["ld"], 16)
            sp.dma_start(pi[1][0:FULL - ROWS_A, :], v[P * ROWS_A - 1:P * FULL - 1].rearrange("(t e) -> t e", e=P)).then_inc(s["ld"], 16)
            sp.dma_start(pi[1][FULL - ROWS_A:FULL - ROWS_A + 1, 0:REST + 1],
                         v[P * FULL - 1:E].rearrange("(t e) -> t e", t=1)).then_inc(s["ld"], 16)
            sp.wait_ge(s["st"], 1)
            sp.dma_start(m.NEW[0:ROWS_A * P].rearrange("(t e) -> t e", e=P), new[0]).then_inc(s["pp"], 16)
            sp.dma_start(m.NEW[ROWS_A * P:EPAD].rearrange("(t e) -> t e", e=P), new[1][B, :]).then_inc(s["pp"], 16)
            sp.dma_start(m.NEW[EPAD:EPAD + P].rearrange("(t e) -> t e", t=1), m.ones[0:1, :]).then_inc(s["pp"], 16)
            sp.wait_ge(s["pp"], 48)

        @block.vector
        def _(v):
            n = [0]

            def link(ins):
                n[0] += 1
                ins.then_inc(s["d"], 1)
                v.wait_ge(s["d"], n[0])

            link(nc.vector.memset(m.small_i[:, 0:2 * P], -1))
            link(nc.vector.memset(m.small_i[:, 2 * P:4 * P], 0))
            link(nc.vector.memset(pi[0], -5))
            link(nc.vector.memset(pi[1], -1))
            nc.vector.memset(cols[:], 0.0).then_inc(s["fill"], 1)
            v.wait_ge(s["ld"], 10 * 16)
            v.wait_ge(s["fill"], 1)
            for b, r in blocks:
                q = slice(0, r)
                link(nc.vector.tensor_copy(dst[b][q], di[b][q]))
                link(nc.vector.tensor_copy(prev[b][q], pi[b][q]))
                link(nc.vector.tensor_copy(srcf[b][q], si[b][q]))
                link(nc.vector.tensor_tensor(new[b][q], dst[b][q], prev[b][q], ALU.not_equal))
                link(nc.vector.tensor_tensor_scan(scan[b][q], new[b][q], m.zeros[q, 0:P], 0.0, ALU.add, ALU.add))
                link(nc.vector.tensor_copy(cols[q, b:b + 1], scan[b][q, P - 1:P]))
                link(nc.vector.tensor_scalar(ok[b][q], dst[b][q], 0.0, None, ALU.is_ge))
            nc.vector.tensor_copy(cols[:, 2:3], cols[:, 0:1]).then_inc(s["st"], 1)
            v.wait_ge(s["pe"], 1)
            link(nc.vector.tensor_scalar(base[:, 0:2], m.ps[0][:, 0:2], -1.0, None, ALU.add))
            for b, r in blocks:
                q = slice(0, r)
                link(nc.vector.tensor_scalar(rnk[b][q], scan[b][q], base[q, b:b + 1], None, ALU.add))
                link(nc.vector.tensor_scalar(loc[b][q], rnk[b][q], rnk[b][q, 0:1], 1.0, ALU.subtract, ALU.add))
                link(nc.vector.tensor_tensor(loc[b][q], loc[b][q], ok[b][q], ALU.mult))
                link(nc.vector.tensor_scalar(loc[b][q], loc[b][q], -1.0, None, ALU.add))
                link(nc.vector.tensor_tensor(tmp[b][q], new[b][q], ok[b][q], ALU.mult))
                link(nc.vector.scalar_tensor_tensor(out=hidx[b][q], in0=dst[b][q], scalar=-SKIP, in1=tmp[b][q],
                                                    op0=ALU.add, op1=ALU.mult))
                link(nc.vector.tensor_scalar(hidx[b][q], hidx[b][q], SKIP, None, ALU.add))
            nc.vector.tensor_copy(cols[:, 3:4], cols[:, 0:1]).then_inc(s["st"], 1)
            v.wait_ge(s["pe"], 2)
            link(nc.vector.tensor_copy(m.rank[:], m.ps[1][:, 0:TILES]))
            link(nc.vector.tensor_copy(cols[0:1, 0:TILES], m.ps[1][0:1, 0:TILES]))
            f4 = cols[0:1, 0:TILES].rearrange("o (g j) -> o g j", j=J)
            d3 = base[0:1, 0:3 * GROUPS].rearrange("o (g j) -> o g j", j=3)
            link(nc.vector.tensor_copy(m.first[:].unsqueeze(2), f4[:, :, 0:1]))
            link(nc.vector.tensor_tensor(d3, f4[:, :, 1:4], f4[:, :, 0:3], ALU.subtract))
            for c in (2, 1):
                link(nc.vector.scalar_tensor_tensor(out=d3[:, :, c - 1:c], in0=d3[:, :, c:c + 1], scalar=float(STEP),
                                                    in1=d3[:, :, c - 1:c], op0=ALU.mult, op1=ALU.add))
            link(nc.vector.tensor_copy(m.steps[:].unsqueeze(2), d3[:, :, 0:1]))
            link(nc.vector.tensor_copy(m.local[:], m.ps[2][:, 0:TILES]))
            link(nc.vector.tensor_copy(m.src_old[:], m.ps[3][:, 0:TILES]))
            link(nc.vector.tensor_copy(m.has_idx[:], m.ps[4][:, 0:TILES]))

        @block.tensor
        def _(pe):
            pe.wait_ge(s["st"], 1)
            nc.tensor.matmul(m.ps[0][:, 0:1], m.upper[:], cols[:, 0:1], start=True, stop=True)
            nc.tensor.matmul(m.ps[0][:, 1:2], m.ones[:], cols[:, 0:1], start=True, stop=False)
            nc.tensor.matmul(m.ps[0][:, 1:2], m.upper[:], cols[:, 1:2], start=False, stop=True).then_inc(s["pe"], 1)
            pe.wait_ge(s["st"], 2)
            for k, x in enumerate((rnk, loc, srcf, hidx)):
                nc.tensor.transpose(m.ps[1 + k][:, 0:ROWS_A], x[0][A], m.ident[:])
                last = nc.tensor.transpose(m.ps[1 + k][:, ROWS_A:TILES], x[1][B], m.ident[0:ROWS_B, 0:ROWS_B])
            last.then_inc(s["pe"], 1)


def indexed_loop(nc, s, cols, stages, each, free):
    pool = nc.gpsimd

    def body(i, last):
        for u in range(2):
            free(i, u)
            stage = stages[u][:, 0:J]
            nc.gpsimd.tensor_copy(stage, cols[:, bass.ds((2 * i + u) * J, J)]).then_inc(s["idx_ready"], 1)
            pool.wait_ge(s["idx_ready"], 1)
            pool.sem_clear(s["idx_ready"])
            each(i, u, stage)
    over_groups(pool, body)


def mark_receivers(nc, m):
    with semaphores(nc, "has", "idx_ready sc0 sc1 d") as s, nc.Block() as block:
        sc = [s["sc0"], s["sc1"]]

        @block.gpsimd
        def _(pool):
            def free(i, u):
                after(pool, sc[u], i * 16 * J)

            def each(i, u, stage):
                for j in range(J):
                    pool.indirect_dma_start(
                        out=m.HAS, out_offset=bass.IndirectOffsetOnAxis(ap=stage[:, j:j + 1], axis=0),
                        in_=m.ones[:, 0:1], in_offset=None, bounds_check=N - 1, oob_is_err=False).then_inc(sc[u], 16)
            indexed_loop(nc, s, m.has_idx, m.stage_idx, each, free)
            for u in range(2):
                pool.wait_ge(sc[u], GROUPS // 2 * 16 * J)


def renumber(nc, m):
    has, inc, num, t = (m.big[k][0:HP, 0:HC] for k in range(4))
    permi = m.small_i[0:HP, 0:HC]
    with semaphores(nc, "perm", "ld d tot pe io out back") as s, nc.Block() as block:
        @block.sync
        def _(sp):
            sp.dma_start(has, m.HAS.rearrange("(p c) o -> p (c o)", p=HP)).then_inc(s["ld"], 16)
            sp.wait_ge(s["out"], 1)
            sp.dma_start(m.PERM.rearrange("(p c) o -> p (c o)", p=HP), permi).then_inc(s["back"], 16)
            sp.wait_ge(s["back"], 16)
            full = (NWIN - 1) * WIN
            sp.dma_start(m.perm[:, 0:(NWIN - 1) * J].rearrange("p (w j) -> p w j", j=J),
                         m.PERM[0:full, :].rearrange("(w p j) o -> p w (j o)", p=P, j=J)).then_inc(s["back"], 16)
            sp.dma_start(m.perm[0:TAIL_P, (NWIN - 1) * J:NWIN * J],
                         m.PERM[full:N, :].rearrange("(p j) o -> p (j o)", j=J)).then_inc(s["back"], 16)
            sp.wait_ge(s["back"], 48)

        @block.gpsimd
        def _(pool):
            nc.gpsimd.iota(num, pattern=[[1, HC]], base=0, channel_multiplier=HC,
                           allow_small_or_imprecise_dtypes=True).then_inc(s["io"], 1)

        @block.vector
        def _(v):
            n = [0]

            def link(ins):
                n[0] += 1
                ins.then_inc(s["d"], 1)
                v.wait_ge(s["d"], n[0])
            v.wait_ge(s["ld"], 16)
            link(nc.vector.tensor_tensor_scan(inc, has, m.zeros[0:HP, 0:HC], 0.0, ALU.add, ALU.add))
            nc.vector.tensor_copy(m.sm[0][0:HP, 0:1], inc[:, HC - 1:HC]).then_inc(s["tot"], 1)
            v.wait_ge(s["pe"], 1)
            link(nc.vector.tensor_copy(m.sm[1][0:HP, 0:2], m.ps[0][0:HP, 0:2]))
            link(nc.vector.tensor_scalar(inc, inc, m.sm[1][0:HP, 0:1], None, ALU.add))
            v.wait_ge(s["io"], 1)
            link(nc.vector.scalar_tensor_tensor(out=t, in0=num, scalar=m.sm[1][0:HP, 1:2], in1=inc,
                                                op0=ALU.add, op1=ALU.subtract))
            link(nc.vector.scalar_tensor_tensor(out=inc, in0=inc, scalar=-1.0, in1=t, op0=ALU.add, op1=ALU.subtract))
            link(nc.vector.tensor_tensor(inc, inc, has, ALU.mult))
            nc.vector.tensor_tensor(permi, inc, t, ALU.add).then_inc(s["out"], 1)

        @block.tensor
        def _(pe):
            pe.wait_ge(s["tot"], 1)
            nc.tensor.matmul(m.ps[0][:, 0:1], m.upper[0:HP, :], m.sm[0][0:HP, 0:1], start=True, stop=True)
            nc.tensor.matmul(m.ps[0][:, 1:2], m.ones[0:HP, :], m.sm[0][0:HP, 0:1], start=True, stop=True).then_inc(s["pe"], 1)


def renumber_senders(nc, pool, m, s):
    got_i = [m.small_i[:, u * J:(u + 1) * J] for u in range(2)]
    g = [s["s0"], s["s1"]]

    def keep(turn, u):
        pool.wait_ge(g[u], 16 * J * (turn + 1))
        nc.gpsimd.tensor_copy(m.src[:, bass.ds((2 * turn + u) * J, J)], got_i[u]).then_inc(s["kept"], 1)

    def free(i, u):
        if started(i):
            keep(i - 1, u)
            pool.wait_ge(s["kept"], 2 * i + u - 1)

    def each(i, u, stage):
        for j in range(J):
            pool.indirect_dma_start(
                out=got_i[u][:, j:j + 1], out_offset=None, in_=m.PERM,
                in_offset=bass.IndirectOffsetOnAxis(ap=stage[:, j:j + 1], axis=0)).then_inc(g[u], 16)
    indexed_loop(nc, s, m.src_old, m.stage_idx, each, free)
    for u in range(2):
        keep(GROUPS // 2 - 1, u)
    pool.wait_ge(s["kept"], GROUPS)
    nc.gpsimd.tensor_scalar(m.src_c[:], m.src[:], float(SCOLS), None, ALU.min).then_inc(s["kept"], 1)
    pool.wait_ge(s["kept"], GROUPS + 1)


def relation_weights(nc, m):
    ew = [m.big[0][:, 0:P], m.big[0][:, P:2 * P]]
    ti = [m.small_i[:, 0:P], m.small_i[:, P:2 * P]]
    tf = [m.big[1][:, 0:P], m.big[1][:, P:2 * P]]
    lin = m.big[2][0:100, 0:250]
    c = m.sm[0]
    with semaphores(nc, "types", "fill ld d a pe b") as s, nc.Block() as block:
        @block.sync
        def _(sp):
            sp.wait_ge(s["fill"], 1)
            load_tiled(sp, ew[0], ew[1], m.a["edge_weight"], s["ld"])
            load_tiled(sp, ti[0], ti[1], m.a["edge_type_4"], s["ld"])
            sp.dma_start(lin, m.a["edge_weight"].rearrange("(p c) -> p c", p=100)).then_inc(s["ld"], 16)

        @block.vector
        def _(v):
            n = [0]

            def link(ins):
                n[0] += 1
                ins.then_inc(s["d"], 1)
                v.wait_ge(s["d"], n[0])
            link(nc.vector.memset(m.big[0][:, 0:2 * P], 0.0))
            nc.vector.memset(m.small_i[:, 0:2 * P], 0).then_inc(s["fill"], 1)
            v.wait_ge(s["ld"], 7 * 16)
            link(nc.vector.tensor_copy(m.big[1][:, 0:2 * P], m.small_i[:, 0:2 * P]))
            link(nc.vector.tensor_reduce(c[0:100, 0:1], lin, AX.X, ALU.max))
            link(nc.vector.tensor_reduce(c[0:100, 1:2], lin, AX.X, ALU.min))
            nc.vector.tensor_copy(c[0:100, 2:4], c[0:100, 0:2]).then_inc(s["a"], 1)
            v.wait_ge(s["pe"], 1)
            link(nc.vector.tensor_copy(m.sm[3][:, 0:TILES], m.ps[1][:, 0:TILES]))
            link(nc.vector.tensor_copy(m.sm[4][:, 0:TILES], m.ps[2][:, 0:TILES]))
            link(nc.vector.tensor_reduce(m.sm[1][0:1, 0:1], m.ps[0][0:1, 0:100], AX.X, ALU.max))
            link(nc.vector.tensor_reduce(m.sm[1][0:1, 1:2], m.ps[3][0:1, 0:100], AX.X, ALU.min))
            link(nc.vector.tensor_tensor(m.sm[1][0:1, 2:3], m.sm[1][0:1, 0:1], m.sm[1][0:1, 1:2], ALU.subtract))
            link(nc.vector.tensor_scalar(m.sm[1][0:1, 2:3], m.sm[1][0:1, 2:3], 1e-8, None, ALU.add))
            nc.vector.reciprocal(m.sm[1][0:1, 2:3], m.sm[1][0:1, 2:3]).then_inc(s["b"], 1)
            v.wait_ge(s["pe"], 2)
            link(nc.vector.tensor_copy(m.sm[2][:, 0:2], m.ps[4][:, 0:2]))
            link(nc.vector.tensor_scalar(m.sm[3][:, 0:TILES], m.sm[3][:, 0:TILES], m.sm[2][:, 0:1], m.sm[2][:, 1:2],
                                         ALU.subtract, ALU.mult))
            for r in range(J):
                link(nc.vector.scalar_tensor_tensor(out=m.tw[:, :, r], in0=m.sm[4][:, 0:TILES], scalar=float(r),
                                                    in1=m.sm[3][:, 0:TILES], op0=ALU.is_equal, op1=ALU.mult))

        @block.tensor
        def _(pe):
            pe.wait_ge(s["a"], 1)
            for k, x in ((1, ew), (2, tf)):
                nc.tensor.transpose(m.ps[k][:, 0:ROWS_A], x[0], m.ident[:])
                nc.tensor.transpose(m.ps[k][:, ROWS_A:TILES], x[1][0:ROWS_B], m.ident[0:ROWS_B, 0:ROWS_B])
            nc.tensor.transpose(m.ps[0][0:1, 0:100], c[0:100, 2:3], m.ident[0:100, 0:100])
            nc.tensor.transpose(m.ps[3][0:1, 0:100], c[0:100, 3:4], m.ident[0:100, 0:100]).then_inc(s["pe"], 1)
            pe.wait_ge(s["b"], 1)
            nc.tensor.matmul(m.ps[4][:, 0:2], m.ones[0:1, :], m.sm[1][0:1, 1:3], start=True, stop=True).then_inc(s["pe"], 1)


def degrees(nc, m):
    edge_pass(nc, m, "ones")
    deg = m.dis
    with semaphores(nc, "deg", "io z a d") as s, nc.Block() as block:
        @block.sync
        def _(sp):
            sp.dma_start(m.DEG.rearrange("(o n) -> o n", o=1), m.sums[0:1, :]).then_inc(s["io"], 16)
            sp.wait_ge(s["io"], 16)
            sp.wait_ge(s["z"], 1)
            sp.dma_start(deg[:, 0:SWIN * J].rearrange("p (w j) -> p w j", j=J),
                         m.DEG.rearrange("(w p j) -> p w j", p=P, j=J)).then_inc(s["io"], 16)

        @block.vector
        def _(v):
            nc.vector.memset(deg[:], 0.0).then_inc(s["z"], 1)
            v.wait_ge(s["io"], 32)
            nc.vector.memset(m.sums[:], 0.0)
            nc.vector.tensor_scalar(deg[:], deg[:], 1.0, None, ALU.add).then_inc(s["d"], 1)
            v.wait_ge(s["a"], 1)
            nc.vector.reciprocal(m.dis[:], deg[:]).then_inc(s["d"], 1)

        @block.scalar
        def _(act):
            act.wait_ge(s["d"], 1)
            nc.scalar.activation(deg[:], deg[:], ACT.Sqrt).then_inc(s["a"], 1)


def permute_input(nc, m):
    with semaphores(nc, "permx", "ld0 ld1 ld2 ld3 sc0 sc1 sc2 sc3 idx_ready") as s, nc.Block() as block:
        ld, sc = ([s[f"{n}{u}"] for u in range(U)] for n in ("ld", "sc"))

        @block.sync
        def _(sp):
            def body(i, summed, last):
                for u in slots(last):
                    p = parts(last, u)
                    after(sp, sc[u], i * 16 * J)
                    sp.dma_start(m.big[u][:p, :], rows(m.a["x"], U * i + u, p)).then_inc(ld[u], 16)
            over_windows(sp, body)

        @block.gpsimd
        def _(pool):
            def body(i, summed, last):
                for u in slots(last):
                    p = parts(last, u)
                    pool.wait_ge(ld[u], 16 * (i + 1))
                    nc.gpsimd.tensor_copy(m.stage_idx[u][:p, 0:J], m.perm[:p, bass.ds((U * i + u) * J, J)]).then_inc(s["idx_ready"], 1)
                    pool.wait_ge(s["idx_ready"], 1)
                    pool.sem_clear(s["idx_ready"])
                    for j in range(J):
                        pool.indirect_dma_start(
                            out=m.X, out_offset=bass.IndirectOffsetOnAxis(ap=m.stage_idx[u][:p, j:j + 1], axis=0),
                            in_=m.big[u][:p, j * P:(j + 1) * P], in_offset=None).then_inc(sc[u], 16)
            over_windows(pool, body)
            for u in range(U):
                pool.wait_ge(sc[u], rounds(u) * 16 * J)


def tile_columns(pe, m, banks, g):
    packed = pe.value_load(m.steps[0:1, bass.ds(g, 1)], min_val=0, max_val=P * (1 + STEP + STEP * STEP))
    first = [0]
    for j in range(1, J):
        step = (packed >> (8 * (j - 1))) & (STEP - 1) if j < J - 1 else packed >> (8 * (j - 1))
        first.append(pe.snap((first[-1] + step).with_bounds(min_val=0, max_val=j * P)))
    return [[bank[:, bass.ds(x, P)] for x in first] for bank in banks]


def clear_bank(nc, m, bank):
    nc.tensor.matmul(bank[:], m.zero_k[:, 0:P], m.zero_k[:], start=True, stop=False, skip_group_check=True)


def group_columns(v, m, g):
    first = v.value_load(m.first[0:1, bass.ds(g, 1)], min_val=0, max_val=EPAD - WIN)
    return m.sums[:, bass.ds(first, WIN)]


def add_sums(nc, v, s, g, cols, bank):
    after(v, s["added"], g)
    nc.vector.tensor_tensor(cols, cols, bank[:], ALU.add).then_inc(s["added"], 1)


def edge_pass(nc, m, source, scaled=False, normed=False):
    got_t = m.big[0:2]
    tr = m.big[2:4]
    hot = m.big[4:6]
    with semaphores(nc, "edge", "idx_ready g0 g1 g2 g3 g4 g5 g6 g7 hot hot2 mul tr relu mm added s0 s1 kept") as s, nc.Block() as block:
        got = [s["g0"], s["g1"], s["g2"], s["g3"], s["g4"], s["g5"], s["g6"], s["g7"]]
        if source == "gather":
            @block.gpsimd
            def _(pool):
                def free(i, u):
                    after(pool, s["mul"] if normed else s["mm"], 2 * i + u - 1)

                def each(i, u, stage):
                    for j in range(J):
                        pool.indirect_dma_start(
                            out=got_t[u][:, j * P:(j + 1) * P], out_offset=None, in_=m.H,
                            in_offset=bass.IndirectOffsetOnAxis(ap=stage[:, j:j + 1], axis=0)).then_inc(got[J * u + j], 16)
                indexed_loop(nc, s, m.src, m.stage_idx, each, free)
        if source == "ones":
            @block.gpsimd
            def _(pool):
                renumber_senders(nc, pool, m, s)
        if source == "values":
            @block.sync
            def _(sp):
                def body(i, last):
                    for u in range(2):
                        g = 2 * i + u
                        after(sp, s["mm"], g - 1)
                        sp.dma_start(jview(got_t[u]), m.V[bass.ds(g * WIN, WIN), :].rearrange("(j p) f -> p j f", p=P)).then_inc(got[u], 16)
                over_groups(sp, body)

        @block.vector
        def _(v):
            def add(g, u):
                cols = group_columns(v, m, g)
                v.wait_ge(s["mm"], g + 1)
                add_sums(nc, v, s, g, cols, m.ps[u])

            def body(i, last):
                for u in range(2):
                    g = 2 * i + u
                    after(v, s["mm"], g - 1)
                    nc.vector.tensor_tensor(
                        jview(hot[u]), bc(m.iota[:, :].unsqueeze(1), [P, J, P]),
                        bc(m.local[:, bass.ds(g * J, J)].unsqueeze(2), [P, J, P]), ALU.is_equal).then_inc(s["hot"], 1)
                    if scaled:
                        v.wait_ge(s["hot"], g + 1)
                        nc.vector.tensor_tensor(
                            jview(hot[u]), jview(hot[u]),
                            bc(m.alpha[:, bass.ds(g * J, J)].unsqueeze(2), [P, J, P]), ALU.mult).then_inc(s["hot2"], 1)
                    if started(i):
                        add(g - 2, u)
                    if normed:
                        for j in range(J):
                            v.wait_ge(got[J * u + j], 16 * (i + 1))
                        nc.vector.tensor_tensor(jview(tr[u]), jview(got_t[u]), bc(m.scale_row[:, :].unsqueeze(1), [P, J, P]),
                                                ALU.mult).then_inc(s["mul"], 1)
                        v.wait_ge(s["mul"], g + 1)
                        nc.vector.tensor_tensor(jview(tr[u]), jview(tr[u]), bc(m.shift_row[:, :].unsqueeze(1), [P, J, P]),
                                                ALU.add).then_inc(s["tr"], 1)
            over_groups(v, body)
            add(GROUPS - 2, 0)
            add(GROUPS - 1, 1)
            v.wait_ge(s["added"], GROUPS)

        if normed:
            @block.scalar
            def _(act):
                def body(i, last):
                    for u in range(2):
                        act.wait_ge(s["tr"], 2 * i + u + 1)
                        nc.scalar.activation(tr[u][:], tr[u][:], ACT.Relu).then_inc(s["relu"], 1)
                over_groups(act, body)

        @block.tensor
        def _(pe):
            def body(i, last):
                for u in range(2):
                    g = 2 * i + u
                    pe.wait_ge(s["hot2"] if scaled else s["hot"], g + 1)
                    if normed:
                        pe.wait_ge(s["relu"], g + 1)
                    elif source == "values":
                        pe.wait_ge(got[u], 16 * (i + 1))
                    at = tile_columns(pe, m, [m.ps[u]], g)[0]
                    after(pe, s["added"], g - 1)
                    clear_bank(nc, m, m.ps[u])
                    for j in range(J):
                        if source == "gather" and not normed:
                            pe.wait_ge(got[J * u + j], 16 * (i + 1))
                        lhs = m.ones[:] if source == "ones" else (tr if normed else got_t)[u][:, j * P:(j + 1) * P]
                        last_mm = nc.tensor.matmul(at[j], lhs, hot[u][:, j * P:(j + 1) * P],
                                                   start=False, stop=(j == J - 1), skip_group_check=True)
                    last_mm.then_inc(s["mm"], 1)
            over_groups(pe, body)


def relation_pass(nc, m, weights):
    got_t, hot = m.big[0:2], m.big[2:4]
    by_type = [m.big[4 + J * u:4 + J * (u + 1)] for u in range(2)]
    hot_w = [m.big[12 + J * u:12 + J * (u + 1)] for u in range(2)]
    w4 = m.wide
    with semaphores(nc, "rel", "idx_ready g0 g1 g2 g3 g4 g5 g6 g7 hot w hw ag cp mm added") as s, nc.Block() as block:
        got = [s[f"g{k}"] for k in range(2 * J)]

        @block.sync
        def _(sp):
            sp.dma_start(w4[:].rearrange("p (r f) -> p r f", r=J), weights.rearrange("r i o -> i r o")).then_inc(s["w"], 16)

        @block.gpsimd
        def _(pool):
            def free(i, u):
                after(pool, s["ag"], (2 * i + u - 1) * J)

            def each(i, u, stage):
                for j in range(J):
                    pool.indirect_dma_start(
                        out=got_t[u][:, j * P:(j + 1) * P], out_offset=None, in_=m.H,
                        in_offset=bass.IndirectOffsetOnAxis(ap=stage[:, j:j + 1], axis=0)).then_inc(got[J * u + j], 16)
            indexed_loop(nc, s, m.src, m.stage_idx, each, free)

        @block.vector
        def _(v):
            def add(g, u):
                cols = group_columns(v, m, g)
                v.wait_ge(s["mm"], g + 1)
                add_sums(nc, v, s, g, cols, m.ps[J + u])

            def body(i, last):
                for u in range(2):
                    g = 2 * i + u
                    after(v, s["hw"], (g - 1) * J)
                    nc.vector.tensor_tensor(
                        jview(hot[u]), bc(m.iota[:, :].unsqueeze(1), [P, J, P]),
                        bc(m.local[:, bass.ds(g * J, J)].unsqueeze(2), [P, J, P]), ALU.is_equal).then_inc(s["hot"], 1)
                    v.wait_ge(s["hot"], g + 1)
                    after(v, s["ag"], (g - 1) * J)
                    for r in range(J):
                        nc.vector.tensor_tensor(
                            jview(hot_w[u][r]), jview(hot[u]),
                            bc(m.tw[:, bass.ds(g * J, J), r:r + 1], [P, J, P]), ALU.mult).then_inc(s["hw"], 1)
                    if started(i):
                        add(g - 2, u)
            over_groups(v, body)
            add(GROUPS - 2, 0)
            add(GROUPS - 1, 1)
            v.wait_ge(s["added"], GROUPS)

        @block.scalar
        def _(act):
            def body(i, last):
                for u in range(2):
                    g = 2 * i + u
                    after(act, s["mm"], g - 1)
                    for r in range(J):
                        act.wait_ge(s["ag"], g * J + r + 1)
                        nc.scalar.activation(by_type[u][r][:], m.ps[r][:], ACT.Copy).then_inc(s["cp"], 1)
            over_groups(act, body)

        @block.tensor
        def _(pe):
            pe.wait_ge(s["w"], 16)

            def body(i, last):
                for u in range(2):
                    g = 2 * i + u
                    out = m.ps[J + u]
                    at = tile_columns(pe, m, m.ps[0:J], g)

                    def through(r):
                        pe.wait_ge(s["cp"], g * J + r + 1)
                        return nc.tensor.matmul(out[:], w4[:, r * P:(r + 1) * P], by_type[u][r][:], start=(r == 0), stop=(r == J - 1))
                    for j in range(J):
                        pe.wait_ge(got[J * u + j], 16 * (i + 1))
                    for r in range(J):
                        after(pe, s["cp"], (g - 1) * J + r + 1)
                        clear_bank(nc, m, m.ps[r])
                        pe.wait_ge(s["hw"], g * J + r + 1)
                        for j in range(J):
                            ag = nc.tensor.matmul(at[r][j], got_t[u][:, j * P:(j + 1) * P], hot_w[u][r][:, j * P:(j + 1) * P],
                                                  start=False, stop=(j == J - 1), skip_group_check=True)
                        ag.then_inc(s["ag"], 1)
                        if r == 0:
                            after(pe, s["added"], g - 1)
                        else:
                            through(r - 1)
                    through(J - 1).then_inc(s["mm"], 1)
            over_groups(pe, body)


def over_residual(eng, body):
    def single(i):
        body(i, i // 2, i % 2, i < SWIN // U, i == ITERS - 1)

    mid = SWIN // U // 2
    single(0)
    single(1)
    with eng.Fori(1, mid) as turn:
        body(2 * turn, turn, 0, True, False)
        body(2 * turn + 1, turn, 1, True, False)
    single(2 * mid)
    single(2 * mid + 1)
    with eng.Fori(mid + 1, ITERS // 2) as turn:
        body(2 * turn, turn, 0, False, False)
        body(2 * turn + 1, turn, 1, False, False)
    single(ITERS - 1)


def move(eng, table, tiles, w, short, store, sem, apart=False):
    if short or apart:
        pairs = [(table[bass.ds((w + k) * WIN, p * J), :].rearrange("(p j) f -> p j f", j=J),
                  tiles[:p, k, :].rearrange("p (j f) -> p j f", j=J)) for k, p in ((0, P), (1, TAIL_P if short else P))]
    else:
        pairs = [(table[bass.ds(w * WIN, 2 * WIN), :].rearrange("(k p j) f -> p k (j f)", k=2, j=J), tiles)]
    for rows_, tile in pairs:
        eng.dma_start(*((rows_, tile) if store else (tile, rows_))).then_inc(sem, 16)


def residual_pass(nc, m, kind, weight=None, bias=None, scaled=False):
    table = kind in ("gcn", "rel")
    hin, hs, cw, t1, x0, ho = (m.big[k * U:(k + 1) * U] for k in range(6))
    beside = kind == "rel"
    per_store = 32 if beside else 16
    spare = {"ln0": 0, "gat": 0, "gcn": 2, "rel": 3}[kind]
    xt = x0 + m.big[spare * U:(spare + 1) * U]
    hin_pair, ho_pair = ([m.work[:, k * U + 2 * h:k * U + 2 * h + 2, :] for h in range(2)] for k in (0, 5))
    xt_pair = [m.work[:, k * U + 2 * h:k * U + 2 * h + 2, :] for k in (4, spare) for h in range(2)]
    st, rs, nb, ve = (m.sm[0:2], *([m.sm[k][:, 0:8], m.sm[k][:, 8:16]] for k in (2, 3, 4)))
    flag, b_col = m.sm[4][:, 32:32 + U], m.sm[4][:, 40:41]
    w_sb = m.w_sb[:]
    names = "w wb ldh0 ldh1 ldx0 ldx1 ldx2 ldx3 tp hs cw py yd t1 xs bs ba ve sq rc ds nb ho sth0 sth1 stx0 stx1 stx2 stx3"
    with semaphores(nc, "res", names) as s, nc.Block() as block:
        ldh, sth = ([s[f"{n}{h}"] for h in range(2)] for n in ("ldh", "sth"))
        ldx, stx = ([s[f"{n}{k}"] for k in range(4)] for n in ("ldx", "stx"))
        read = s["yd"] if kind == "gcn" else s["xs"]

        def pair(h):
            return (2 * h, 2 * h + 1)

        @block.sync
        def _(sp):
            if table:
                sp.dma_start(w_sb, weight).then_inc(s["w"], 16)
                sp.dma_start(m.bias_row[:], bc(bias.unsqueeze(0), [P, P])).then_inc(s["wb"], 16)
                sp.dma_start(b_col, bias.rearrange("(f o) -> f o", o=1)).then_inc(s["wb"], 16)

            def store_rows(i, h, last):
                sp.wait_ge(s["ho"], U * i + 2 * h + 2)
                move(sp, m.H, ho_pair[h], U * i + 2 * h, last, True, sth[h])

            def store_residual(i, half, h, last):
                if kind != "ln0":
                    sp.wait_ge(s["xs"], U * i + 2 * h + 2)
                    move(sp, m.XZ[:, 0:P] if beside else m.X, xt_pair[2 * half + h], U * i + 2 * h, last, True, stx[2 * half + h], beside)

            def body(i, turn, half, summed, last):
                if table:
                    for h in range(1 if last else 2):
                        w = U * i + 2 * h
                        after(sp, s["tp"], w - U + 2)
                        move(sp, m.H, hin_pair[h], w, last, False, ldh[h])

                def load_residual(h):
                    w, k = U * i + 2 * h, 2 * half + h
                    after(sp, s["ho"], w - 2 * U + 2)
                    if kind != "ln0":
                        after(sp, stx[k], per_store * (turn + 1) - per_store)
                    move(sp, m.X, xt_pair[k], w, last, False, ldx[k])

                if started(i, 2):
                    store_residual(i - 2, half, 1, False)
                    store_rows(i - 2, 0, False)
                load_residual(0)
                if started(i):
                    store_residual(i - 1, 1 - half, 0, False)
                if started(i, 2):
                    store_rows(i - 2, 1, False)
                if not last:
                    load_residual(1)
            over_residual(sp, body)
            final = ITERS - 1
            store_residual(final - 1, 1 - final % 2, 1, False)
            store_rows(final - 1, 0, False)
            store_residual(final, final % 2, 0, True)
            store_rows(final - 1, 1, False)
            store_rows(final, 0, True)
            sp.wait_ge(sth[0], 16 * (ITERS + 1))
            sp.wait_ge(sth[1], 16 * (ITERS - 1))
            if kind != "ln0":
                for k in range(4):
                    turns = -(-(ITERS - k // 2) // 2) - (1 if k == 1 else 0)
                    sp.wait_ge(stx[k], per_store * turns + (16 if k == 0 and not beside else 0))

        if kind != "ln0":
            @block.gpsimd
            def _(pool):
                clear_sums(nc, pool, m, s["hs"] if kind == "gcn" else s["cw"])

            @block.tensor
            def _(pe):
                if table:
                    pe.wait_ge(s["w"], 16)

                def body(i, turn, half, summed, last):
                    if table:
                        for u in slots(last):
                            w, p = U * i + u, parts(last, u)
                            pe.wait_ge(ldh[u // 2], 16 * (i + 1) + (16 if last else 0))
                            after(pe, s["hs"], w - U + 1)
                            for j in range(J):
                                tp = nc.tensor.transpose(m.ps[u][:, j * p:(j + 1) * p], hin[u][:p, j * P:(j + 1) * P], m.ident[:p, :p])
                            tp.then_inc(s["tp"], 1)
                    if kind == "gat" and not summed:
                        return
                    for u in slots(last):
                        w, p = U * i + u, parts(last, u)
                        if table:
                            pe.wait_ge(s["hs"], w + 1)
                        if kind != "gcn" and summed:
                            pe.wait_ge(s["cw"], w + 1)
                        after(pe, read, w - U + 1)
                        for j in range(J):
                            o = m.ps[U + u][:p, j * P:(j + 1) * P]
                            if kind == "gat":
                                mm = nc.tensor.transpose(o, cw[u][:, j * P:(j + 1) * P], m.ident[:])
                                continue
                            both = kind == "rel" and summed
                            mm = nc.tensor.matmul(o, hs[u][:, j * p:(j + 1) * p], w_sb, start=True, stop=not both)
                            if both:
                                mm = nc.tensor.matmul(o, cw[u][:, j * P:(j + 1) * P], m.ident[:], start=False, stop=True)
                        mm.then_inc(s["py"], 1)
                over_residual(pe, body)

        @block.vector
        def _(v):
            if table:
                v.wait_ge(s["wb"], 32)

            def inputs(i, u, summed, last):
                w, p = U * i + u, parts(last, u)
                sums = m.sums[:, bass.ds(w * WIN, WIN)].rearrange("f (p j) -> f j p", j=J) if summed else None
                if kind == "gcn":
                    v.wait_ge(s["tp"], w + 1)
                    after(v, s["py"], w - U + 1)
                    if summed:
                        nc.vector.tensor_tensor(jview(hs[u]), jview(m.ps[u]), sums, ALU.add).then_inc(s["hs"], 1)
                    else:
                        nc.vector.tensor_copy(hs[u][:, 0:J * p], m.ps[u][:, 0:J * p]).then_inc(s["hs"], 1)
                elif kind != "ln0" and summed:
                    after(v, s["py"], w - U + 1)
                    if kind == "gat":
                        nc.vector.tensor_scalar(jview(cw[u]), sums, 0.0, None, ALU.max).then_inc(s["cw"], 1)
                    else:
                        nc.vector.tensor_scalar(jview(cw[u]), sums, b_col, None, ALU.add).then_inc(s["cw"], 1)

            def scales(q, h):
                mean2 = st[h][:, 64:72].unsqueeze(2)
                v.wait_ge(s["sq"], q + 1)
                after(v, s["ho"], 2 * (q - 1))
                nc.vector.reciprocal(rs[h], ve[h]).then_inc(s["rc"], 1)
                v.wait_ge(s["rc"], q + 1)
                if scaled:
                    nc.vector.tensor_tensor(rs[h], rs[h], m.dis[:, bass.ds(2 * q * J, 2 * J)], ALU.mult).then_inc(s["ds"], 1)
                    v.wait_ge(s["ds"], q + 1)
                nc.vector.scalar_tensor_tensor(out=nb[h].unsqueeze(2), in0=mean2, scalar=-0.5, in1=rs[h].unsqueeze(2),
                                               op0=ALU.mult, op1=ALU.mult).then_inc(s["nb"], 1)

            def update(i, turn, half, h, summed, last):
                q = 2 * i + h
                loaded = 16 * (turn + 1) + (16 if last else 0)
                views = {}
                for u in pair(h):
                    w, p, xu = U * i + u, parts(last, u), U * half + u
                    bias_b = bc(m.bias_row[:p, :].unsqueeze(1), [p, J, P])
                    py, t, x = jview(m.ps[U + u], p), jview(t1[u], p), jview(xt[xu], p)
                    views[u] = w, p, xu, py, t, x
                    if kind == "gcn":
                        v.wait_ge(s["yd"], w + 1)
                        nc.vector.tensor_tensor(t, t, bias_b, ALU.add).then_inc(s["t1"], 1)
                    if kind == "rel" and not summed:
                        v.wait_ge(ldx[2 * half + h], loaded)
                        nc.vector.tensor_tensor(x, x, bias_b, ALU.add).then_inc(s["t1"], 1)
                for u in pair(h):
                    w, p, xu, py, t, x = views[u]
                    if kind != "rel" or summed:
                        v.wait_ge(ldx[2 * half + h], loaded)
                    if kind == "gcn":
                        v.wait_ge(s["t1"], w + 1)
                        nc.vector.scalar_tensor_tensor(out=xt[xu][:p], in0=t1[u][:p], scalar=0.0, in1=xt[xu][:p],
                                                       op0=ALU.max, op1=ALU.add).then_inc(s["xs"], 1)
                    elif kind == "rel" or kind == "gat" and summed:
                        v.wait_ge(s["py"], w + 1)
                        if not summed:
                            v.wait_ge(s["t1"], w - SWIN + 1)
                        nc.vector.tensor_tensor(x, x, py, ALU.add).then_inc(s["xs"], 1)
                    elif kind == "gat":
                        nc.vector.memset(flag[:, u:u + 1], 0.0).then_inc(s["xs"], 1)
                lagging = h == 1 or started(i)
                if kind == "gcn" and lagging:
                    scales(q - 1, 1 - h)
                for u in pair(h):
                    w, p, xu, py, t, x = views[u]
                    if kind != "ln0":
                        v.wait_ge(s["xs"], w + 1)
                    after(v, s["nb"], q - 1)
                    for j in range(J):
                        c = 24 * (u - 2 * h) + 6 * j
                        bs = nc.vector.bn_stats(st[h][:p, c:c + 6], xt[xu][:p, j * P:(j + 1) * P])
                    bs.then_inc(s["bs"], 1)
                v.wait_ge(s["bs"], 2 * q + 2)
                halves = st[h][:, 0:48].rearrange("p (k c) -> p k c", c=6)
                e, o, ee, oo = (halves[:, :, c:c + 1] for c in (1, 4, 2, 5))
                mean2, diff, sq = (st[h][:, 64 + 8 * c:72 + 8 * c].unsqueeze(2) for c in range(3))
                nc.vector.tensor_tensor(mean2, e, o, ALU.add)
                nc.vector.tensor_tensor(diff, e, o, ALU.subtract)
                nc.vector.tensor_tensor(sq, ee, oo, ALU.add).then_inc(s["ba"], 1)
                v.wait_ge(s["ba"], 2 * q + 1)
                nc.vector.tensor_tensor(diff, diff, diff, ALU.mult)
                nc.vector.tensor_scalar(sq, sq, 1.0 / P, EPS, ALU.mult, ALU.add).then_inc(s["ba"], 1)
                v.wait_ge(s["ba"], 2 * q + 2)
                after(v, s["rc"], q - 1)
                nc.vector.scalar_tensor_tensor(out=ve[h].unsqueeze(2), in0=diff, scalar=0.25, in1=sq, op0=ALU.mult, op1=ALU.add).then_inc(s["ve"], 1)
                if kind != "gcn" and lagging:
                    scales(q - 1, 1 - h)

            def body(i, turn, half, summed, last):
                for u in slots(last):
                    inputs(i, u, summed, last)
                if started(i):
                    update(i - 1, turn - (1 - half), 1 - half, 1, i <= SWIN // U if isinstance(i, int) else summed, False)
                update(i, turn, half, 0, summed, last)
            over_residual(v, body)
            scales(2 * (ITERS - 1), 0)

        @block.scalar
        def _(act):
            def scaled_products(i, h, last):
                for u in pair(h):
                    w, p = U * i + u, parts(last, u)
                    act.wait_ge(s["py"], w + 1)
                    after(act, s["xs"], w - U + 1)
                    for j in range(J):
                        y = nc.scalar.activation(t1[u][:p, j * P:(j + 1) * P], m.ps[U + u][:p, j * P:(j + 1) * P], ACT.Copy,
                                                 scale=m.dis[:p, bass.ds(w * J + j, 1)])
                    y.then_inc(s["yd"], 1)

            def root(i, h):
                act.wait_ge(s["ve"], 2 * i + h + 1)
                nc.scalar.activation(ve[h], ve[h], ACT.Sqrt).then_inc(s["sq"], 1)

            def norm(i, half, h, last):
                act.wait_ge(s["nb"], 2 * i + h + 1)
                after(act, sth[h], 16 * i)
                for u in pair(h):
                    w, p, xu = U * i + u, parts(last, u), U * half + u
                    for j in range(J):
                        c = J * (u - 2 * h) + j
                        r = nc.scalar.activation(ho[u][:p, j * P:(j + 1) * P], xt[xu][:p, j * P:(j + 1) * P], ACT.Relu,
                                                 bias=nb[h][:p, c:c + 1], scale=rs[h][:p, c:c + 1])
                    r.then_inc(s["ho"], 1)

            def body(i, turn, half, summed, last):
                if kind == "rel":
                    for u in slots(last):
                        w, c = U * i + u, J * parts(last, u)
                        act.wait_ge(s["tp"], w + 1)
                        after(act, s["py"], w - U + 1)
                        nc.scalar.activation(hs[u][:, 0:c], m.ps[u][:, 0:c], ACT.Copy).then_inc(s["hs"], 1)
                lagging = started(i)
                if kind == "gcn":
                    scaled_products(i, 0, last)
                    if lagging:
                        norm(i - 1, 1 - half, 0, False)
                        root(i - 1, 1)
                    if not last:
                        scaled_products(i, 1, last)
                    if lagging:
                        norm(i - 1, 1 - half, 1, False)
                    root(i, 0)
                else:
                    if lagging:
                        root(i - 1, 1)
                        norm(i - 1, 1 - half, 0, False)
                    root(i, 0)
                    if lagging:
                        norm(i - 1, 1 - half, 1, False)
            over_residual(act, body)
            norm(ITERS - 1, (ITERS - 1) % 2, 0, True)


def node_pass(nc, m, kind, weight=None, bias=None):
    table = kind != "gat"
    hin, hs, cw, t1, ho = (m.big[k * U:(k + 1) * U] for k in (0, 1, 2, 3, 5))
    w_sb = m.w_sb[:]
    windows = NWIN if table else SWIN
    dest = m.H if table else m.HC
    names = "w wb ldh0 ldh1 ldh2 ldh3 tp hs cw py yd t1 ho sth0 sth1 sth2 sth3"
    with semaphores(nc, "node", names) as s, nc.Block() as block:
        ldh, sth = ([s[f"{n}{u}"] for u in range(U)] for n in ("ldh", "sth"))
        read = s["ho"] if kind == "gat" else s["yd"]

        @block.sync
        def _(sp):
            if table:
                sp.dma_start(w_sb, weight).then_inc(s["w"], 16)
                sp.dma_start(m.bias_row[:], bc(bias.unsqueeze(0), [P, P])).then_inc(s["wb"], 16)

                def body(i, summed, last):
                    for u in slots(last):
                        w, p = U * i + u, parts(last, u)
                        after(sp, s["tp"], w - U + 1)
                        sp.dma_start(hin[u][:p], rows(m.H, w, p)).then_inc(ldh[u], 16)
                over_windows(sp, body)

        @block.gpsimd
        def _(pool):
            clear_sums(nc, pool, m, s["hs"] if kind == "gcn" else s["cw"])

        @block.tensor
        def _(pe):
            if table:
                pe.wait_ge(s["w"], 16)

            def body(i, summed, last):
                if table:
                    for u in slots(last):
                        w, p = U * i + u, parts(last, u)
                        pe.wait_ge(ldh[u], 16 * (i + 1))
                        after(pe, s["hs"], w - U + 1)
                        for j in range(J):
                            tp = nc.tensor.transpose(m.ps[u][:, j * p:(j + 1) * p], hin[u][:p, j * P:(j + 1) * P], m.ident[:p, :p])
                        tp.then_inc(s["tp"], 1)
                for u in slots(last):
                    w, p = U * i + u, parts(last, u)
                    if table:
                        pe.wait_ge(s["hs"], w + 1)
                    if kind != "gcn" and summed:
                        pe.wait_ge(s["cw"], w + 1)
                    after(pe, read, w - U + 1)
                    for j in range(J):
                        o = m.ps[U + u][:p, j * P:(j + 1) * P]
                        if kind == "gat":
                            mm = nc.tensor.transpose(o, cw[u][:, j * P:(j + 1) * P], m.ident[:])
                            continue
                        both = kind == "rel" and summed
                        mm = nc.tensor.matmul(o, hs[u][:, j * p:(j + 1) * p], w_sb, start=True, stop=not both)
                        if both:
                            mm = nc.tensor.matmul(o, cw[u][:, j * P:(j + 1) * P], m.ident[:], start=False, stop=True)
                    mm.then_inc(s["py"], 1)
            over_windows(pe, body, windows)

        @block.vector
        def _(v):
            if table:
                v.wait_ge(s["wb"], 16)

            def inputs(i, u, summed, last):
                w, p = U * i + u, parts(last, u)
                sums = m.sums[:, bass.ds(w * WIN, WIN)].rearrange("f (p j) -> f j p", j=J) if summed else None
                if table:
                    v.wait_ge(s["tp"], w + 1)
                    after(v, s["py"], w - U + 1)
                    if kind == "gcn" and summed:
                        nc.vector.tensor_tensor(jview(hs[u]), jview(m.ps[u]), sums, ALU.add).then_inc(s["hs"], 1)
                    else:
                        nc.vector.tensor_copy(hs[u][:, 0:J * p], m.ps[u][:, 0:J * p]).then_inc(s["hs"], 1)
                if kind != "gcn" and summed:
                    after(v, s["py"], w - U + 1)
                    if kind == "gat":
                        nc.vector.tensor_scalar(jview(cw[u]), sums, 0.0, None, ALU.max).then_inc(s["cw"], 1)
                    else:
                        nc.vector.tensor_copy(jview(cw[u]), sums).then_inc(s["cw"], 1)

            def biased(i, u, last):
                w, p = U * i + u, parts(last, u)
                bias_b = bc(m.bias_row[:p, :].unsqueeze(1), [p, J, P])
                if kind == "gcn":
                    v.wait_ge(s["yd"], w + 1)
                    nc.vector.tensor_tensor(jview(t1[u], p), jview(t1[u], p), bias_b, ALU.add).then_inc(s["t1"], 1)
                else:
                    v.wait_ge(s["py"], w + 1)
                    after(v, s["ho"], w - U + 1)
                    nc.vector.tensor_tensor(jview(t1[u], p), jview(m.ps[U + u], p), bias_b, ALU.add).then_inc(s["yd"], 1)

            def finished(i, u, last):
                w, p = U * i + u, parts(last, u)
                dis = bc(m.dis[:p, bass.ds(w * J, J)].unsqueeze(2), [p, J, P])
                v.wait_ge(s["t1"], w + 1)
                after(v, sth[u], 16 * i)
                nc.vector.scalar_tensor_tensor(out=jview(ho[u], p), in0=jview(t1[u], p), scalar=0.0, in1=dis,
                                               op0=ALU.max, op1=ALU.mult).then_inc(s["ho"], 1)

            def update(i, last):
                for h in range(1 if last else 2):
                    for u in (2 * h, 2 * h + 1):
                        biased(i, u, last)
                    if kind == "gcn":
                        for u in (2 * h, 2 * h + 1):
                            finished(i, u, last)

            def body(i, summed, last):
                for u in slots(last):
                    inputs(i, u, summed, last)
                if kind == "rel":
                    update(i, last)
                if kind == "gcn" and started(i):
                    update(i - 1, False)
            over_windows(v, body, windows)
            if kind == "gcn":
                update(ITERS - 1, True)

        @block.scalar
        def _(act):
            def store(i, u, last):
                w, p = U * i + u, parts(last, u)
                act.wait_ge(s["ho"], w + 1)
                act.dma_start(rows(dest, w, p), ho[u][:p]).then_inc(sth[u], 16)

            def body(i, summed, last):
                for u in slots(last):
                    w, p = U * i + u, parts(last, u)
                    if kind == "gcn":
                        if started(i):
                            store(i - 1, u, False)
                        act.wait_ge(s["py"], w + 1)
                        for j in range(J):
                            y = nc.scalar.activation(t1[u][:p, j * P:(j + 1) * P], m.ps[U + u][:p, j * P:(j + 1) * P], ACT.Copy,
                                                     scale=m.dis[:p, bass.ds(w * J + j, 1)])
                        y.then_inc(s["yd"], 1)
                        continue
                    after(act, sth[u], 16 * i)
                    if kind == "rel":
                        act.wait_ge(s["yd"], w + 1)
                        nc.scalar.activation(ho[u][:p], t1[u][:p], ACT.Relu).then_inc(s["ho"], 1)
                    else:
                        act.wait_ge(s["py"], w + 1)
                        nc.scalar.activation(ho[u][:], m.ps[U + u][:], ACT.Copy).then_inc(s["ho"], 1)
                    store(i, u, last)
                if kind == "gcn" and last:
                    for u in range(NWIN % U, U):
                        store(i - 1, u, False)
            over_windows(act, body, windows)
            if kind == "gcn":
                for u in slots(True):
                    store(ITERS - 1, u, True)
            for u in range(U):
                act.wait_ge(sth[u], 16 * rounds(u, windows))


def attention_scores(nc, m, hop):
    a = m.a
    gs, gq, ea = m.big[0:2], m.big[2:4], m.big[4:6]
    sT, qT, eT, vs, f = m.big[6], m.big[7], m.big[8], m.big[9], m.big[10]
    vt = m.big[12:14]
    wn, we, wq = (m.wide[:, k * P:(k + 1) * P] for k in range(3))
    bias = m.sm[0]
    table, idx = (m.H, m.src) if hop == 0 else (m.HC, m.src_c)
    bS, bQ, bE, bV, bF, bC, bT = m.ps[0:7]
    names = "idx_ready w g0 g1 q0 q1 e0 e1 z bb tS tQ tE cS cQ cE pV pF vs f1 f2 sc vT cc vc st0 st1"
    with semaphores(nc, "att", names) as s, nc.Block() as block:
        gS, gQ, gE, stv = [s["g0"], s["g1"]], [s["q0"], s["q1"]], [s["e0"], s["e1"]], [s["st0"], s["st1"]]

        @block.sync
        def _(sp):
            for k, x in enumerate((a["L1_gnn_Wn"], a["L1_gnn_We"], a["L1_gnn_Wq"])):
                sp.dma_start((wn, we, wq)[k], x[hop]).then_inc(s["w"], 16)
            for k, x in ((0, a["L1_gnn_bq"]), (2, a["L1_gnn_attn"]), (3, a["L1_gnn_bn"]), (4, a["L1_gnn_be"])):
                sp.dma_start(bias[:, k:k + 1], x[hop].rearrange("(f o) -> f o", o=1)).then_inc(s["w"], 16)
            sp.wait_ge(s["z"], 1)

            def body(i, last):
                for u in range(2):
                    g = 2 * i + u
                    if last and u == 1:
                        continue
                    after(sp, s["tE"], g - 1)
                    if not last:
                        sp.dma_start(jview(ea[u]), a["edge_attr_128"][bass.ds(g * WIN, WIN), :].rearrange("(j p) f -> p j f", p=P)).then_inc(gE[u], 16)
                    else:
                        full = FULL % J
                        e0 = g * WIN
                        sp.dma_start(jview(ea[u])[:, 0:full, :], a["edge_attr_128"][e0:e0 + full * P, :].rearrange("(j p) f -> p j f", p=P)).then_inc(gE[u], 16)
                        sp.dma_start(ea[u][0:REST, full * P:(full + 1) * P], a["edge_attr_128"][FULL * P:E, :]).then_inc(gE[u], 16)
            over_groups(sp, body)

        @block.gpsimd
        def _(pool):
            def body(i, last):
                for u in range(2):
                    g = 2 * i + u
                    after(pool, s["tQ"], g - 1)
                    for k, cols in ((0, idx), (1, m.rank)):
                        nc.gpsimd.tensor_copy(m.stage_idx[u][:, k * J:(k + 1) * J], cols[:, bass.ds(g * J, J)]).then_inc(s["idx_ready"], 1)
                    pool.wait_ge(s["idx_ready"], 2)
                    pool.sem_clear(s["idx_ready"])
                    for k, dst_t, sem in ((0, gs[u], gS[u]), (1, gq[u], gQ[u])):
                        for j in range(J):
                            pool.indirect_dma_start(
                                out=dst_t[:, j * P:(j + 1) * P], out_offset=None, in_=table,
                                in_offset=bass.IndirectOffsetOnAxis(ap=m.stage_idx[u][:, k * J + j:k * J + j + 1], axis=0)).then_inc(sem, 16)
            over_groups(pool, body)

        @block.tensor
        def _(pe):
            pe.wait_ge(s["w"], 7 * 16)

            def body(i, last):
                for u in range(2):
                    g = 2 * i + u
                    for tile, bank, sem, read, done, when in (
                            (ea[u], bE, gE[u], s["cE"], s["tE"], 16 * (i + 1) + (16 if last and u == 0 else 0) - (16 if last and u == 1 else 0)),
                            (gs[u], bS, gS[u], s["cS"], s["tS"], 16 * J * (i + 1)), (gq[u], bQ, gQ[u], s["cQ"], s["tQ"], 16 * J * (i + 1))):
                        pe.wait_ge(sem, when)
                        after(pe, read, g)
                        for j in range(J):
                            tp = nc.tensor.transpose(bank[:, j * P:(j + 1) * P], tile[:, j * P:(j + 1) * P], m.ident[:])
                        tp.then_inc(done, 1)
                    after(pe, s["vs"], g)
                    pe.wait_ge(s["cE"], g + 1)
                    nc.tensor.matmul(bV[:], we, eT[:], start=True, stop=False)
                    pe.wait_ge(s["cS"], g + 1)
                    nc.tensor.matmul(bV[:], wn, sT[:], start=False, stop=True).then_inc(s["pV"], 1)
                    pe.wait_ge(s["cQ"], g + 1)
                    after(pe, s["f1"], g)
                    nc.tensor.matmul(bF[:], wq, qT[:], start=True, stop=True).then_inc(s["pF"], 1)
                    pe.wait_ge(s["vs"], g + 1)
                    after(pe, s["vc"], g)
                    for j in range(J):
                        t = nc.tensor.transpose(bT[:, j * P:(j + 1) * P], vs[:, j * P:(j + 1) * P], m.ident[:])
                    t.then_inc(s["vT"], 1)
                    pe.wait_ge(s["f2"], g + 1)
                    after(pe, s["cc"], g)
                    for j in range(J):
                        t = nc.tensor.matmul(bC[:, j:j + 1], f[:, j * P:(j + 1) * P], bias[:, 2:3], start=True, stop=True)
                    t.then_inc(s["sc"], 1)
            over_groups(pe, body)

        @block.scalar
        def _(act):
            act.wait_ge(s["bb"], 1)

            def body(i, last):
                for u in range(2):
                    g = 2 * i + u
                    act.wait_ge(s["tE"], g + 1)
                    after(act, s["pV"], g)
                    nc.scalar.activation(eT[:], bE[:], ACT.Copy).then_inc(s["cE"], 1)
                    act.wait_ge(s["tS"], g + 1)
                    nc.scalar.activation(sT[:], bS[:], ACT.Copy).then_inc(s["cS"], 1)
                    act.wait_ge(s["pV"], g + 1)
                    after(act, s["f1"], g)
                    after(act, s["vT"], g)
                    nc.scalar.activation(vs[:], bV[:], ACT.Identity, bias=bias[:, 1:2]).then_inc(s["vs"], 1)
                    act.wait_ge(s["vT"], g + 1)
                    after(act, stv[u], 16 * i)
                    nc.scalar.activation(vt[u][:], bT[:], ACT.Copy).then_inc(s["vc"], 1)
                    act.wait_ge(s["vc"], g + 1)
                    act.dma_start(m.V[bass.ds(g * WIN, WIN), :].rearrange("(j p) f -> p j f", p=P), jview(vt[u])).then_inc(stv[u], 16)
            over_groups(act, body)
            for u in range(2):
                act.wait_ge(stv[u], 16 * GROUPS // 2)

        @block.vector
        def _(v):
            nc.vector.memset(ea[0][:], 0.0)
            nc.vector.memset(ea[1][:], 0.0).then_inc(s["z"], 1)
            v.wait_ge(s["w"], 7 * 16)
            nc.vector.tensor_tensor(bias[:, 1:2], bias[:, 3:4], bias[:, 4:5], ALU.add).then_inc(s["bb"], 1)

            def body(i, last):
                for u in range(2):
                    g = 2 * i + u
                    v.wait_ge(s["tQ"], g + 1)
                    after(v, s["pF"], g)
                    nc.vector.tensor_copy(qT[:], bQ[:]).then_inc(s["cQ"], 1)
                    v.wait_ge(s["pF"], g + 1)
                    v.wait_ge(s["vs"], g + 1)
                    after(v, s["sc"], g)
                    nc.vector.scalar_tensor_tensor(out=f[:], in0=bF[:], scalar=bias[:, 0:1], in1=vs[:],
                                                   op0=ALU.add, op1=ALU.add).then_inc(s["f1"], 1)
                    v.wait_ge(s["f1"], g + 1)
                    nc.vector.scalar_tensor_tensor(out=f[:], in0=f[:], scalar=0.2, in1=f[:],
                                                   op0=ALU.mult, op1=ALU.max).then_inc(s["f2"], 1)
                    v.wait_ge(s["sc"], g + 1)
                    nc.vector.tensor_copy(m.score[:, bass.ds(g * J, J)], bC[:, 0:J]).then_inc(s["cc"], 1)
            over_groups(v, body)


def segment_softmax(nc, m):
    sc, fw, new, nxt, pen, penn, keep, tot = (m.big[k][:, 0:EC] for k in range(8))
    col, row = m.sm[1], m.sm[2]
    with semaphores(nc, "soft", "pa pb io d vp pv va av") as s, nc.Block() as block:
        @block.sync
        def _(sp):
            sp.dma_start(new, m.NEW[0:EPAD].rearrange("(p c) -> p c", c=EC)).then_inc(s["io"], 16)
            sp.dma_start(nxt, m.NEW[1:EPAD + 1].rearrange("(p c) -> p c", c=EC)).then_inc(s["io"], 16)
            sp.wait_ge(s["pb"], 1)
            sp.dma_start(m.LIN[0:ROWS_A * P].rearrange("(t e) -> t e", e=P), m.big[8][:, 0:P]).then_inc(s["io"], 16)
            sp.dma_start(m.LIN[ROWS_A * P:EPAD].rearrange("(t e) -> t e", e=P), m.big[8][0:ROWS_B, P:2 * P]).then_inc(s["io"], 16)
            sp.wait_ge(s["io"], 64)
            sp.dma_start(sc, m.LIN.rearrange("(p c) -> p c", c=EC)).then_inc(s["io"], 16)
            sp.wait_ge(s["pb"], 2)
            sp.dma_start(m.LIN.rearrange("(p c) -> p c", c=EC), tot).then_inc(s["io"], 16)
            sp.wait_ge(s["io"], 96)
            sp.dma_start(m.big[8][:, 0:P], m.LIN[0:ROWS_A * P].rearrange("(t e) -> t e", e=P)).then_inc(s["io"], 16)
            sp.dma_start(m.big[8][0:ROWS_B, P:2 * P], m.LIN[ROWS_A * P:EPAD].rearrange("(t e) -> t e", e=P)).then_inc(s["io"], 16)

        @block.tensor
        def _(pe):
            nc.tensor.transpose(m.ps[0][:, 0:P], m.score[:, 0:ROWS_A], m.ident[:])
            nc.tensor.transpose(m.ps[0][0:ROWS_B, P:2 * P], m.score[:, ROWS_A:TILES], m.ident[:]).then_inc(s["pa"], 1)
            for k in range(4):
                pe.wait_ge(s["vp"], 2 * k + 1)
                nc.tensor.transpose(m.ps[1][0:1, 0:P], col[:, 0:1], m.ident[:])
                nc.tensor.transpose(m.ps[1][0:1, P:2 * P], col[:, 1:2], m.ident[:]).then_inc(s["pv"], 1)
                pe.wait_ge(s["vp"], 2 * k + 2)
                nc.tensor.transpose(m.ps[2][:, 0:1], row[0:1, 0:P], m.ident[0:1, 0:1]).then_inc(s["pv"], 1)
            pe.wait_ge(s["io"], 128)
            nc.tensor.transpose(m.ps[3][:, 0:ROWS_A], m.big[8][:, 0:P], m.ident[:])
            nc.tensor.transpose(m.ps[3][:, ROWS_A:TILES], m.big[8][0:ROWS_B, P:2 * P], m.ident[0:ROWS_B, 0:ROWS_B]).then_inc(s["pa"], 1)

        @block.scalar
        def _(act):
            act.wait_ge(s["va"], 1)
            nc.scalar.activation(sc, sc, ACT.Exp).then_inc(s["av"], 1)

        @block.vector
        def _(v):
            n = [0]

            def link(ins):
                n[0] += 1
                ins.then_inc(s["d"], 1)
                v.wait_ge(s["d"], n[0])

            def rev(x):
                return x[:, ::-1]

            k = [0]

            def scan(dst, stop_, x, backward, op0, op1, unit):
                r = rev if backward else (lambda y: y)
                link(nc.vector.tensor_tensor_scan(r(dst), r(stop_), r(x), unit, op0, op1))
                end = 0 if backward else EC - 1
                link(nc.vector.tensor_copy(col[:, 0:1], dst[:, end:end + 1]))
                link(nc.vector.tensor_reduce(col[:, 1:2], stop_, AX.X, ALU.min))
                nc.vector.memset(row[0:1, 0:P], unit).then_inc(s["vp"], 1)
                k[0] += 1
                v.wait_ge(s["pv"], k[0])
                v.wait_ge(s["vp"], k[0])
                link(nc.vector.tensor_copy(row[0:1, P:2 * P], m.ps[1][0:1, P:2 * P]))
                link(nc.vector.tensor_copy(m.sm[3][0:1, 0:P], m.ps[1][0:1, 0:P]))
                link(nc.vector.tensor_tensor_scan(r(m.sm[3][0:1, P:2 * P]), r(row[0:1, P:2 * P]), r(m.sm[3][0:1, 0:P]),
                                                  unit, op0, op1))
                if backward:
                    nc.vector.tensor_copy(row[0:1, 0:P - 1], m.sm[3][0:1, P + 1:2 * P]).then_inc(s["vp"], 1)
                else:
                    nc.vector.tensor_copy(row[0:1, 1:P], m.sm[3][0:1, P:2 * P - 1]).then_inc(s["vp"], 1)
                k[0] += 1
                v.wait_ge(s["pv"], k[0])
                link(nc.vector.tensor_copy(col[:, 2:3], m.ps[2][:, 0:1]))
                link(nc.vector.tensor_tensor_scan(r(dst), r(stop_), r(x), col[:, 2:3], op0, op1))

            v.wait_ge(s["pa"], 1)
            link(nc.vector.tensor_copy(m.big[8][:, 0:P], m.ps[0][:, 0:P]))
            nc.vector.tensor_copy(m.big[8][0:ROWS_B, P:2 * P], m.ps[0][0:ROWS_B, P:2 * P]).then_inc(s["pb"], 1)
            v.wait_ge(s["io"], 80)
            link(nc.vector.tensor_scalar(pen, new, -BIG, None, ALU.mult))
            link(nc.vector.tensor_scalar(penn, nxt, -BIG, None, ALU.mult))
            link(nc.vector.tensor_scalar(keep, new, -1.0, 1.0, ALU.mult, ALU.add))
            scan(fw, pen, sc, False, ALU.add, ALU.max, -BIG)
            scan(tot, penn, fw, True, ALU.add, ALU.max, -BIG)
            nc.vector.tensor_tensor(sc, sc, tot, ALU.subtract).then_inc(s["va"], 1)
            v.wait_ge(s["av"], 1)
            scan(fw, keep, sc, False, ALU.mult, ALU.add, 0.0)
            scan(tot, penn, fw, True, ALU.add, ALU.max, -BIG)
            link(nc.vector.reciprocal(tot, tot))
            nc.vector.tensor_tensor(tot, tot, sc, ALU.mult).then_inc(s["pb"], 1)
            v.wait_ge(s["pa"], 2)
            nc.vector.tensor_copy(m.alpha[:], m.ps[3][:, 0:TILES]).then_inc(s["va"], 1)


def gin_first(nc, m, layer):
    hin, hT, z = m.big[0:U], m.big[U:2 * U], m.big[2 * U:3 * U]
    w_sb, b = m.w_sb[:], m.sm[0]
    with semaphores(nc, "gin1", "w ldh0 ldh1 ldh2 ldh3 tp hT hs pz z1 bs st0 st1 st2 st3") as s, nc.Block() as block:
        ldh, stz = ([s[f"{n}{u}"] for u in range(U)] for n in ("ldh", "st"))

        @block.sync
        def _(sp):
            sp.dma_start(w_sb, m.a["L3_gnn_W1"][layer]).then_inc(s["w"], 16)
            sp.dma_start(b[:, 0:1], m.a["L3_gnn_b1"][layer].rearrange("(f o) -> f o", o=1)).then_inc(s["w"], 16)

            def body(i, summed, last):
                for u in slots(last):
                    w, p = U * i + u, parts(last, u)
                    after(sp, s["tp"], w - U + 1)
                    sp.dma_start(hin[u][:p], rows(m.H, w, p)).then_inc(ldh[u], 16)
            over_windows(sp, body)

        @block.gpsimd
        def _(pool):
            clear_sums(nc, pool, m, s["hs"])

        @block.tensor
        def _(pe):
            pe.wait_ge(s["w"], 32)

            def body(i, summed, last):
                for u in slots(last):
                    w, p = U * i + u, parts(last, u)
                    pe.wait_ge(ldh[u], 16 * (i + 1))
                    after(pe, s["hT"], w - U + 1)
                    for j in range(J):
                        t = nc.tensor.transpose(m.ps[u][:, j * p:(j + 1) * p], hin[u][:p, j * P:(j + 1) * P], m.ident[:p, :p])
                    t.then_inc(s["tp"], 1)
                if started(i):
                    product(i - 1, False)

            def product(i, last):
                for u in slots(last):
                    w, p = U * i + u, parts(last, u)
                    pe.wait_ge(s["hs"], w + 1)
                    after(pe, s["z1"], w - U + 1)
                    nc.tensor.matmul(m.ps[U + u][:, 0:J * p], w_sb, hT[u][:, 0:J * p], start=True, stop=True).then_inc(s["pz"], 1)
            over_windows(pe, body)
            product(ITERS - 1, True)

        @block.scalar
        def _(act):
            act.wait_ge(s["w"], 32)

            def body(i, summed, last):
                for u in slots(last):
                    w, c = U * i + u, J * parts(last, u)
                    act.wait_ge(s["tp"], w + 1)
                    after(act, s["pz"], w - U + 1)
                    if layer:
                        nc.scalar.activation(hT[u][:, 0:c], m.ps[u][:, 0:c], ACT.Relu, bias=m.shift[:], scale=m.scale[:]).then_inc(s["hT"], 1)
                    else:
                        nc.scalar.activation(hT[u][:, 0:c], m.ps[u][:, 0:c], ACT.Copy).then_inc(s["hT"], 1)
                if started(i):
                    add_bias(i - 1, False)

            def add_bias(i, last):
                for u in slots(last):
                    w, c = U * i + u, J * parts(last, u)
                    act.wait_ge(s["pz"], w + 1)
                    after(act, s["bs"], w - U + 1)
                    after(act, stz[u], 16 * i)
                    nc.scalar.activation(z[u][:, 0:c], m.ps[U + u][:, 0:c], ACT.Identity, bias=b[:, 0:1]).then_inc(s["z1"], 1)
                for u in slots(last):
                    w, c = U * i + u, J * parts(last, u)
                    act.wait_ge(s["z1"], w + 1)
                    act.dma_start(m.Z1[bass.ds(w * P, P), 0:c], z[u][:, 0:c]).then_inc(stz[u], 16)
            over_windows(act, body)
            add_bias(ITERS - 1, True)
            for u in range(U):
                act.wait_ge(stz[u], 16 * rounds(u))

        @block.vector
        def _(v):
            def body(i, summed, last):
                for u in slots(last):
                    w = U * i + u
                    v.wait_ge(s["hT"], w + 1)
                    if summed:
                        sums = m.sums[:, bass.ds(w * WIN, WIN)].rearrange("f (p j) -> f j p", j=J)
                        nc.vector.tensor_tensor(jview(hT[u]), jview(hT[u]), sums, ALU.add).then_inc(s["hs"], 1)
                    else:
                        nc.vector.memset(m.sm[1][:, u:u + 1], 0.0).then_inc(s["hs"], 1)
                if started(i):
                    measure(i - 1, False)

            def measure(i, last):
                for u in slots(last):
                    w, c = U * i + u, J * parts(last, u)
                    v.wait_ge(s["z1"], w + 1)
                    nc.vector.bn_stats(m.stats[:, bass.ds(w * 6, 6)], z[u][:, 0:c]).then_inc(s["bs"], 1)
            over_windows(v, body)
            measure(ITERS - 1, True)
            v.wait_ge(s["bs"], NWIN)


def batch_norm(nc, m, gamma, beta, extra, layer):
    p = m.sm[0]
    with semaphores(nc, "bn", "ld d v a pe") as s, nc.Block() as block:
        @block.sync
        def _(sp):
            for k, x in enumerate((gamma, beta, extra)):
                if x is not None:
                    sp.dma_start(p[:, k:k + 1], x[layer].rearrange("(f o) -> f o", o=1)).then_inc(s["ld"], 16)

        @block.scalar
        def _(act):
            act.wait_ge(s["v"], 1)
            nc.scalar.activation(p[:, 5:6], p[:, 4:5], ACT.Sqrt).then_inc(s["a"], 1)

        @block.tensor
        def _(pe):
            pe.wait_ge(s["v"], 2)
            nc.tensor.matmul(m.ps[0][:, 0:P], m.sm[1][:, 0:P], m.ident[:], start=True, stop=True)
            nc.tensor.matmul(m.ps[0][:, P:2 * P], m.sm[2][:, 0:P], m.ident[:], start=True, stop=True).then_inc(s["pe"], 1)

        @block.vector
        def _(v):
            n = [0]

            def link(ins):
                n[0] += 1
                ins.then_inc(s["d"], 1)
                v.wait_ge(s["d"], n[0])
            link(nc.vector.bn_aggr(p[:, 3:5], m.stats[:]))
            v.wait_ge(s["ld"], 16 * (2 if extra is None else 3))
            nc.vector.tensor_scalar(p[:, 4:5], p[:, 4:5], EPS, None, ALU.add).then_inc(s["v"], 1)
            if extra is not None:
                link(nc.vector.tensor_tensor(p[:, 3:4], p[:, 3:4], p[:, 2:3], ALU.add))
            v.wait_ge(s["a"], 1)
            link(nc.vector.reciprocal(p[:, 6:7], p[:, 5:6]))
            link(nc.vector.tensor_tensor(m.scale[:], p[:, 6:7], p[:, 0:1], ALU.mult))
            link(nc.vector.tensor_tensor(p[:, 7:8], p[:, 3:4], m.scale[:], ALU.mult))
            link(nc.vector.tensor_tensor(m.shift[:], p[:, 1:2], p[:, 7:8], ALU.subtract))
            link(nc.vector.tensor_scalar(m.sm[1][:, 0:P], m.ones[:], m.scale[:], None, ALU.mult))
            nc.vector.tensor_scalar(m.sm[2][:, 0:P], m.ones[:], m.shift[:], None, ALU.mult).then_inc(s["v"], 1)
            v.wait_ge(s["pe"], 1)
            link(nc.vector.tensor_copy(m.scale_row[:], m.ps[0][:, 0:P]))
            link(nc.vector.tensor_copy(m.shift_row[:], m.ps[0][:, P:2 * P]))


def gin_second(nc, m, layer):
    final = layer == m.a["L3_gnn_W1"].shape[0] - 1
    zin, act_t, ho = m.big[0:U], m.big[U:2 * U], m.big[2 * U:3 * U]
    w_sb = m.w_sb[:]
    with semaphores(nc, "gin2", "w wb ld0 ld1 ld2 ld3 a py pz ho bs st0 st1 st2 st3") as s, nc.Block() as block:
        ld, sto = ([s[f"{n}{u}"] for u in range(U)] for n in ("ld", "st"))

        @block.sync
        def _(sp):
            sp.dma_start(w_sb, m.a["L3_gnn_W2"][layer]).then_inc(s["w"], 16)
            sp.dma_start(m.bias_row[:], bc(m.a["L3_gnn_b2"][layer].unsqueeze(0), [P, P])).then_inc(s["wb"], 16)

            def body(i, summed, last):
                for u in slots(last):
                    w, p = U * i + u, parts(last, u)
                    after(sp, s["a"], w - U + 1)
                    sp.dma_start(zin[u][:, 0:J * p], m.Z1[bass.ds(w * P, P), 0:J * p]).then_inc(ld[u], 16)
            over_windows(sp, body)

        @block.scalar
        def _(act):
            def body(i, summed, last):
                for u in slots(last):
                    w, c = U * i + u, J * parts(last, u)
                    act.wait_ge(ld[u], 16 * (i + 1))
                    after(act, s["pz"], w - U + 1)
                    nc.scalar.activation(act_t[u][:, 0:c], zin[u][:, 0:c], ACT.Relu, bias=m.shift[:], scale=m.scale[:]).then_inc(s["a"], 1)
                if started(i):
                    store(i - 1, False)

            def store(i, last):
                for u in slots(last):
                    w, p = U * i + u, parts(last, u)
                    act.wait_ge(s["ho"], w + 1)
                    if final:
                        act.dma_start(m.XZ[bass.ds(w * WIN, p * J), P:2 * P].rearrange("(p j) f -> p j f", j=J),
                                      jview(ho[u], p)).then_inc(sto[u], 16)
                    else:
                        act.dma_start(rows(m.H, w, p), ho[u][:p]).then_inc(sto[u], 16)
            over_windows(act, body)
            store(ITERS - 1, True)
            for u in range(U):
                act.wait_ge(sto[u], 16 * rounds(u))

        @block.tensor
        def _(pe):
            pe.wait_ge(s["w"], 16)

            def body(i, summed, last):
                for u in slots(last):
                    w, p = U * i + u, parts(last, u)
                    pe.wait_ge(s["a"], w + 1)
                    after(pe, s["ho"], w - U + 1)
                    for j in range(J):
                        t = nc.tensor.matmul(m.ps[u][:p, j * P:(j + 1) * P], act_t[u][:, j * p:(j + 1) * p], w_sb, start=True, stop=True)
                    t.then_inc(s["py"], 1)
                    after(pe, s["bs"], w - U + 1)
                    nc.tensor.matmul(m.ps[U + u][:, 0:J * p], w_sb, act_t[u][:, 0:J * p], start=True, stop=True).then_inc(s["pz"], 1)
            over_windows(pe, body)

        @block.vector
        def _(v):
            v.wait_ge(s["wb"], 16)

            def body(i, summed, last):
                for u in slots(last):
                    w, p = U * i + u, parts(last, u)
                    v.wait_ge(s["py"], w + 1)
                    after(v, sto[u], 16 * i)
                    nc.vector.tensor_tensor(jview(ho[u], p), jview(m.ps[u], p), bc(m.bias_row[:p, :].unsqueeze(1), [p, J, P]), ALU.add).then_inc(s["ho"], 1)
                    v.wait_ge(s["pz"], w + 1)
                    nc.vector.bn_stats(m.stats[:, bass.ds(w * 6, 6)], m.ps[U + u][:, 0:J * p]).then_inc(s["bs"], 1)
            over_windows(v, body)
            v.wait_ge(s["bs"], NWIN)


def finish(nc, m):
    xz, o = m.pair, m.big[0:U]
    with semaphores(nc, "fin", "idx_ready g0 g1 g2 g3 t1 t2 t3 st0 st1 st2 st3") as s, nc.Block() as block:
        g, sto = ([s[f"{n}{u}"] for u in range(U)] for n in ("g", "st"))

        @block.gpsimd
        def _(pool):
            def body(i, summed, last):
                for u in slots(last):
                    w, p = U * i + u, parts(last, u)
                    after(pool, s["t3"], w - U + 1)
                    nc.gpsimd.tensor_copy(m.stage_idx[u][:p, 0:J], m.perm[:p, bass.ds(w * J, J)]).then_inc(s["idx_ready"], 1)
                    pool.wait_ge(s["idx_ready"], 1)
                    pool.sem_clear(s["idx_ready"])
                    for j in range(J):
                        pool.indirect_dma_start(
                            out=xz[u][:p, j, :], out_offset=None, in_=m.XZ,
                            in_offset=bass.IndirectOffsetOnAxis(ap=m.stage_idx[u][:p, j:j + 1], axis=0)).then_inc(g[u], 16)
            over_windows(pool, body)

        @block.vector
        def _(v):
            def body(i, summed, last):
                for u in slots(last):
                    w, p = U * i + u, parts(last, u)
                    v.wait_ge(g[u], 16 * J * (i + 1))
                    after(v, sto[u], 16 * i)
                    x, z, t = xz[u][:p, :, 0:P], xz[u][:p, :, P:2 * P], jview(o[u], p)
                    nc.vector.tensor_tensor(t, z, bc(m.scale_row[:p, :].unsqueeze(1), [p, J, P]), ALU.mult).then_inc(s["t1"], 1)
                    v.wait_ge(s["t1"], w + 1)
                    nc.vector.tensor_tensor(t, t, bc(m.shift_row[:p, :].unsqueeze(1), [p, J, P]), ALU.add).then_inc(s["t2"], 1)
                    v.wait_ge(s["t2"], w + 1)
                    nc.vector.tensor_tensor(t, t, x, ALU.add).then_inc(s["t3"], 1)
            over_windows(v, body)

        @block.sync
        def _(sp):
            def body(i, summed, last):
                for u in slots(last):
                    w, p = U * i + u, parts(last, u)
                    sp.wait_ge(s["t3"], w + 1)
                    sp.dma_start(rows(m.out, w, p), o[u][:p]).then_inc(sto[u], 16)
            over_windows(sp, body)
            for u in range(U):
                sp.wait_ge(sto[u], 16 * rounds(u))


INPUTS = ["x", "src", "dst", "edge_attr_128", "edge_type_4", "edge_weight", "L0_gnn_W", "L0_gnn_b", "L1_gnn_Wq",
          "L1_gnn_bq", "L1_gnn_Wn", "L1_gnn_bn", "L1_gnn_We", "L1_gnn_be", "L1_gnn_attn", "L2_gnn_W1", "L2_gnn_root1",
          "L2_gnn_b1", "L2_gnn_W2", "L2_gnn_root2", "L2_gnn_b2", "L3_gnn_W1", "L3_gnn_b1", "L3_gnn_g1", "L3_gnn_be1",
          "L3_gnn_W2", "L3_gnn_b2", "L3_gnn_g2", "L3_gnn_be2"]


def kernel(**inputs):
    import numpy as _np
    import concourse.bacc as _bacc
    from concourse import mybir as _mybir
    from concourse.bass_utils import run_bass_kernel_spmd as _run

    nc = _bacc.Bacc("TRN2", target_bir_lowering=False, num_devices=1)
    arrays, aps = {}, {}
    for name in INPUTS:
        arr = _np.ascontiguousarray(inputs[name])
        arrays[f"in_{name}_dram"] = arr
        aps[name] = nc.dram_tensor(f"in_{name}_dram", arr.shape, _mybir.dt.from_np(arr.dtype), kind="ExternalInput").ap()
    out = nc.dram_tensor("out_dram", (N, P), _mybir.dt.float32, kind="ExternalOutput").ap()
    build(nc, aps, out)
    r = _run(nc, [arrays], core_ids=[0])
    return r.results[0]["out_dram"]
```
